# Optimizing a Trainium2 kernel written in Bass

```python
import numpy as np
import jax
import jax.numpy as jnp

def _softmax(x, axis=-1):
    return jax.nn.softmax(x, axis=axis)

def _gelu(x):
    return jax.nn.gelu(x, approximate=True)

def _silu(x):
    return jax.nn.silu(x)

def _sigmoid(x):
    return jax.nn.sigmoid(x)

def _layernorm(x, axis=-1, eps=1e-05):
    m = jnp.mean(x, axis=axis, keepdims=True)
    v = jnp.var(x, axis=axis, keepdims=True)
    return (x - m) / jnp.sqrt(v + eps)

def _scatter_add(tgt, idx, src, axis=0):
    return tgt.at[idx].add(src)

def _segment_sum(src, seg, n):
    return jax.ops.segment_sum(src, seg, n)
kernel_name = 'mk_gnn_preln_d4_gnn_r64_228c9c'

def setup_inputs(seed: int=0):
    np.random.seed(seed)
    _w = jnp.asarray

    def _rec_inputs():
        import jax
        import jax.numpy as jnp
        _gk = jax.random.key(seed)
        x = -0.000202 + 1 * jax.random.normal(jax.random.fold_in(_gk, 1), (100000, 64), jnp.float32)
        src = jax.random.randint(jax.random.fold_in(_gk, 2), (25000,), 0, 100000, jnp.int32)
        dst = jax.random.randint(jax.random.fold_in(_gk, 3), (25000,), 0, 100000, jnp.int32)
        _o = jnp.argsort(dst, stable=True)
        src = src[_o]
        dst = dst[_o]
        edge_attr_64 = -4.21973e-05 + 0.999841 * jax.random.normal(jax.random.fold_in(_gk, 12), (25000, 64), jnp.float32)
        return (x, src, dst, edge_attr_64)
    x, src, dst, edge_attr_64 = _rec_inputs()

    def _L0_gnn_setup():
        import jax, jax.numpy as jnp
        import numpy as np
        N_NODES = 100000
        N_EDGES = 25000
        IN_CH = 64
        OUT_CH = 64
        MEM = 64
        key = jax.random.key(seed)
        ks = jax.random.split(key, 8)
        s = 0.1
        return {'x': jax.random.normal(ks[0], (N_NODES, IN_CH), dtype=jnp.float32), 'edge_index': jax.random.randint(ks[1], (2, N_EDGES), 0, N_NODES, dtype=jnp.int64), 'memory_weights': jnp.zeros((MEM,), dtype=jnp.float32), 'gru_w_ih': jax.random.normal(ks[2], (3 * MEM, MEM), dtype=jnp.float32) * s, 'gru_w_hh': jax.random.normal(ks[3], (3 * MEM, MEM), dtype=jnp.float32) * s, 'gru_b_ih': jax.random.normal(ks[4], (3 * MEM,), dtype=jnp.float32) * s, 'gru_b_hh': jax.random.normal(ks[5], (3 * MEM,), dtype=jnp.float32) * s, 'wt_w': jax.random.normal(ks[6], (IN_CH * OUT_CH, MEM), dtype=jnp.float32) * s, 'wt_b': jax.random.normal(ks[7], (IN_CH * OUT_CH,), dtype=jnp.float32) * s, 'gcn_bias': jnp.zeros((OUT_CH,), dtype=jnp.float32)}
    _L0_gnn_all = _L0_gnn_setup()
    _L0_gnn_in = {k: v for k, v in _L0_gnn_all.items() if k in ('memory_weights', 'gru_w_ih', 'gru_w_hh', 'gru_b_ih', 'gru_b_hh', 'wt_w', 'wt_b', 'gcn_bias')}
    del _L0_gnn_all

    def _L1_gnn_setup():
        import jax, jax.numpy as jnp
        import numpy as np
        N_NODES = 100000
        N_EDGES = 18750
        D = 64
        key = jax.random.key(seed)
        k1, k2, k3, k4, k5 = jax.random.split(key, 5)
        node_feat = jax.random.normal(k1, (N_NODES, D), dtype=jnp.float32)
        edge_feat = jax.random.normal(k2, (N_EDGES, D), dtype=jnp.float32)
        edge_index = jax.random.randint(k3, (2, N_EDGES), 0, N_NODES, dtype=jnp.int32)
        W1 = jax.random.normal(k4, (D, 2 * D), dtype=jnp.float32) / np.sqrt(D)
        b1 = jnp.zeros((2 * D,), dtype=jnp.float32)
        W2 = jax.random.normal(k5, (2 * D, D), dtype=jnp.float32) / np.sqrt(2 * D)
        b2 = jnp.zeros((D,), dtype=jnp.float32)
        return {'node_feat': node_feat, 'edge_feat': edge_feat, 'edge_index': edge_index, 'W1': W1, 'b1': b1, 'W2': W2, 'b2': b2}
    _L1_gnn_all = _L1_gnn_setup()
    _L1_gnn_in = {k: v for k, v in _L1_gnn_all.items() if k in ('W1', 'b1', 'W2', 'b2')}
    del _L1_gnn_all

    def _L2_gnn_setup():
        import jax, jax.numpy as jnp
        import numpy as np
        N_NODES = 100000
        N_EDGES = 25000
        D_IN = 64
        D_OUT = 64
        key = jax.random.key(seed)
        k = jax.random.split(key, 6)
        x = jax.random.normal(k[0], (N_NODES, D_IN), dtype=jnp.float32)
        W_self = jax.random.normal(k[1], (D_IN, D_OUT), dtype=jnp.float32) / np.sqrt(D_IN)
        W_neigh = jax.random.normal(k[2], (D_IN, D_OUT), dtype=jnp.float32) / np.sqrt(D_IN)
        bias = jnp.zeros((D_OUT,), dtype=jnp.float32)
        src = jax.random.randint(k[3], (N_EDGES,), 0, N_NODES, dtype=jnp.int32)
        dst = jax.random.randint(k[4], (N_EDGES,), 0, N_NODES, dtype=jnp.int32)
        return {'x': x, 'W_self': W_self, 'W_neigh': W_neigh, 'bias': bias, 'src': src, 'dst': dst, 'layer_id': 1, 'n_layers': 3}
    _L2_gnn_all = _L2_gnn_setup()
    _L2_gnn_in = {k: v for k, v in _L2_gnn_all.items() if k in ('W_self', 'W_neigh', 'bias')}
    del _L2_gnn_all

    def _L3_gnn_setup():
        import jax, jax.numpy as jnp
        import numpy as np
        N = 100000
        E = 12500
        F_IN = 64
        F_OUT = 64
        H = 4
        HOPS = 2
        NEG_SLOPE = 0.2

        def _segment_softmax(scores, dst, num_segments):
            m = jax.ops.segment_max(scores, dst, num_segments=num_segments)
            m = jnp.where(jnp.isneginf(m), 0.0, m)
            ex = jnp.exp(scores - m[dst])
            den = jax.ops.segment_sum(ex, dst, num_segments=num_segments)
            return ex / jnp.maximum(den[dst], 1e-16)

        def _multi_head_attention(x, src, dst, W_att, a_src, a_dst):
            h = jnp.einsum('ni,hio->nho', x, W_att)
            e = jnp.einsum('eho,ho->eh', h[src], a_src) + jnp.einsum('eho,ho->eh', h[dst], a_dst)
            e = jax.nn.leaky_relu(e, NEG_SLOPE)
            alpha = _segment_softmax(e, dst, N)
            msg = alpha[:, :, None] * h[src]
            out = jax.ops.segment_sum(msg, dst, num_segments=N)
            return out.mean(axis=1)

        def _gf(x, src, dst, num_hops):
            ones = jnp.ones((src.shape[0],), x.dtype)
            deg = jax.ops.segment_sum(ones, dst, num_segments=N)
            deg = jnp.maximum(deg, 1.0)[:, None]
            h = x
            for _ in range(num_hops):
                h = jax.ops.segment_sum(h[src], dst, num_segments=N) / deg
            return h
        key = jax.random.key(seed)
        ks = jax.random.split(key, 9)
        node_features = jax.random.normal(ks[0], (N, F_IN), jnp.float32)
        edge_index = jax.random.randint(ks[1], (2, E), 0, N, dtype=jnp.int64)
        s_in = 1.0 / np.sqrt(F_IN)
        s_out = 1.0 / np.sqrt(F_OUT)
        W_att = jax.random.normal(ks[2], (H, F_IN, F_OUT), jnp.float32) * s_in
        a_src = jax.random.normal(ks[3], (H, F_OUT), jnp.float32) * s_out
        a_dst = jax.random.normal(ks[4], (H, F_OUT), jnp.float32) * s_out
        W_g = jax.random.normal(ks[5], (F_IN, F_OUT), jnp.float32) * s_in
        b_g = jnp.zeros((F_OUT,), jnp.float32)
        W_w = jax.random.normal(ks[6], (2 * F_OUT, F_OUT), jnp.float32) * (1.0 / np.sqrt(2 * F_OUT))
        b_w = jnp.zeros((F_OUT,), jnp.float32)
        return {'node_features': node_features, 'edge_index': edge_index, 'W_att': W_att, 'a_src': a_src, 'a_dst': a_dst, 'W_g': W_g, 'b_g': b_g, 'W_w': W_w, 'b_w': b_w}
    _L3_gnn_all = _L3_gnn_setup()
    _L3_gnn_in = {k: v for k, v in _L3_gnn_all.items() if k in ('W_att', 'a_src', 'a_dst', 'W_g', 'b_g', 'W_w', 'b_w')}
    del _L3_gnn_all
    return {'x': x, 'src': src, 'dst': dst, 'edge_attr_64': edge_attr_64, 'L0_gnn_memory_weights': _L0_gnn_in['memory_weights'], 'L0_gnn_gru_w_ih': _L0_gnn_in['gru_w_ih'], 'L0_gnn_gru_w_hh': _L0_gnn_in['gru_w_hh'], 'L0_gnn_gru_b_ih': _L0_gnn_in['gru_b_ih'], 'L0_gnn_gru_b_hh': _L0_gnn_in['gru_b_hh'], 'L0_gnn_wt_w': _L0_gnn_in['wt_w'], 'L0_gnn_wt_b': _L0_gnn_in['wt_b'], 'L0_gnn_gcn_bias': _L0_gnn_in['gcn_bias'], 'L1_gnn_W1': _L1_gnn_in['W1'], 'L1_gnn_b1': _L1_gnn_in['b1'], 'L1_gnn_W2': _L1_gnn_in['W2'], 'L1_gnn_b2': _L1_gnn_in['b2'], 'L2_gnn_W_self': _L2_gnn_in['W_self'], 'L2_gnn_W_neigh': _L2_gnn_in['W_neigh'], 'L2_gnn_bias': _L2_gnn_in['bias'], 'L3_gnn_W_att': _L3_gnn_in['W_att'], 'L3_gnn_a_src': _L3_gnn_in['a_src'], 'L3_gnn_a_dst': _L3_gnn_in['a_dst'], 'L3_gnn_W_g': _L3_gnn_in['W_g'], 'L3_gnn_b_g': _L3_gnn_in['b_g'], 'L3_gnn_W_w': _L3_gnn_in['W_w'], 'L3_gnn_b_w': _L3_gnn_in['b_w']}

def reference(x, src, dst, edge_attr_64, L0_gnn_memory_weights, L0_gnn_gru_w_ih, L0_gnn_gru_w_hh, L0_gnn_gru_b_ih, L0_gnn_gru_b_hh, L0_gnn_wt_w, L0_gnn_wt_b, L0_gnn_gcn_bias, L1_gnn_W1, L1_gnn_b1, L1_gnn_W2, L1_gnn_b2, L2_gnn_W_self, L2_gnn_W_neigh, L2_gnn_bias, L3_gnn_W_att, L3_gnn_a_src, L3_gnn_a_dst, L3_gnn_W_g, L3_gnn_b_g, L3_gnn_W_w, L3_gnn_b_w):
    import jax
    import jax.numpy as jnp

    def _L0_gnn_ref(x, edge_index, memory_weights, gru_w_ih, gru_w_hh, gru_b_ih, gru_b_hh, wt_w, wt_b, gcn_bias):
        import jax, jax.numpy as jnp
        import numpy as np
        N_NODES = 100000
        N_EDGES = 25000
        IN_CH = 64
        OUT_CH = 64
        MEM = 64
        gi = gru_w_ih @ memory_weights + gru_b_ih
        gh = gru_b_hh
        i_r, i_z, i_n = jnp.split(gi, 3)
        h_r, h_z, h_n = jnp.split(gh, 3)
        r = jax.nn.sigmoid(i_r + h_r)
        z = jax.nn.sigmoid(i_z + h_z)
        n = jnp.tanh(i_n + r * h_n)
        update_memory = (1.0 - z) * n
        new_w = (wt_w @ update_memory + wt_b).reshape(OUT_CH, IN_CH)
        new_w = jax.lax.stop_gradient(new_w)
        xw = x @ new_w.T
        row, col = (edge_index[0], edge_index[1])
        deg = jax.ops.segment_sum(jnp.ones(row.shape[0], x.dtype), col, num_segments=N_NODES) + 1.0
        dinv = jax.lax.rsqrt(deg)
        norm = dinv[row] * dinv[col]
        agg = jax.ops.segment_sum(xw[row] * norm[:, None], col, num_segments=N_NODES)
        out = agg + xw * (dinv * dinv)[:, None] + gcn_bias
        return out

    def _L1_gnn_ref(node_feat, edge_feat, edge_index, W1, b1, W2, b2):
        import jax, jax.numpy as jnp
        import numpy as np
        N_NODES = 100000
        N_EDGES = 18750
        D = 64
        src, dst = (edge_index[0], edge_index[1])
        msg = node_feat[src] + edge_feat
        agg = jax.ops.segment_sum(msg, dst, num_segments=node_feat.shape[0])
        h = jax.nn.relu(agg @ W1 + b1)
        out = h @ W2 + b2
        return out

    def _L2_gnn_ref(x, W_self, W_neigh, bias, src, dst, layer_id, n_layers):
        import jax, jax.numpy as jnp
        import numpy as np
        N_NODES = 100000
        N_EDGES = 25000
        D_IN = 64
        D_OUT = 64
        n = x.shape[0]
        agg = jax.ops.segment_sum(x[src], dst, num_segments=n)
        deg = jax.ops.segment_sum(jnp.ones((src.shape[0],), x.dtype), dst, num_segments=n)
        h_neigh = agg / jnp.maximum(deg, 1.0)[:, None]
        h = x @ W_self + h_neigh @ W_neigh + bias
        return jnp.maximum(h, 0.0)

    def _L3_gnn_ref(node_features, edge_index, W_att, a_src, a_dst, W_g, b_g, W_w, b_w):
        import jax, jax.numpy as jnp
        import numpy as np
        N = 100000
        E = 12500
        F_IN = 64
        F_OUT = 64
        H = 4
        HOPS = 2
        NEG_SLOPE = 0.2

        def _segment_softmax(scores, dst, num_segments):
            m = jax.ops.segment_max(scores, dst, num_segments=num_segments)
            m = jnp.where(jnp.isneginf(m), 0.0, m)
            ex = jnp.exp(scores - m[dst])
            den = jax.ops.segment_sum(ex, dst, num_segments=num_segments)
            return ex / jnp.maximum(den[dst], 1e-16)

        def _multi_head_attention(x, src, dst, W_att, a_src, a_dst):
            h = jnp.einsum('ni,hio->nho', x, W_att)
            e = jnp.einsum('eho,ho->eh', h[src], a_src) + jnp.einsum('eho,ho->eh', h[dst], a_dst)
            e = jax.nn.leaky_relu(e, NEG_SLOPE)
            alpha = _segment_softmax(e, dst, N)
            msg = alpha[:, :, None] * h[src]
            out = jax.ops.segment_sum(msg, dst, num_segments=N)
            return out.mean(axis=1)

        def _gf(x, src, dst, num_hops):
            ones = jnp.ones((src.shape[0],), x.dtype)
            deg = jax.ops.segment_sum(ones, dst, num_segments=N)
            deg = jnp.maximum(deg, 1.0)[:, None]
            h = x
            for _ in range(num_hops):
                h = jax.ops.segment_sum(h[src], dst, num_segments=N) / deg
            return h
        src, dst = (edge_index[0], edge_index[1])
        local = _multi_head_attention(node_features, src, dst, W_att, a_src, a_dst)
        glob = _gf(node_features, src, dst, HOPS)
        glob = glob @ W_g + b_g
        cat = jnp.concatenate([local, glob], axis=-1)
        return cat @ W_w + b_w
    edge_index = jnp.stack([src, dst])
    h = jnp.maximum(_layernorm(x, axis=-1), 0.0)
    x = x + _L0_gnn_ref(h, edge_index, L0_gnn_memory_weights, L0_gnn_gru_w_ih, L0_gnn_gru_w_hh, L0_gnn_gru_b_ih, L0_gnn_gru_b_hh, L0_gnn_wt_w, L0_gnn_wt_b, L0_gnn_gcn_bias)
    h = jnp.maximum(_layernorm(x, axis=-1), 0.0)
    x = x + _L1_gnn_ref(h, edge_attr_64, edge_index, L1_gnn_W1, L1_gnn_b1, L1_gnn_W2, L1_gnn_b2)
    h = jnp.maximum(_layernorm(x, axis=-1), 0.0)
    x = x + _L2_gnn_ref(h, L2_gnn_W_self, L2_gnn_W_neigh, L2_gnn_bias, src, dst, 1, 3)
    h = jnp.maximum(_layernorm(x, axis=-1), 0.0)
    x = x + _L3_gnn_ref(h, edge_index, L3_gnn_W_att, L3_gnn_a_src, L3_gnn_a_dst, L3_gnn_W_g, L3_gnn_b_g, L3_gnn_W_w, L3_gnn_b_w)
    return x

_drawn_inputs = setup_inputs


def setup_inputs(seed=0):
    import zlib

    import numpy as np

    out = dict(_drawn_inputs(seed))
    spreads = {'L0_gnn_memory_weights': (0.0, 0.1),
     'L0_gnn_gcn_bias': (0.0, 0.1),
     'L1_gnn_b1': (0.0, 0.1),
     'L1_gnn_b2': (0.0, 0.1),
     'L2_gnn_bias': (0.0, 0.1),
     'L3_gnn_b_g': (0.0, 0.1),
     'L3_gnn_b_w': (0.0, 0.1)}
    factors = {}
    for name, (base, spread) in spreads.items():
        noise = np.random.default_rng([zlib.crc32(name.encode()), seed]).standard_normal(out[name].shape)
        drawn = base * np.exp(spread * noise) if base else spread * noise
        out[name] = jnp.asarray(drawn.astype(out[name].dtype))
    for name, factor in factors.items():
        out[name] = (out[name] * factor).astype(out[name].dtype)
    return out
```

```python
import numpy as np
import concourse.bass as bass
from concourse import mybir

F32 = mybir.dt.float32
I32 = mybir.dt.int32
ALU = mybir.AluOpType
ACT = mybir.ActivationFunctionType
AX = mybir.AxisListType

N, E, D = 100000, 25000, 64
P = 125
T = E // P
G = 5
GC = T // G
UC = 8
GU = GC // UC
NODES = N // P
STAGES = 5
DC = NODES // (STAGES * G)
DU = DC // UC
HEADS = 4
HID = 2 * D
EPS = 1e-5
SLOPE = 0.2
BIG = 1e30
NOREP = 32768


_NORM = 8
_DENSE = {"dl": 32, "ds": 32, "df": 1, "dr": 1}
PER = [
    {"gx": 16 * GC, "gt": 16 * GC, "hc": 1, "std": 4, **_DENSE, "o": GU + 2 * DU, "dve": 2 + _NORM + 1 + 2 * _NORM},
    {"gx": 16 * GC, "std": 3, **_DENSE, "o": 2 * DU, "dve": _NORM + 1 + 2 + 2 * _NORM},
    {"gx": 16 * GC, "hc": 1, "std": 3, **_DENSE, "o": GU + 2 * DU, "dve": 3 * _NORM},
    {"gx": 16 * GC, "hc": 1, "std": 3, **_DENSE, "o": GU + 2 * DU, "dve": 3 * _NORM},
    {"am": HEADS * GU, "std": 2, **_DENSE, "o": 2 * DU, "dve": 2 * _NORM},
]
DPER = [
    {"xl": 32, "xu": 1, "o": GU, "dve": _NORM + 3, "std": 1},
    {"xl": 32, "xu": 1, "o": GU},
    {"xl": 32, "xu": 1, "o": GU, "dve": _NORM + 1, "std": 1},
    {"xl": 32, "xu": 1, "o": GU, "dve": _NORM + 1, "std": 1},
    {"xl": 32, "xu": 1, "o": GU, "dve": 1},
]


class Seen:

    def __init__(self):
        self.n, self.g, self.per, self.start = {name: 1 for name in COUNT_FROM_ONE}, None, {}, {}

    def add(self, name, k=1):
        self.n[name] = self.n.get(name, 0) + k
        return self.value(name)

    def value(self, name):
        v = self.n.get(name, 0)
        return v if self.g is None else self.g * self.per.get(name, 0) + v

    def enter(self, g, per):
        self.g, self.per, self.start = g, per, dict(self.n)

    def leave(self, turns):
        got = {k: v - self.start.get(k, 0) for k, v in self.n.items() if v != self.start.get(k, 0)}
        assert got == {k: v for k, v in self.per.items() if v}, (got, self.per)
        for k, v in got.items():
            self.n[k] += v * (turns - 1)
        self.g, self.per = None, {}


COUNT_FROM_ONE = ("o", "zu", "am", "hc", "df", "dr", "xu")


def gnn_kernel(nc, a, out):
    def sb(name, shape, dt=F32):
        return nc.alloc_sbuf_tensor(name, shape, dt)

    def sem(name):
        return nc.alloc_semaphore(name)

    node_tab = nc.dram_tensor("node_tab", (N, 2), F32, kind="Internal").ap()
    xt = nc.dram_tensor("xt", (E, D), F32, kind="Internal").ap()
    gt = nc.dram_tensor("gt", (E, D), F32, kind="Internal").ap()
    xt_v = xt.rearrange("(p t) d -> p t d", p=P)
    gt_v = gt.rearrange("(p t) d -> p t d", p=P)
    ea_v = a["edge_attr_64"].rearrange("(p t) d -> p t d", p=P)
    x_v = a["x"].rearrange("(p t) d -> p t d", p=P)
    out_v = out.rearrange("(p t) d -> p t d", p=P)

    Xs = sb("Xs", [P, T, D])
    Y = sb("Y", [128, T, D])
    tmpA = sb("tmpA", [P, GC, D])
    tmpB = sb("tmpB", [P, GC, D])
    xdg = sb("xdg", [P, GC, D])
    din = sb("din", [P, DC, D])
    dout = sb("dout", [P, DC, D])
    dh = sb("dh", [P, DC, D])
    HT = sb("HT", [128, 2, 512])
    YT = sb("YT", [128, 2, 512])
    src_i = sb("src_i", [P, T], I32)
    dst_i = sb("dst_i", [P, T], I32)
    rep_i = sb("rep_i", [P, T], I32)
    sct_i = sb("sct_i", [P, T], I32)
    dstf = sb("dstf", [P, T])
    nextf = sb("nextf", [P, 1])
    next_i = sb("next_i", [P, 1], I32)
    same = sb("same", [P, T])
    notlast = sb("notlast", [P, T])
    infirst = sb("infirst", [P, T])
    inopen = sb("inopen", [P, T])
    dinvd = sb("dinvd", [P, T])
    dinvs = sb("dinvs", [P, T])
    invdeg = sb("invdeg", [P, T])
    S = sb("S", [P, T, HEADS])
    Sd = sb("Sd", [P, T, HEADS])
    Tg = sb("Tg", [P, T, 2])
    W8 = sb("W8", [P, T])
    st = sb("st", [P, GC, 6])
    sm = sb("sm", [P, 6, GC])
    ident = sb("ident", [128, 128])
    ones = sb("ones", [128, 128])
    Kc = sb("Kc", [P, P])
    KP = sb("KP", [P, P])
    Bm = sb("Bm", [P, P])
    diag = sb("diag", [P, HEADS, P])
    BW = sb("BW", [128, 8, 128])
    BV = sb("BV", [128, 2, 2 * HEADS])
    W1 = sb("W1", [128, HID])
    W2 = sb("W2", [HID, D])
    brow = sb("brow", [1, 4, D])
    c1b = sb("c1b", [P, D])
    b1c = sb("b1c", [128, 2])
    b2c = sb("b2c", [128, 1])
    carry = sb("carry", [P, D])
    lmax = sb("lmax", [1, 2])
    lmax_i = sb("lmax_i", [1, 1], I32)
    c8 = sb("c8", [P, 4])
    gru = tmpB[0:64, 0:4, :]
    gsm = sb("gsm", [64, 12])
    wtb = din[0:64, 0:2, :]
    BROW_L0, BROW_DENSE, BROW_L1, BROW_END = range(4)
    W_L0, W_SELF, W_NEIGH, W_ATT, W_HOP = 0, 1, 2, 3, 7

    wa = sb("wa", [128, 4, D])
    aB = sb("aB", [128, 2, 4, D])
    wg = sb("wg", [128, D])
    wwt = sb("wwt", [64, 2, D])
    bgc = sb("bgc", [64, 1])
    bwr = sb("bwr", [1, 3, D])


    epsc = sb("epsc", [P, 1])
    bcol = sb("bcol", [P, 8])
    mcol = sb("mcol", [P, 16])
    psT = [nc.alloc_psum_tensor(f"psT{i}", [128, 512], F32) for i in range(2)]
    psM = [nc.alloc_psum_tensor(f"psM{i}", [128, 512], F32) for i in range(2)]
    psO = [nc.alloc_psum_tensor(f"psO{i}", [128, 512], F32) for i in range(2)]
    psZ = nc.alloc_psum_tensor("psZ", [128, 512], F32)
    psS = nc.alloc_psum_tensor("psS", [128, 512], F32)

    s_in = sem("inputs_loaded")
    s_preset = sem("constants_preset")
    s_kcut = sem("carry_matrices_cut")
    s_dve = sem("dve_chain")
    s_gate = sem("gates_summed")
    s_act = sem("act_setup")
    s_um = sem("memory_updated")
    s_c1 = sem("c1_row_ready")
    s_ids = sem("ids_on_diagonals")
    s_kraw = sem("carry_matrices_raw")
    s_cnt = sem("counts_scanned")
    s_pay = sem("payload_ready")
    s_set = sem("setup_done")
    s_pe = sem("setup_product")
    s_tab = sem("node_table_written")
    s_gx = sem("src_rows_gathered")
    s_gt = sem("table_rows_gathered")
    s_gd = sem("dst_rows_gathered")
    s_xs = sem("dst_rows_stored")
    s_xl = sem("dst_rows_loaded")
    s_xu = sem("dst_rows_updated")
    s_ea = sem("edge_attr_loaded")
    s_var = sem("variances_ready")
    s_std = sem("roots_ready")
    s_h = sem("h_ready")
    s_hc = sem("h_copied")
    s_tr = sem("transposed")
    s_ht = sem("transposed_evacuated")
    s_m = sem("mid_ready")
    s_y = sem("mid_evacuated")
    s_o = sem("unit_ready")
    s_ou = sem("unit_used")
    s_am = sem("head_done")
    s_zu = sem("messages_used")
    s_dl = sem("dense_loaded")
    s_df = sem("dense_input_free")
    s_dr = sem("dense_result_ready")
    s_ds = sem("dense_result_stored")
    s_sum = sem("stage_sums_ready")
    s_st = sem("stage_done")
    s_fix = sem("carries_added")
    s_ct = sem("tails_ready")
    s_cp = sem("carries_ready")
    s_ex = sem("exp_input_ready")
    s_exd = sem("exp_done")
    s_g1 = sem("hop_rows_stored")
    s_out = sem("rows_scattered")

    PARTS = [(0, 120), (120, P)]

    def row(v):
        return v.rearrange("(a m) -> a m", a=1)

    def column(v):
        return v.rearrange("(p a) -> p a", a=1)

    loads = [
        (src_i[:, :], a["src"].rearrange("(p t) -> p t", p=P)),
        (dst_i[:, :], a["dst"].rearrange("(p t) -> p t", p=P)),
        (next_i[0:P - 1, :], a["dst"].rearrange("(p t) -> p t", p=P)[1:P, 0:1]),
        (gru[:, 0:3, :], a["L0_gnn_gru_w_ih"].rearrange("(g j) m -> j g m", g=3)),
        (gru[:, 3, :], row(a["L0_gnn_memory_weights"]).to_broadcast([64, D])),
        (gsm[:, 0:3], a["L0_gnn_gru_b_ih"].rearrange("(g j) -> j g", g=3)),
        (gsm[:, 3:6], a["L0_gnn_gru_b_hh"].rearrange("(g j) -> j g", g=3)),
        (W2[:, :], a["L1_gnn_W2"]),
        (b1c[:, 0:1], column(a["L1_gnn_b1"])),
        (bwr[:, 0, :], row(a["L0_gnn_gcn_bias"])),
        (bwr[:, 1, :], row(a["L1_gnn_b2"])),
        (bwr[:, 2, :], row(a["L3_gnn_b_w"])),
        (wwt[:, :, :], a["L3_gnn_W_w"].rearrange("(a i) o -> i a o", a=2)),
        (bgc[:, :], column(a["L3_gnn_b_g"])),
    ]
    for k, name in enumerate(("L3_gnn_a_src", "L3_gnn_a_dst")):
        loads.append((aB[:, k, :, :].rearrange("p h o -> p (h o)"),
                      a[name].rearrange("(a h) o -> a (h o)", a=1).to_broadcast([128, HEADS * D])))
    for k in range(2):
        h = slice(64 * k, 64 * k + 64)
        loads += [
            (Y[h, 0:64, :], a["L0_gnn_wt_w"].rearrange("(o i) m -> i o m", i=D)),
            (wtb[:, k, :], a["L0_gnn_wt_b"].rearrange("(o i) -> o i", i=D)),
            (W1[h, :], a["L1_gnn_W1"]),
            (b2c[h, :], column(a["L2_gnn_bias"])),
            (wa[h, :, :], a["L3_gnn_W_att"].rearrange("h i o -> i h o")),
            (wg[h, :], a["L3_gnn_W_g"]),
            (BW[h, W_SELF, h], a["L2_gnn_W_self"]),
            (BW[h, W_NEIGH, h], a["L2_gnn_W_neigh"]),
        ]
    NLOAD = 16 * len(loads)
    CHUNKS = STAGES * G
    CARRY = {0: ["sum"], 1: ["sum"], 2: ["sum"], 3: ["sum"], 4: ["sum", "messages"]}
    SOFTMAX = ["hold", "max", "hold", "den", "hold"]

    def cols(t, g, lo=0, n=GC):
        return t[0:P, bass.ds(g * GC + lo, n)] if len(t.shape) == 2 else t[0:P, bass.ds(g * GC + lo, n), :]

    def pairs(t, c):
        return t[0:P, c:c + 2, :].rearrange("p a b -> p (a b)")

    def unit_rows(ps):
        return ps[0:P, :].rearrange("p (c d) -> p c d", d=D)

    with nc.Block() as block:

        @block.sync
        def _(sp):
            see = Seen()

            def await_(semaphore, count):
                sp.wait_ge(semaphore, count)
                sp.nop(nofuse=True)

            def dense_load(c):
                for lo, hi in PARTS:
                    sp.dma_start(din[lo:hi, :, :], x_v[lo:hi, bass.ts(c, DC), :]).then_inc(s_dl, 16)

            def dense_store(c):
                for lo, hi in PARTS:
                    sp.dma_start(out_v[lo:hi, bass.ts(c, DC), :], dout[lo:hi, :, :]).then_inc(s_ds, 16)

            def x_store(g):
                for lo, hi in PARTS:
                    sp.dma_start(xt_v[lo:hi, bass.ts(g, GC), :], xdg[lo:hi, :, :]).then_inc(s_xs, 16)
                await_(s_xs, see.add("xs", 32))

            sp.wait_ge(s_preset, 3)
            for dst, src in loads:
                sp.dma_start(dst, src, allow_slow_non_contiguous=True).then_inc(s_in, 16)
            for lo, hi in PARTS:
                sp.dma_start(node_tab.rearrange("(p n) c -> p (n c)", p=P)[lo:hi, :],
                             tmpA[lo:hi, 0:25, :].rearrange("p a b -> p (a b)")).then_inc(s_ds, 16)
            sp.wait_ge(s_set, 1)
            dense_load(0)

            def chunk(stage, g, last):
                if stage == 0:
                    await_(s_gd, see.add("gd", 16 * GC))
                    x_store(g)
                await_(s_df, see.add("df"))
                if not last:
                    dense_load(g + (stage * G + 1))
                await_(s_dr, see.add("dr"))
                dense_store(g + stage * G)

            for stage in range(STAGES):
                if stage == 1:
                    sp.wait_ge(s_st, 1)
                    for g in range(G):
                        for lo, hi in PARTS:
                            sp.dma_start(Y[lo:hi, g * GC:(g + 1) * GC, :], ea_v[lo:hi, g * GC:(g + 1) * GC, :]).then_inc(s_ea, 16)
                turns = G if stage < STAGES - 1 else G - 1
                with sp.Fori(0, turns) as g:
                    see.enter(g, {"df": 1, "dr": 1, **({"gd": 16 * GC, "xs": 32} if stage == 0 else {})})
                    chunk(stage, g, False)
                    see.leave(turns)
                if turns < G:
                    chunk(stage, G - 1, True)
                with sp.Fori(0, G) as g:
                    see.enter(g, {"xu": 1, **({"xs": 32} if stage < 3 else {"g1": 32} if stage == 3 else {"out": 16 * GC})})
                    for lo, hi in PARTS:
                        sp.dma_start(xdg[lo:hi, :, :], xt_v[lo:hi, bass.ts(g, GC), :]).then_inc(s_xl, 16)
                    await_(s_xu, see.add("xu"))
                    if stage < 3:
                        x_store(g)
                    elif stage == 3:
                        for lo, hi in PARTS:
                            sp.dma_start(gt_v[lo:hi, bass.ts(g, GC), :], tmpB[lo:hi, :, :]).then_inc(s_g1, 16)
                        await_(s_g1, see.add("g1", 32))
                    else:
                        await_(s_out, see.add("out", 16 * GC))
                    see.leave(G)
            sp.wait_ge(s_ds, 32 * (CHUNKS + 1))

        @block.gpsimd
        def _(pool):
            see = Seen()
            nc.gpsimd.memset(BW[:, :, :], 0.0).then_inc(s_preset, 1)
            nc.gpsimd.memset(next_i[:, :], -1).then_inc(s_preset, 1)
            nc.gpsimd.memset(tmpA[:, :, :], 0.0).then_inc(s_preset, 1)
            nc.gpsimd.memset(ones[:, :], 1.0).then_inc(s_preset, 1)
            nc.gpsimd.memset(BV[:, :, :], 0.0).then_inc(s_preset, 1)
            nc.gpsimd.iota(rep_i[:, :], pattern=[[1, T]], base=-NOREP, channel_multiplier=T).then_inc(s_preset, 1)
            nc.gpsimd.memset(epsc[:, :], EPS).then_inc(s_preset, 1)
            for k, semaphore in enumerate((s_o, s_ou, s_zu, s_am, s_hc, s_df, s_dr, s_xu)):
                nc.gpsimd.memset(bcol[:, k:k + 1], 0.0).then_inc(semaphore, 1)
            nc.gpsimd.memset(ident[:, :], 0.0).then_inc(s_preset, 1)
            pool.wait_ge(s_preset, 8)
            nc.gpsimd.affine_select(out=ident[:, :], in_=ident[:, :], compare_op=ALU.not_equal, fill=1.0,
                                    base=0, pattern=[[-1, 128]], channel_multiplier=1).then_inc(s_preset, 1)
            pool.wait_ge(s_kraw, 3)
            nc.gpsimd.affine_select(out=Kc[:, :], in_=Kc[:, :], compare_op=ALU.is_ge, fill=0.0,
                                    base=-1, pattern=[[1, P]], channel_multiplier=-1).then_inc(s_kcut, 1)
            for m in (Bm, KP):
                nc.gpsimd.affine_select(out=m[:, :], in_=m[:, :], compare_op=ALU.is_ge, fill=0.0,
                                        base=-1, pattern=[[-1, P]], channel_multiplier=1).then_inc(s_kcut, 1)

            def gather(dst, table, rows, index, t, s):
                nc.gpsimd.indirect_dma_start(dst, None, table, bass.IndirectOffsetOnAxis(ap=index[:, t:t + 1], axis=0),
                                             bounds_check=rows - 1, oob_is_err=False).then_inc(s, 16)

            def scatter(table, rows, index, t, src, s):
                nc.gpsimd.indirect_dma_start(table, bass.IndirectOffsetOnAxis(ap=index[:, t:t + 1], axis=0), src, None,
                                             bounds_check=rows - 1, oob_is_err=False).then_inc(s, 16)

            def columns(g):
                return range(g * GC, (g + 1) * GC)

            pool.wait_ge(s_pay, 1)
            pool.wait_ge(s_ds, 32)
            for t in range(T):
                scatter(node_tab, N, sct_i, t, Tg[:, t, :], s_tab)
            pool.wait_ge(s_tab, 16 * T)
            for g in range(G):
                for t in columns(g):
                    gather(Tg[:, t, :], node_tab, N, src_i, t, s_gt)
                for t in columns(g):
                    gather(Xs[:, t, :], a["x"], N, src_i, t, s_gx)
                if g > 0:
                    pool.wait_ge(s_xs, 32 * g)
                for t in columns(g):
                    gather(xdg[:, t - g * GC, :], a["x"], N, dst_i, t, s_gd)
                pool.wait_ge(s_gt, 16 * GC * (g + 1))
                pool.wait_ge(s_gx, 16 * GC * (g + 1))
                pool.wait_ge(s_gd, 16 * GC * (g + 1))
            for stage in range(1, STAGES):
                pool.wait_ge(s_st, stage)
                if stage < 4:
                    pool.wait_ge(s_xs, 32 * G * (stage + 1))
                else:
                    pool.wait_ge(s_g1, 32 * G)
                for g in range(G):
                    for t in columns(g):
                        if stage < 4:
                            gather(Xs[:, t, :], xt, E, rep_i, t, s_gx)
                        else:
                            gather(Y[0:P, t, :], gt, E, rep_i, t, s_gx)
                    pool.wait_ge(s_gx, 16 * GC * (stage * G + g + 1))
            pool.wait_ge(s_ds, 32 * (CHUNKS + 1))
            for g in range(G):
                pool.wait_ge(s_xu, 4 * G + g + 2)
                for t in columns(g):
                    scatter(out, N, sct_i, t, xdg[:, t - g * GC, :], s_out)
            pool.wait_ge(s_out, 16 * T)

        @block.tensor
        def _(pe):
            see = Seen()

            def done(ins):
                ins.then_inc(s_pe, 1)

            pe.wait_ge(s_in, NLOAD)
            pe.wait_ge(s_preset, 9)
            done(nc.tensor.transpose(psO[0][:, 0:64], wtb.rearrange("p a b -> p (a b)"), ident[0:64, 0:64]))
            for h in range(HEADS):
                done(nc.tensor.transpose(psT[0][0:64, 128 * h:128 * h + 128], wa[:, h, :], ident[:, :]))
            done(nc.tensor.transpose(psT[1][0:64, 0:128], wg[:, :], ident[:, :]))
            pe.wait_ge(s_um, 2)
            done(nc.tensor.matmul(psS[:, 0:64], ones[0:64, :], diag[0:64, 0, 0:64], start=True, stop=True))
            done(nc.tensor.matmul(psO[1][0:1, 0:64], b1c[:, 1:2], W2[:, :], start=True, stop=True))
            done(nc.tensor.matmul(psO[1][0:1, 64:128], bgc[:, :], wwt[:, 1, :], start=True, stop=True))
            pe.wait_ge(s_act, 4)
            for h in range(HEADS):
                done(nc.tensor.matmul(psM[0][:, 64 * h:64 * h + 64], HT[0:64, 0, 128 * h:128 * h + 128],
                                      wwt[:, 0, :], start=True, stop=True))
            done(nc.tensor.matmul(psM[0][:, 256:320], HT[0:64, 1, 0:128], wwt[:, 1, :], start=True, stop=True))
            pe.wait_ge(s_ids, 2)
            done(nc.tensor.matmul(psS[0:P, 64:64 + P], ones[0:P, 0:P], diag[:, 1, :], start=True, stop=True))
            done(nc.tensor.matmul(psS[0:P, 192:192 + P], ones[0:P, 0:P], diag[:, 2, :], start=True, stop=True))
            pe.wait_ge(s_cnt, 1)
            pe.wait_ge(s_kcut, 3)
            done(nc.tensor.matmul(psS[0:P, 320:321], Kc[:, :], invdeg[:, T - 1:T], start=True, stop=True))
            done(nc.tensor.transpose(psS[0:1, 384:384 + P], c8[:, 0:1], ident[0:P, 0:P]))
            pe.wait_ge(s_c1, 1)
            done(nc.tensor.matmul(psO[1][0:P, 128:192], ones[0:1, 0:P], carry[0:1, :], start=True, stop=True))

            def transposes(src, col, bank):
                for q in range(UC // 2):
                    last = nc.tensor.transpose(psT[bank][:, q * P:(q + 1) * P], pairs(src, col + 2 * q), ident[0:P, 0:P])
                last.then_inc(s_tr, 1)

            def bias(k, r):
                nc.tensor.matmul(psO[k % 2][0:P, :], ones[0:1, 0:P], brow[0:1, r:r + 1, :].to_broadcast([1, UC, D]),
                                 start=True, stop=False)

            def free_result(k):
                n = see.add("o") - 1
                pe.wait_ge(s_ou, n if k == 0 else n - 1)

            def lin(src, n, w, r):
                pe.wait_ge(s_h, see.add("h"))
                for k in range(n + 1):
                    if k < n:
                        transposes(src, UC * k, k % 2)
                    if k >= 1:
                        u = k - 1
                        free_result(u)
                        bias(u, r)
                        pe.wait_ge(s_ht, see.add("ht"))
                        for q in range(UC // 2):
                            last = nc.tensor.matmul(psO[u % 2][0:P, 128 * q:128 * q + 128], HT[:, u % 2, q * P:(q + 1) * P],
                                                    BW[:, w, :], start=False, stop=(q == UC // 2 - 1))
                        last.then_inc(s_o, 1)

            def score(src, n, v):
                pe.wait_ge(s_h, see.add("h"))
                for k in range(n + 1):
                    if k < n:
                        transposes(src, UC * k, k % 2)
                    if k >= 1:
                        u = k - 1
                        free_result(u)
                        pe.wait_ge(s_ht, see.add("ht"))
                        for q in range(UC // 2):
                            last = nc.tensor.matmul(psO[u % 2][0:P, 8 * q:8 * q + 8], HT[:, u % 2, q * P:(q + 1) * P],
                                                    BV[:, v, :], start=True, stop=True)
                        last.then_inc(s_o, 1)

            def back(u, r):
                free_result(u)
                if r is not None:
                    bias(u, r)
                pe.wait_ge(s_y, see.add("y"))
                for q in range(UC // 2):
                    last = nc.tensor.matmul(psO[u % 2][0:P, 128 * q:128 * q + 128], YT[:, u % 2, q * P:(q + 1) * P],
                                            ident[:, :], start=(r is None), stop=(r is None or q == UC // 2 - 1))
                last.then_inc(s_o, 1)

            def relu_units(src, n, r):
                pe.wait_ge(s_h, see.add("h"))
                for k in range(n + 2):
                    if k < n:
                        transposes(src, UC * k, k % 2)
                    if 1 <= k <= n:
                        u = k - 1
                        pe.wait_ge(s_ht, see.add("ht"))
                        nc.tensor.matmul(psM[u % 2][:, 0:4 * P], BW[:, W_SELF, :], HT[:, u % 2, 0:4 * P],
                                         start=True, stop=True).then_inc(s_m, 1)
                    if k >= 2:
                        back(k - 2, r)

            def neigh_units(n):
                pe.wait_ge(s_h, see.add("h"))
                for u in range(n):
                    transposes(tmpA, UC * u, 0)
                    transposes(tmpB, UC * u, 1)
                    if u >= 1:
                        back(u - 1, None)
                    pe.wait_ge(s_ht, see.add("ht", 2))
                    nc.tensor.matmul(psM[u % 2][:, 0:4 * P], BW[:, W_SELF, :], HT[:, 0, 0:4 * P], start=True, stop=False)
                    nc.tensor.matmul(psM[u % 2][:, 0:4 * P], BW[:, W_NEIGH, :], HT[:, 1, 0:4 * P],
                                     start=False, stop=True).then_inc(s_m, 1)
                back(n - 1, None)

            def mlp_units(n):
                pe.wait_ge(s_hc, see.add("hc"))
                transposes(tmpA, 0, 0)
                for u in range(n):
                    if u + 1 < n:
                        transposes(tmpA, UC * (u + 1), (u + 1) % 2)
                    pe.wait_ge(s_ht, see.add("ht"))
                    for z in range(2):
                        half = slice(64 * z, 64 * z + 64)
                        last = nc.tensor.matmul(psM[z][:, 0:4 * P], W1[half, :], HT[half, u % 2, 0:4 * P], start=True, stop=True)
                    last.then_inc(s_m, 1)
                    free_result(u)
                    bias(u, BROW_L1)
                    pe.wait_ge(s_y, see.add("y"))
                    for q in range(UC // 2):
                        for z in range(2):
                            last = nc.tensor.matmul(psO[u % 2][0:P, 128 * q + 64 * z:128 * q + 64 * z + 64],
                                                    YT[:, z, q * P:(q + 1) * P], W2[:, :], start=False,
                                                    stop=(q == UC // 2 - 1 and z == 1))
                    last.then_inc(s_o, 1)

            def messages(n):
                for u in range(n):
                    src = tmpA if u % 2 == 0 else tmpB
                    pe.wait_ge(s_h, see.add("h"))
                    for k in range(HEADS + 1):
                        if k < HEADS:
                            transposes(src, UC * k, k % 2)
                        if k >= 1:
                            h = k - 1
                            if h == 0:
                                pe.wait_ge(s_zu, see.add("zu") - 1)
                            pe.wait_ge(s_ht, see.add("ht"))
                            for q in range(UC // 2):
                                last = nc.tensor.matmul(psZ[0:P, 128 * q:128 * q + 128], HT[:, h % 2, q * P:(q + 1) * P],
                                                        BW[:, W_ATT + h, :], start=(h == 0 and q == 0),
                                                       stop=(h == HEADS - 1 and q == UC // 2 - 1))
                            last.then_inc(s_am, 1)

            def carries(kinds, stage):
                for kind in kinds:
                    pe.wait_ge(s_ct, see.add("ct"))
                    if kind == "sum":
                        last = nc.tensor.matmul(psS[0:P, 0:D], Kc[:, :], Y[0:P, T - 1, :], start=True, stop=True)
                    elif kind == "messages":
                        last = nc.tensor.matmul(psS[0:P, 0:D], Kc[:, :], Xs[:, T - 1, :], start=True, stop=True)
                    elif kind == "den":
                        last = nc.tensor.matmul(psS[0:P, 0:HEADS], Kc[:, :], Sd[:, T - 1, :], start=True, stop=True)
                    elif kind == "hold":
                        last = nc.tensor.matmul(psS[0:P, 0:HEADS], Bm[:, :], Sd[:, 0, :], start=True, stop=True)
                    else:
                        last = nc.tensor.matmul(psS[0:P, 0:HEADS * P], ones[0:P, 0:P], diag[:, :, :], start=True, stop=True)
                    last.then_inc(s_cp, 1)

            for stage in range(STAGES):
                edge = {0: {"h": 1, "ht": GU, "o": GU}, 1: {}, 2: {"h": 1, "ht": GU, "o": GU, "y": GU},
                        3: {"h": 1, "ht": GU, "o": GU}, 4: {"h": GU, "ht": HEADS * GU, "zu": GU}}[stage]
                per = {"h": 2, "ht": 2 * DU, "o": 2 * DU, "y": DU}
                for k, v in edge.items():
                    per[k] = per.get(k, 0) + v
                with pe.Fori(0, G) as g:
                    see.enter(g, per)
                    if stage == 0:
                        lin(tmpA, GU, W_L0, BROW_L0)
                    elif stage == 2:
                        relu_units(tmpA, GU, None)
                    elif stage == 3:
                        score(tmpA, GU, 0)
                    elif stage == 4:
                        messages(GU)
                    lin(dh, DU, W_L0, BROW_DENSE)
                    relu_units(dh, DU, BROW_END)
                    see.leave(G)
                carries(CARRY[stage], stage)
                per = {0: {"h": 1, "ht": GU, "o": GU}, 1: {"hc": 1, "ht": GU, "y": GU, "o": GU},
                       2: {"h": 1, "ht": 2 * GU, "y": GU, "o": GU}, 3: {"h": 1, "ht": GU, "o": GU},
                       4: {"h": 1, "ht": GU, "o": GU}}[stage]
                if stage == 1:
                    see.add("hc", G)
                with pe.Fori(0, G) as g:
                    see.enter(g, per)
                    if stage == 0:
                        lin(tmpA, GU, W_L0, BROW_L0)
                    elif stage == 1:
                        mlp_units(GU)
                    elif stage == 2:
                        neigh_units(GU)
                    elif stage == 3:
                        score(tmpA, GU, 1)
                    else:
                        lin(tmpA, GU, W_HOP, BROW_END)
                    see.leave(G)
                if stage == 3:
                    carries(SOFTMAX, stage)

        @block.scalar
        def _(act):
            see = Seen()
            act.wait_ge(s_preset, 9)
            act.wait_ge(s_gate, 1)
            nc.scalar.activation(gsm[:, 9:11], gsm[:, 9:11], ACT.Sigmoid).then_inc(s_act, 1)
            act.wait_ge(s_gate, 2)
            nc.scalar.activation(gsm[:, 11:12], gsm[:, 11:12], ACT.Tanh).then_inc(s_act, 1)
            act.wait_ge(s_pe, 6)
            nc.scalar.activation(HT[0:64, 0, :], psT[0][0:64, :], ACT.Copy).then_inc(s_act, 1)
            nc.scalar.activation(HT[0:64, 1, 0:128], psT[1][0:64, 0:128], ACT.Copy).then_inc(s_act, 1)
            act.wait_ge(s_gate, 3)
            nc.scalar.activation(dinvd[:, :], dinvd[:, :], ACT.Sqrt).then_inc(s_act, 1)
            act.wait_ge(s_pe, 14)

            def evac(bank):
                act.wait_ge(s_tr, see.add("tr"))
                nc.scalar.activation(HT[:, bank, 0:4 * P], psT[bank][:, 0:4 * P], ACT.Copy).then_inc(s_ht, 1)

            def free_transposed(k):
                n = see.add("o") - 1
                act.wait_ge(s_o, n if k == 0 else n - 1)

            def lin(n):
                for k in range(n):
                    free_transposed(k)
                    evac(k % 2)

            def relu(u):
                act.wait_ge(s_m, see.add("m"))
                nc.scalar.activation(YT[:, u % 2, 0:4 * P], psM[u % 2][:, 0:4 * P], ACT.Relu, bias=b2c[:, 0:1]).then_inc(s_y, 1)

            def relu_units(n):
                for k in range(n + 1):
                    if k < n:
                        free_transposed(k)
                        evac(k % 2)
                    if k >= 1:
                        relu(k - 1)

            def neigh_units(n):
                for u in range(n):
                    free_transposed(u)
                    if u > 0:
                        act.wait_ge(s_m, see.value("m"))
                    evac(0)
                    evac(1)
                    relu(u)

            def mlp_units(n):
                for k in range(n + 1):
                    if k < n:
                        free_transposed(k)
                        evac(k % 2)
                    if k >= 1:
                        act.wait_ge(s_m, see.add("m"))
                        o = see.value("o") - (2 if k < n else 1)
                        act.wait_ge(s_o, o)
                        for z in range(2):
                            last = nc.scalar.activation(YT[:, z, 0:4 * P], psM[z][:, 0:4 * P], ACT.Relu, bias=b1c[:, 0:1])
                        last.then_inc(s_y, 1)

            def messages(n):
                for u in range(n):
                    for h in range(HEADS):
                        m = see.add("am") - 1
                        if u == 0 and h == 0:
                            act.wait_ge(s_o, see.value("o"))
                        act.wait_ge(s_am, m if h == 0 else m - 1)
                        evac(h % 2)

            def roots(n):
                act.wait_ge(s_var, see.add("var"))
                nc.scalar.activation(sm[:, 5, 0:n], sm[:, 2, 0:n], ACT.Sqrt, bias=epsc[:, 0:1], scale=1.0 / D).then_inc(s_std, 1)

            def copy_h(dst, src):
                nc.scalar.activation(dst, src, ACT.Copy).then_inc(s_hc, 1)

            for stage in range(STAGES):
                per = {"h": 2, "tr": 2 * DU, "o": 2 * DU, "m": DU, "var": 3 if stage < 4 else 2, **({"gt": 16 * GC} if stage == 0 else {})}
                edge = {0: {"h": 1, "tr": GU, "o": GU}, 1: {}, 2: {"h": 1, "tr": GU, "o": GU, "m": GU},
                        3: {"h": 1, "tr": GU, "o": GU}, 4: {"h": GU, "tr": HEADS * GU, "am": HEADS * GU}}[stage]
                for k, v in edge.items():
                    per[k] = per.get(k, 0) + v
                with act.Fori(0, G) as g:
                    see.enter(g, per)
                    if stage == 0:
                        act.wait_ge(s_gt, see.add("gt", 16 * GC))
                        nc.scalar.activation(cols(dinvs, g), Tg[:, bass.ts(g, GC), 1], ACT.Sqrt, bias=ones[0:P, 0:1]).then_inc(s_std, 1)
                    if stage < 4:
                        roots(GC)
                    if stage in (0, 2, 3):
                        act.wait_ge(s_h, see.add("h"))
                        copy_h(cols(Xs if stage == 3 else Y, g), tmpA[:, :, :])
                    if stage < 4:
                        roots(DC)
                    if stage in (0, 3):
                        lin(GU)
                    elif stage == 2:
                        relu_units(GU)
                    elif stage == 4:
                        see.add("h", GU)
                        messages(GU)
                        roots(DC)
                    see.add("h", 2)
                    lin(DU)
                    roots(DC)
                    relu_units(DU)
                    see.leave(G)
                per = {0: {"h": 1, "tr": GU, "o": GU, "var": 1}, 1: {"tr": GU, "m": GU, "o": GU},
                       2: {"h": 1, "tr": 2 * GU, "m": GU, "o": GU, "var": 1}, 3: {"h": 1, "tr": GU, "o": GU, "var": 1},
                       4: {"h": 1, "tr": GU, "o": GU}}[stage]
                if stage == 1:
                    act.wait_ge(s_sum, 2)
                with act.Fori(0, G) as g:
                    see.enter(g, per)
                    if stage in (0, 2, 3):
                        roots(GC)
                    if stage == 1:
                        act.wait_ge(s_tr, see.value("tr"))
                        copy_h(tmpA[:, :, :], cols(Y, g))
                        mlp_units(GU)
                    else:
                        see.add("h")
                        if stage == 2:
                            neigh_units(GU)
                        else:
                            lin(GU)
                    see.leave(G)
                if stage == 3:
                    act.wait_ge(s_ex, 1)
                    nc.scalar.activation(S[:, :, :], S[:, :, :], ACT.Exp).then_inc(s_exd, 1)

        @block.vector
        def _(dve):
            see = Seen()
            v = nc.vector

            def chain(ins):
                ins.then_inc(s_dve, 1)
                see.add("dve")

            def settle():
                dve.wait_ge(s_dve, see.value("dve"))

            def step(ins):
                chain(ins)
                settle()

            marks = {"gate": (0, s_gate), "set": (1, s_set), "df": (2, s_df), "dr": (3, s_dr), "ct": (4, s_ct),
                     "sum": (5, s_sum), "xu": (6, s_xu), "st": (7, s_st), "fix": (8, s_fix)}
            see.add("gate", 2)

            def mark(name):
                k, semaphore = marks[name]
                n = see.add(name)
                if not isinstance(n, int) or n > 1:
                    dve.wait_ge(semaphore, n - 1)
                v.memset(mcol[:, k:k + 1], 0.0).then_inc(semaphore, 1)

            dve.wait_ge(s_in, NLOAD)
            dve.wait_ge(s_preset, 9)
            step(v.tensor_tensor(gru[:, 0:3, :], gru[:, 0:3, :], gru[:, 3:4, :].to_broadcast([64, 3, D]), ALU.mult))
            step(v.tensor_reduce(gsm[:, 6:9], gru[:, 0:3, :], AX.X, ALU.add))
            step(v.tensor_tensor(gsm[:, 6:9], gsm[:, 6:9], gsm[:, 0:3], ALU.add))
            v.tensor_tensor(gsm[:, 9:11], gsm[:, 6:8], gsm[:, 3:5], ALU.add).then_inc(s_gate, 1)
            dve.wait_ge(s_act, 1)
            step(v.tensor_tensor(gsm[:, 11:12], gsm[:, 9:10], gsm[:, 5:6], ALU.mult))
            v.tensor_tensor(gsm[:, 11:12], gsm[:, 11:12], gsm[:, 8:9], ALU.add).then_inc(s_gate, 1)
            v.tensor_scalar(b1c[:, 1:2], b1c[:, 0:1], 0.0, None, ALU.max).then_inc(s_um, 1)
            dve.wait_ge(s_act, 2)
            step(v.tensor_scalar(gsm[:, 10:11], gsm[:, 10:11], -1.0, 1.0, ALU.mult, ALU.add))
            step(v.tensor_tensor(gsm[:, 11:12], gsm[:, 11:12], gsm[:, 10:11], ALU.mult))
            v.tensor_scalar(diag[0:64, 0, 0:64], ident[0:64, 0:64], gsm[:, 11:12], None, ALU.mult).then_inc(s_um, 1)
            chain(v.tensor_copy(dstf[:, :], dst_i[:, :]))
            chain(v.tensor_copy(nextf[:, :], next_i[:, :]))
            chain(v.memset(same[:, 0:1], 0.0))
            chain(v.memset(W8[:, :], 1.0))
            settle()
            v.tensor_scalar(diag[:, 1, :], ident[0:P, 0:P], dstf[:, 0:1], None, ALU.mult).then_inc(s_ids, 1)
            v.tensor_scalar(diag[:, 2, :], ident[0:P, 0:P], dstf[:, T - 1:T], None, ALU.mult).then_inc(s_ids, 1)
            chain(v.tensor_tensor(same[:, 1:T], dstf[:, 1:T], dstf[:, 0:T - 1], ALU.is_equal))
            chain(v.tensor_tensor(notlast[:, 0:T - 1], dstf[:, 1:T], dstf[:, 0:T - 1], ALU.is_equal))
            chain(v.tensor_tensor(notlast[:, T - 1:T], dstf[:, T - 1:T], nextf[:, :], ALU.is_equal))
            chain(v.tensor_scalar(infirst[:, :], dstf[:, :], dstf[:, 0:1], None, ALU.is_equal))
            chain(v.tensor_tensor(c8[:, 1:2], dstf[:, 0:1], nextf[:, :], ALU.not_equal))
            settle()
            chain(v.tensor_scalar(inopen[:, :], dstf[:, :], dstf[:, T - 1:T], notlast[:, T - 1:T], ALU.is_equal, ALU.mult))
            chain(v.tensor_reduce(c8[:, 0:1], infirst[:, :], AX.X, ALU.add))
            v.tensor_tensor_scan(invdeg[:, :], same[:, :], W8[:, :], 0.0, ALU.mult, ALU.add).then_inc(s_cnt, 1)
            dve.wait_ge(s_pe, 16)
            v.tensor_scalar(Kc[:, :], psS[0:P, 64:64 + P], dstf[:, T - 1:T], None, ALU.is_equal).then_inc(s_kraw, 1)
            v.tensor_scalar(KP[:, :], psS[0:P, 192:192 + P], dstf[:, 0:1], None, ALU.is_equal).then_inc(s_kraw, 1)
            v.tensor_scalar(Bm[:, :], psS[0:P, 192:192 + P], dstf[:, 0:1], c8[:, 1:2], ALU.is_equal, ALU.mult).then_inc(s_kraw, 1)
            dve.wait_ge(s_pe, 18)
            chain(v.tensor_copy(c8[:, 2:3], psS[0:P, 320:321]))
            chain(v.tensor_reduce(lmax[:, 0:1], psS[0:1, 384:384 + P], AX.X, ALU.max))
            dve.wait_ge(s_cnt, 1)
            settle()
            chain(v.scalar_tensor_tensor(invdeg[:, :], infirst[:, :], c8[:, 2:3], invdeg[:, :], ALU.mult, ALU.add))
            chain(v.tensor_copy(lmax_i[:, :], lmax[:, 0:1]))
            chain(v.tensor_copy(Tg[:, :, 0], rep_i[:, :]))
            settle()
            chain(v.tensor_copy(Tg[:, :, 1], invdeg[:, :]))
            chain(v.tensor_scalar(dinvd[:, :], invdeg[:, :], 1.0, None, ALU.add))
            settle()
            v.scalar_tensor_tensor(sct_i[:, :], notlast[:, :], float(2 * N), dstf[:, :], ALU.mult, ALU.add).then_inc(s_pay, 1)
            mark("gate")
            step(v.tensor_scalar(invdeg[:, :], invdeg[:, :], 1.0, None, ALU.max))
            dve.wait_ge(s_act, 5)
            chain(v.reciprocal(dinvd[:, :], dinvd[:, :]))
            chain(v.reciprocal(invdeg[:, :], invdeg[:, :]))
            dve.wait_ge(s_kcut, 3)
            chain(v.tensor_scalar(KP[:, :], KP[:, :], -1.0, BIG, ALU.add, ALU.mult))
            first_len = dve.value_load(lmax_i[0:1, 0:1], min_val=1, max_val=T)
            dve.wait_ge(s_pe, 14)
            chain(v.tensor_tensor(Y[:, 0:64, :], Y[:, 0:64, :], psS[:, 0:64].unsqueeze(1).to_broadcast([128, 64, D]), ALU.mult))
            for k in range(2):
                chain(v.tensor_tensor(Y[:, 64 + 4 * k:68 + 4 * k, :], wa[:, :, :], aB[:, k, :, :], ALU.mult))
            settle()
            chain(v.tensor_reduce(YT[:, 0, 0:64], Y[:, 0:64, :], AX.X, ALU.add))
            chain(v.tensor_reduce(YT[:, 1, 0:8], Y[:, 64:72, :], AX.X, ALU.add))
            chain(v.tensor_copy(brow[:, BROW_L0, :], bwr[:, 0, :]))
            chain(v.tensor_copy(brow[:, BROW_L1, :], bwr[:, 1, :]))
            chain(v.tensor_tensor(brow[:, BROW_END, :], psO[1][0:1, 64:128], bwr[:, 2, :], ALU.add))
            v.tensor_tensor(carry[0:1, :], psO[1][0:1, 0:64], bwr[:, 1, :], ALU.add).then_inc(s_c1, 1)
            dve.wait_ge(s_c1, 1)
            chain(v.tensor_tensor(brow[:, BROW_DENSE, :], carry[0:1, :], bwr[:, 0, :], ALU.add))
            settle()
            for k in range(2):
                h = slice(64 * k, 64 * k + 64)
                chain(v.tensor_tensor(BW[h, W_L0, h], YT[h, 0, 0:64], psO[0][h, 0:64], ALU.add))
                chain(v.tensor_copy(BW[h, W_HOP, h], psM[0][h, 256:320]))
                for j in range(HEADS):
                    chain(v.tensor_scalar(BW[h, W_ATT + j, h], psM[0][h, 64 * j:64 * j + 64], 1.0 / HEADS, None, ALU.mult))
                for j in range(2):
                    chain(v.tensor_copy(BV[h, j, 4 * k:4 * k + 4], YT[h, 1, 4 * j:4 * j + 4]))
            dve.wait_ge(s_pe, 19)
            chain(v.tensor_copy(c1b[:, :], psO[1][0:P, 128:192]))
            settle()
            mark("set")

            def wide(col, n):
                return col.unsqueeze(2).to_broadcast([P, n, D])

            def norm_relu(x, dst, n, scale=None, signal=None):
                for j in range(n):
                    last = v.bn_stats(st[:, j, :], x(j))
                step(last)
                k = sm[:, :, 0:n]
                chain(v.tensor_tensor(k[:, 0, :], st[:, 0:n, 1], st[:, 0:n, 4], ALU.add))
                chain(v.tensor_tensor(k[:, 1, :], st[:, 0:n, 1], st[:, 0:n, 4], ALU.subtract))
                chain(v.tensor_tensor(k[:, 2, :], st[:, 0:n, 2], st[:, 0:n, 5], ALU.add))
                settle()
                chain(v.tensor_scalar(k[:, 4, :], k[:, 0, :], 0.5, None, ALU.mult))
                chain(v.scalar_tensor_tensor(k[:, 3, :], k[:, 1, :], D / 4.0, k[:, 1, :], ALU.mult, ALU.mult))
                settle()
                v.tensor_tensor(k[:, 2, :], k[:, 2, :], k[:, 3, :], ALU.add).then_inc(s_var, 1)
                chain(v.tensor_tensor(dst, x(None), wide(k[:, 4, :], n), ALU.subtract))
                dve.wait_ge(s_std, see.add("std"))
                step(v.reciprocal(k[:, 5, :], k[:, 5, :]))
                if scale is not None:
                    step(v.tensor_tensor(k[:, 5, :], k[:, 5, :], scale, ALU.mult))
                ins = v.scalar_tensor_tensor(dst, dst, 0.0, wide(k[:, 5, :], n), ALU.max, ALU.mult)
                if signal is None:
                    step(ins)
                else:
                    ins.then_inc(signal, 1)

            def group_cols(t, g):
                return lambda j: cols(t, g) if j is None else t[0:P, g * GC + j, :]

            def buffer_cols(t):
                return lambda j: t[:, :, :] if j is None else t[:, j, :]

            def add_units(at, n, base=None, free=None):
                for k in range(n):
                    dve.wait_ge(s_o, see.add("o"))
                    v.tensor_tensor(at(k), (base or at)(k), unit_rows(psO[k % 2]), ALU.add).then_inc(s_ou, 1)
                dve.wait_ge(s_ou, see.value("o"))

            def dense(first):
                if first:
                    dve.wait_ge(s_dl, see.add("dl", 32))
                    norm_relu(buffer_cols(din), dh[:, :, :], DC, signal=s_h)
                else:
                    dve.wait_ge(s_ds, see.add("ds", 32))
                    at = lambda k: dout[:, UC * k:UC * k + UC, :]
                    add_units(at, DU, base=lambda k: din[:, UC * k:UC * k + UC, :])
                    mark("df")
                    norm_relu(buffer_cols(dout), dh[:, :, :], DC, signal=s_h)
                    add_units(at, DU)
                    mark("dr")

            def scan_sums(dst, src):
                with dve.Fori(0, D // 4) as f:
                    for k in range(4):
                        v.tensor_tensor_scan(dst[0:P, :, f * 4 + k], same[:, :], src[0:P, :, f * 4 + k], 0.0, ALU.mult, ALU.add)

            def carry_sums(dst):
                mark("ct")
                dve.wait_ge(s_ct, see.value("ct"))
                dve.wait_ge(s_cp, see.add("cp"))
                step(v.tensor_copy(carry[:, :], psS[0:P, 0:D]))
                with dve.Fori(0, first_len) as t:
                    v.scalar_tensor_tensor(dst[0:P, t, :], carry[:, :], infirst[:, bass.ts(t, 1)], dst[0:P, t, :], ALU.mult, ALU.add)
                mark("fix")
                dve.wait_ge(s_fix, see.value("fix"))

            def carry_heads(mask):
                dve.wait_ge(s_cp, see.add("cp"))
                step(v.tensor_copy(carry[:, 0:HEADS], psS[0:P, 0:HEADS]))
                for h in range(HEADS):
                    chain(v.scalar_tensor_tensor(Sd[:, :, h], mask[:, :], carry[:, h:h + 1], Sd[:, :, h], ALU.mult, ALU.add))
                settle()

            def tails_out():
                mark("ct")

            def hold():
                step(v.tensor_scalar(W8[:, :], notlast[:, :], -1.0, 1.0, ALU.mult, ALU.add))
                step(v.tensor_tensor(Sd[:, :, :], Sd[:, :, :], W8[:, :].unsqueeze(2).to_broadcast([P, T, HEADS]), ALU.mult))
                for h in range(HEADS):
                    chain(v.tensor_tensor_scan(Sd[:, ::-1, h], notlast[:, ::-1], Sd[:, ::-1, h], 0.0, ALU.mult, ALU.add))
                settle()
                tails_out()
                carry_heads(inopen)

            def softmax():
                hold()
                step(v.tensor_tensor(S[:, :, :], S[:, :, :], Sd[:, :, :], ALU.add))
                step(v.scalar_tensor_tensor(S[:, :, :], S[:, :, :], SLOPE, S[:, :, :], ALU.mult, ALU.max))
                step(v.tensor_scalar(W8[:, :], same[:, :], -1.0, BIG, ALU.add, ALU.mult))
                for h in range(HEADS):
                    chain(v.tensor_tensor_scan(Sd[:, :, h], W8[:, :], S[:, :, h], -BIG, ALU.add, ALU.max))
                settle()
                for h in range(HEADS):
                    chain(v.tensor_scalar(diag[:, h, :], ident[0:P, 0:P], Sd[:, T - 1, h:h + 1], None, ALU.mult))
                settle()
                tails_out()
                dve.wait_ge(s_cp, see.add("cp"))
                tails = psS[0:P, 0:HEADS * P].rearrange("p (h q) -> p h q", h=HEADS)
                step(v.tensor_tensor(diag[:, :, :], tails, KP[:, :].unsqueeze(1).to_broadcast([P, HEADS, P]), ALU.add))
                chain(v.tensor_reduce(carry[:, 0:HEADS], diag[:, :, :], AX.X, ALU.max))
                chain(v.tensor_scalar(W8[:, :], infirst[:, :], -1.0, BIG, ALU.add, ALU.mult))
                settle()
                for h in range(HEADS):
                    chain(v.scalar_tensor_tensor(Sd[:, :, h], W8[:, :], carry[:, h:h + 1], Sd[:, :, h], ALU.add, ALU.max))
                settle()
                hold()
                v.tensor_tensor(S[:, :, :], S[:, :, :], Sd[:, :, :], ALU.subtract).then_inc(s_ex, 1)
                dve.wait_ge(s_exd, 1)
                for h in range(HEADS):
                    chain(v.tensor_tensor_scan(Sd[:, :, h], same[:, :], S[:, :, h], 0.0, ALU.mult, ALU.add))
                settle()
                tails_out()
                carry_heads(infirst)
                hold()
                step(v.tensor_scalar(Sd[:, :, :], Sd[:, :, :], 1e-16, None, ALU.max))
                step(v.reciprocal(Sd[:, :, :], Sd[:, :, :]))
                step(v.tensor_tensor(S[:, :, :], S[:, :, :], Sd[:, :, :], ALU.mult))

            def weighted(g, u):
                dst = (tmpA if u % 2 == 0 else tmpB)[:, 0:HEADS * UC, :].rearrange("p (h c) d -> p h c d", h=HEADS)
                for h in range(HEADS):
                    last = v.tensor_tensor(dst[:, h, :, :], cols(Xs, g, UC * u, UC),
                                           S[:, bass.ds(g * GC + UC * u, UC), h:h + 1].to_broadcast([P, UC, D]), ALU.mult)
                last.then_inc(s_h, 1)

            def take_messages(g, u):
                dve.wait_ge(s_am, see.add("am", HEADS))
                v.tensor_scalar(cols(Xs, g, UC * u, UC), unit_rows(psZ), 1.0, None, ALU.mult).then_inc(s_zu, 1)

            def edge_work(stage, g):
                if stage < 4:
                    dve.wait_ge(s_gx, see.add("gx", 16 * GC))
                rows = group_cols(Xs, g)
                at = lambda k: cols(Xs, g, UC * k, UC)
                if stage == 0:
                    dve.wait_ge(s_gt, see.add("gt", 16 * GC))
                    chain(v.tensor_scalar(cols(rep_i, g), Tg[:, bass.ts(g, GC), 0], float(NOREP), None, ALU.add))
                    dve.wait_ge(s_std, see.add("std"))
                    step(v.reciprocal(cols(dinvs, g), cols(dinvs, g)))
                    dve.wait_ge(s_hc, see.add("hc") - 1)
                    norm_relu(rows, tmpA[:, :, :], GC, scale=cols(dinvs, g), signal=s_h)
                    return lambda: add_units(at, GU)
                if stage == 1:
                    norm_relu(rows, tmpA[:, :, :], GC)
                    chain(v.tensor_tensor(cols(Xs, g), cols(Xs, g), c1b[:, :].unsqueeze(1).to_broadcast([P, GC, D]), ALU.add))
                    step(v.tensor_tensor(cols(Y, g), cols(Y, g), tmpA[:, :, :], ALU.add))
                    return lambda: None
                if stage == 2:
                    dve.wait_ge(s_hc, see.add("hc") - 1)
                    norm_relu(rows, tmpA[:, :, :], GC, signal=s_h)
                    return lambda: add_units(at, GU)
                if stage == 3:
                    dve.wait_ge(s_hc, see.add("hc") - 1)
                    norm_relu(rows, tmpA[:, :, :], GC, signal=s_h)

                    def take():
                        take_scores(S, g)
                    return take
                for u in range(GU + 1):
                    if u < GU:
                        weighted(g, u)
                    if u >= 1:
                        take_messages(g, u - 1)
                return lambda: None

            def take_scores(dst, g):
                for k in range(GU):
                    dve.wait_ge(s_o, see.add("o"))
                    v.tensor_scalar(cols(dst, g, UC * k, UC), psO[k % 2][0:P, 0:UC * HEADS].rearrange("p (c h) -> p c h", h=HEADS),
                                    1.0, None, ALU.mult).then_inc(s_ou, 1)
                dve.wait_ge(s_ou, see.value("o"))

            def dst_work(stage, g):
                at = lambda k: xdg[:, UC * k:UC * k + UC, :]
                dve.wait_ge(s_xl, see.add("xl", 32))
                if stage == 0:
                    norm_relu(buffer_cols(xdg), tmpA[:, :, :], GC, scale=cols(dinvd, g))
                    step(v.tensor_tensor(tmpA[:, :, :], tmpA[:, :, :], cols(Y, g), ALU.add))
                    v.tensor_tensor(tmpA[:, :, :], tmpA[:, :, :], wide(cols(dinvd, g), GC), ALU.mult).then_inc(s_h, 1)
                    add_units(at, GU)
                elif stage == 1:
                    add_units(at, GU)
                elif stage == 2:
                    chain(v.tensor_tensor(tmpB[:, :, :], cols(Y, g), wide(cols(invdeg, g), GC), ALU.mult))
                    norm_relu(buffer_cols(xdg), tmpA[:, :, :], GC, signal=s_h)
                    add_units(at, GU)
                elif stage == 3:
                    norm_relu(buffer_cols(xdg), tmpA[:, :, :], GC, signal=s_h)
                    chain(v.tensor_tensor(tmpB[:, :, :], cols(Y, g), wide(cols(invdeg, g), GC), ALU.mult))
                    take_scores(Sd, g)
                else:
                    v.tensor_tensor(tmpA[:, :, :], cols(Y, g), wide(cols(invdeg, g), GC), ALU.mult).then_inc(s_h, 1)
                    step(v.tensor_tensor(xdg[:, :, :], xdg[:, :, :], cols(Xs, g), ALU.add))
                    add_units(at, GU)
                mark("xu")

            for stage in range(STAGES):
                if stage == 1:
                    dve.wait_ge(s_ea, 32 * G)
                if stage == 4:
                    dve.wait_ge(s_g1, 32 * G)
                with dve.Fori(0, G) as g:
                    see.enter(g, PER[stage])
                    rest = edge_work(stage, g)
                    dense(True)
                    rest()
                    dense(False)
                    see.leave(G)
                if stage in (0, 2, 3):
                    dve.wait_ge(s_hc, see.value("hc"))
                if stage == 4:
                    dve.wait_ge(s_gx, 16 * T * 5)
                    dve.wait_ge(s_zu, GU * G + 1)
                scan_sums(Y, Xs if stage == 3 else Y)
                carry_sums(Y)
                if stage == 4:
                    scan_sums(Xs, Xs)
                    carry_sums(Xs)
                mark("sum")
                if stage == 1:
                    see.add("hc", G)
                with dve.Fori(0, G) as g:
                    see.enter(g, DPER[stage])
                    dst_work(stage, g)
                    see.leave(G)
                if stage == 3:
                    step(v.memset(Y[:, :, :], 0.0))
                mark("st")
                if stage == 3:
                    softmax()


_INS = ['x', 'src', 'dst', 'edge_attr_64', 'L0_gnn_memory_weights', 'L0_gnn_gru_w_ih', 'L0_gnn_gru_b_ih',
        'L0_gnn_gru_b_hh', 'L0_gnn_wt_w', 'L0_gnn_wt_b', 'L0_gnn_gcn_bias', 'L1_gnn_W1', 'L1_gnn_b1', 'L1_gnn_W2',
        'L1_gnn_b2', 'L2_gnn_W_self', 'L2_gnn_W_neigh', 'L2_gnn_bias', 'L3_gnn_W_att', 'L3_gnn_a_src', 'L3_gnn_a_dst',
        'L3_gnn_W_g', 'L3_gnn_b_g', 'L3_gnn_W_w', 'L3_gnn_b_w']


def kernel(**inputs):
    import concourse.bacc as _bacc
    from concourse.bass_utils import run_bass_kernel_spmd as _run

    nc = _bacc.Bacc("TRN2", target_bir_lowering=False, num_devices=1)
    arrays, args = {}, {}
    for name in _INS:
        v = np.ascontiguousarray(inputs[name])
        arrays[f"in_{name}"] = v
        args[name] = nc.dram_tensor(f"in_{name}", v.shape, mybir.dt.from_np(v.dtype), kind="ExternalInput").ap()
    out = nc.dram_tensor("out_0", (N, D), F32, kind="ExternalOutput").ap()
    gnn_kernel(nc, args, out)
    return _run(nc, [arrays], core_ids=[0]).results[0]["out_0"]
```

```python
import numpy as np
import concourse.bass as bass
from concourse import mybir

F32 = mybir.dt.float32
I32 = mybir.dt.int32
ALU = mybir.AluOpType
ACT = mybir.ActivationFunctionType
AX = mybir.AxisListType

N, E, D = 100000, 25000, 64
P = 125
T = E // P
G = 5
GC = T // G
UC = 8
GU = GC // UC
NODES = N // P
STAGES = 5
DC = 32
DU = DC // UC
HC, HU = DC // 2, DU // 2
LONE = 5
DENSE_STAGES = (1, 3)
HEADS = 4
HID = 2 * D
EPS = 1e-5
SLOPE = 0.2
BIG = 1e30
NOREP = 32768


_NORM = 8


def _turn(dense=False, **edge):
    chunk = {"dl": 32, "ds": 32, "df": 1, "dr": 1, "std": 4, "o": 2 * DU, "dve": 4 * _NORM} if dense else {}
    return {k: edge.get(k, 0) + chunk.get(k, 0) for k in {**edge, **chunk}}


TURN = {
    "rows": _turn(True, gx=16 * GC, hc=1, std=1, o=GU, dve=_NORM),
    "lone": _turn(True),
    "table": _turn(True, gt=16 * GC, std=1, dve=3),
    1: _turn(1 in DENSE_STAGES, gx=16 * GC, std=1, dve=_NORM + 3),
    2: _turn(2 in DENSE_STAGES, gx=16 * GC, hc=1, std=1, o=GU, dve=_NORM),
    3: _turn(3 in DENSE_STAGES, gx=16 * GC, hc=1, std=1, o=GU, dve=_NORM),
    4: _turn(am=HEADS * GU),
}
BY_BUFFER = {"xl0": 32, "xl1": 32}
DST_TURN = [
    {"gd": 16 * GC, "xu": 1, "o": GU, "dve": _NORM + 3, "std": 1},
    {**BY_BUFFER, "xu": 1, "o": GU},
    {**BY_BUFFER, "xu": 1, "o": GU, "dve": _NORM + 1, "std": 1},
    {**BY_BUFFER, "xu": 1, "o": GU, "dve": _NORM + 1, "std": 1, "g1": 32},
    {**BY_BUFFER, "xu": 1, "o": GU, "dve": 1},
]


class Seen:

    def __init__(self):
        self.n, self.g, self.per, self.start = {name: 1 for name in COUNT_FROM_ONE}, None, {}, {}

    def add(self, name, k=1):
        self.n[name] = self.n.get(name, 0) + k
        return self.value(name)

    def value(self, name):
        v = self.n.get(name, 0)
        return v if self.g is None else self.g * self.per.get(name, 0) + v

    def by_pairs(self, engine, per, body):
        with engine.Fori(0, G // 2) as k:
            self.enter(k, {name: v if name in ("xl0", "xl1") else 2 * v for name, v in per.items()})
            body(k * 2, 0)
            body(k * 2 + 1, 1)
            self.leave(G // 2)
        body(G - 1, 0)

    def enter(self, g, per):
        self.g, self.per, self.start = g, per, dict(self.n)

    def leave(self, turns):
        got = {k: v - self.start.get(k, 0) for k, v in self.n.items() if v != self.start.get(k, 0)}
        assert got == {k: v for k, v in self.per.items() if v}, (got, self.per)
        for k, v in got.items():
            self.n[k] += v * (turns - 1)
        self.g, self.per = None, {}


COUNT_FROM_ONE = ("o", "zu", "am", "hc", "df", "dr", "xu", "g1")


def gnn_kernel(nc, a, out):
    def sb(name, shape, dt=F32):
        return nc.alloc_sbuf_tensor(name, shape, dt)

    def sem(name):
        return nc.alloc_semaphore(name)

    node_tab = nc.dram_tensor("node_tab", (N, 2), F32, kind="Internal").ap()
    xt = nc.dram_tensor("xt", (E, D), F32, kind="Internal").ap()
    gt = nc.dram_tensor("gt", (E, D), F32, kind="Internal").ap()
    xt_v = xt.rearrange("(p t) d -> p t d", p=P)
    gt_v = gt.rearrange("(p t) d -> p t d", p=P)
    ea_v = a["edge_attr_64"].rearrange("(p t) d -> p t d", p=P)
    x_v = a["x"].rearrange("(p t) d -> p t d", p=P)
    out_v = out.rearrange("(p t) d -> p t d", p=P)

    Xs = sb("Xs", [P, T, D])
    Y = sb("Y", [128, T, D])
    tmpA = sb("tmpA", [P, GC, D])
    tmpB = sb("tmpB", [P, GC, D])
    xdg = sb("xdg", [P, GC, D])
    din = sb("din", [P, DC, D])
    dbuf = sb("dbuf", [P, 2 * DC, D])
    dout = dbuf[:, 0:DC, :]
    dh = dbuf[:, DC:2 * DC, :]
    xd = [xdg, dbuf[:, 0:GC, :]]
    HT = sb("HT", [128, 2, 512])
    YT = sb("YT", [128, 2, 512])
    src_i = sb("src_i", [P, T], I32)
    dst_i = sb("dst_i", [P, T], I32)
    rep_i = sb("rep_i", [P, T], I32)
    sct_i = sb("sct_i", [P, T], I32)
    dstf = sb("dstf", [P, T])
    nextf = sb("nextf", [P, 1])
    next_i = sb("next_i", [P, 1], I32)
    same = sb("same", [P, T])
    notlast = sb("notlast", [P, T])
    infirst = sb("infirst", [P, T])
    inopen = sb("inopen", [P, T])
    dinvd = sb("dinvd", [P, T])
    dinvs = sb("dinvs", [P, T])
    invdeg = sb("invdeg", [P, T])
    S = sb("S", [P, T, HEADS])
    Sd = sb("Sd", [P, T, HEADS])
    Tg = sb("Tg", [P, T, 2])
    W8 = sb("W8", [P, T])
    st = sb("st", [P, GC, 6])
    sm = sb("sm", [P, 6, GC])
    ident = sb("ident", [128, 128])
    ones = sb("ones", [128, 128])
    Kc = sb("Kc", [P, P])
    KP = sb("KP", [P, P])
    Bm = sb("Bm", [P, P])
    diag = sb("diag", [P, HEADS, P])
    BW = sb("BW", [128, 8, 128])
    BV = sb("BV", [128, 2, 2 * HEADS])
    W1 = sb("W1", [128, HID])
    W2 = sb("W2", [HID, D])
    brow = sb("brow", [1, 4, D])
    c1b = sb("c1b", [P, D])
    b1c = sb("b1c", [128, 2])
    b2c = sb("b2c", [128, 1])
    carry = sb("carry", [P, D])
    lmax = sb("lmax", [1, 2])
    lmax_i = sb("lmax_i", [1, 1], I32)
    c8 = sb("c8", [P, 4])
    gru = tmpB[0:64, 0:4, :]
    gsm = sb("gsm", [64, 12])
    wtb = din[0:64, 0:2, :]
    BROW_L0, BROW_DENSE, BROW_L1, BROW_END = range(4)
    W_L0, W_SELF, W_NEIGH, W_ATT, W_HOP = 0, 1, 2, 3, 7

    wa = sb("wa", [128, 4, D])
    aB = sb("aB", [128, 2, 4, D])
    wg = sb("wg", [128, D])
    wwt = sb("wwt", [64, 2, D])
    bgc = sb("bgc", [64, 1])
    bwr = sb("bwr", [1, 3, D])


    epsc = sb("epsc", [P, 1])
    BF16 = mybir.dt.bfloat16
    ones_b = sb("ones_b", [3, P], BF16)
    parts_b = sb("parts_b", [3, 4, D], BF16)
    part = sb("part", [1, 3, 4 * D], BF16)
    rest = sb("rest", [1, 4 * D])
    bcol = sb("bcol", [P, 9])
    mcol = sb("mcol", [P, 16])
    psT = [nc.alloc_psum_tensor(f"psT{i}", [128, 512], F32) for i in range(2)]
    psM = [nc.alloc_psum_tensor(f"psM{i}", [128, 512], F32) for i in range(2)]
    psO = [nc.alloc_psum_tensor(f"psO{i}", [128, 512], F32) for i in range(2)]
    psZ = nc.alloc_psum_tensor("psZ", [128, 512], F32)
    psS = nc.alloc_psum_tensor("psS", [128, 512], F32)

    s_in = sem("inputs_loaded")
    s_preset = sem("constants_preset")
    s_kcut = sem("carry_matrices_cut")
    s_dve = sem("dve_chain")
    s_gate = sem("gates_summed")
    s_act = sem("act_setup")
    s_um = sem("memory_updated")
    s_c1 = sem("c1_row_ready")
    s_ids = sem("ids_on_diagonals")
    s_kraw = sem("carry_matrices_raw")
    s_cnt = sem("counts_scanned")
    s_pay = sem("payload_ready")
    s_set = sem("setup_done")
    s_pe = sem("setup_product")
    s_part = sem("bias_parts_split")
    s_parts = sem("bias_parts_spread")
    s_tab = sem("node_table_written")
    s_gx = sem("src_rows_gathered")
    s_gt = sem("table_rows_gathered")
    s_gd = sem("dst_rows_gathered")
    s_xs = sem("dst_rows_stored")
    s_xl = [sem("dst_rows_loaded"), sem("dst_rows_loaded_ahead")]
    s_xu = sem("dst_rows_updated")
    s_ea = sem("edge_attr_loaded")
    s_var = sem("variances_ready")
    s_std = sem("roots_ready")
    s_h = sem("h_ready")
    s_hc = sem("h_copied")
    s_tr = sem("transposed")
    s_ht = sem("transposed_evacuated")
    s_m = sem("mid_ready")
    s_y = sem("mid_evacuated")
    s_o = sem("unit_ready")
    s_ou = sem("unit_used")
    s_am = sem("head_done")
    s_zu = sem("messages_used")
    s_dl = sem("dense_loaded")
    s_df = sem("dense_input_free")
    s_dr = sem("dense_result_ready")
    s_ds = sem("dense_result_stored")
    s_sum = sem("stage_sums_ready")
    s_st = sem("stage_done")
    s_fix = sem("carries_added")
    s_ct = sem("tails_ready")
    s_cp = sem("carries_ready")
    s_ex = sem("exp_input_ready")
    s_exd = sem("exp_done")
    s_g1 = sem("hop_rows_stored")
    s_out = sem("rows_scattered")

    PARTS = [(0, 120), (120, P)]

    def row(v):
        return v.rearrange("(a m) -> a m", a=1)

    def column(v):
        return v.rearrange("(p a) -> p a", a=1)

    loads = [
        (src_i[:, :], a["src"].rearrange("(p t) -> p t", p=P)),
        (dst_i[:, :], a["dst"].rearrange("(p t) -> p t", p=P)),
        (next_i[0:P - 1, :], a["dst"].rearrange("(p t) -> p t", p=P)[1:P, 0:1]),
        (gru[:, 0:3, :], a["L0_gnn_gru_w_ih"].rearrange("(g j) m -> j g m", g=3)),
        (gru[:, 3, :], row(a["L0_gnn_memory_weights"]).to_broadcast([64, D])),
        (gsm[:, 0:3], a["L0_gnn_gru_b_ih"].rearrange("(g j) -> j g", g=3)),
        (gsm[:, 3:6], a["L0_gnn_gru_b_hh"].rearrange("(g j) -> j g", g=3)),
        (W2[:, :], a["L1_gnn_W2"]),
        (b1c[:, 0:1], column(a["L1_gnn_b1"])),
        (bwr[:, 0, :], row(a["L0_gnn_gcn_bias"])),
        (bwr[:, 1, :], row(a["L1_gnn_b2"])),
        (bwr[:, 2, :], row(a["L3_gnn_b_w"])),
        (wwt[:, :, :], a["L3_gnn_W_w"].rearrange("(a i) o -> i a o", a=2)),
        (bgc[:, :], column(a["L3_gnn_b_g"])),
    ]
    for k, name in enumerate(("L3_gnn_a_src", "L3_gnn_a_dst")):
        loads.append((aB[:, k, :, :].rearrange("p h o -> p (h o)"),
                      a[name].rearrange("(a h) o -> a (h o)", a=1).to_broadcast([128, HEADS * D])))
    for k in range(2):
        h = slice(64 * k, 64 * k + 64)
        loads += [
            (Y[h, 0:64, :], a["L0_gnn_wt_w"].rearrange("(o i) m -> i o m", i=D)),
            (wtb[:, k, :], a["L0_gnn_wt_b"].rearrange("(o i) -> o i", i=D)),
            (W1[h, :], a["L1_gnn_W1"]),
            (b2c[h, :], column(a["L2_gnn_bias"])),
            (wa[h, :, :], a["L3_gnn_W_att"].rearrange("h i o -> i h o")),
            (wg[h, :], a["L3_gnn_W_g"]),
            (BW[h, W_SELF, h], a["L2_gnn_W_self"]),
            (BW[h, W_NEIGH, h], a["L2_gnn_W_neigh"]),
        ]
    NLOAD = 16 * len(loads)
    CHUNKS = NODES // DC
    FIRST_CHUNK = {"rows": 0, "lone": G, "table": G + LONE,
                   **{stage: (2 + i) * G + LONE for i, stage in enumerate(DENSE_STAGES)}}
    assert (2 + len(DENSE_STAGES)) * G + LONE == CHUNKS

    def chunks_before(stage):
        return 2 * G + LONE + G * sum(s <= stage for s in DENSE_STAGES)

    CARRY = {0: ["sum"], 1: ["sum"], 2: ["sum"], 3: ["sum"], 4: ["sum", "messages"]}
    SOFTMAX = ["hold", "max", "hold", "den", "hold"]

    def cols(t, g, lo=0, n=GC):
        return t[0:P, bass.ds(g * GC + lo, n)] if len(t.shape) == 2 else t[0:P, bass.ds(g * GC + lo, n), :]

    def pairs(t, c):
        return t[0:P, c:c + 2, :].rearrange("p a b -> p (a b)")

    def unit_rows(ps):
        return ps[0:P, :].rearrange("p (c d) -> p c d", d=D)

    with nc.Block() as block:

        @block.sync
        def _(sp):
            see = Seen()

            def await_(semaphore, count):
                sp.wait_ge(semaphore, count)
                sp.nop(nofuse=True)

            def dense_load(c):
                for lo, hi in PARTS:
                    sp.dma_start(din[lo:hi, :, :], x_v[lo:hi, bass.ts(c, DC), :]).then_inc(s_dl, 16)

            def dense_store(c):
                for lo, hi in PARTS:
                    sp.dma_start(out_v[lo:hi, bass.ts(c, DC), :], dout[lo:hi, :, :]).then_inc(s_ds, 16)

            def x_load(g, b):
                for lo, hi in PARTS:
                    sp.dma_start(xd[b][lo:hi, :, :], xt_v[lo:hi, bass.ts(g, GC), :]).then_inc(s_xl[b], 16)

            def x_store(g, b):
                for lo, hi in PARTS:
                    sp.dma_start(xt_v[lo:hi, bass.ts(g, GC), :], xd[b][lo:hi, :, :]).then_inc(s_xs, 16)
                await_(s_xs, see.add("xs", 32))

            sp.wait_ge(s_preset, 3)
            for dst, src in loads:
                sp.dma_start(dst, src, allow_slow_non_contiguous=True).then_inc(s_in, 16)
            for lo, hi in PARTS:
                sp.dma_start(node_tab.rearrange("(p n) c -> p (n c)", p=P)[lo:hi, :],
                             tmpA[lo:hi, 0:25, :].rearrange("p a b -> p (a b)")).then_inc(s_ds, 16)
            sp.wait_ge(s_part, 3)
            for k in range(3):
                sp.dma_start(parts_b[k:k + 1, :, :].rearrange("p a b -> p (a b)"), part[:, k, :]).then_inc(s_parts, 16)
            sp.wait_ge(s_set, 1)
            dense_load(0)

            def chunk(c, last=False):
                await_(s_df, see.add("df"))
                if not last:
                    dense_load(c + 1)
                await_(s_dr, see.add("dr"))
                dense_store(c)

            for phase, turns in (("rows", G), ("lone", LONE), ("table", G)):
                with sp.Fori(0, turns) as g:
                    see.enter(g, {"df": 1, "dr": 1})
                    chunk(g + FIRST_CHUNK[phase])
                    see.leave(turns)

            for stage in range(STAGES):
                if stage == 1:
                    sp.wait_ge(s_st, 1)
                    for g in range(G):
                        for lo, hi in PARTS:
                            sp.dma_start(Y[lo:hi, g * GC:(g + 1) * GC, :], ea_v[lo:hi, g * GC:(g + 1) * GC, :]).then_inc(s_ea, 16)
                if stage in DENSE_STAGES:
                    end = stage == DENSE_STAGES[-1]
                    with sp.Fori(0, G - end) as g:
                        see.enter(g, {"df": 1, "dr": 1})
                        chunk(g + FIRST_CHUNK[stage])
                        see.leave(G - end)
                    if end:
                        chunk(CHUNKS - 1, last=True)

                def dst_rows(g, b):
                    if stage > 0 and not (isinstance(g, int) and g == G - 1):
                        x_load(g + 1, 1 - b)
                    await_(s_xu, see.add("xu"))
                    if stage < 3:
                        x_store(g, b)
                    elif stage == 3:
                        for lo, hi in PARTS:
                            sp.dma_start(gt_v[lo:hi, bass.ts(g, GC), :], tmpB[lo:hi, :, :]).then_inc(s_g1, 16)
                    else:
                        await_(s_out, see.add("out", 16 * GC))

                if stage > 0:
                    await_(s_ds, 32 * (1 + chunks_before(stage)))
                    x_load(0, 0)
                see.by_pairs(sp, {"xu": 1, **({"xs": 32} if stage < 3 else {} if stage == 3 else {"out": 16 * GC})}, dst_rows)
            sp.wait_ge(s_ds, 32 * (CHUNKS + 1))

        @block.gpsimd
        def _(pool):
            see = Seen()
            nc.gpsimd.memset(BW[:, :, :], 0.0).then_inc(s_preset, 1)
            nc.gpsimd.memset(next_i[:, :], -1).then_inc(s_preset, 1)
            nc.gpsimd.memset(tmpA[:, :, :], 0.0).then_inc(s_preset, 1)
            nc.gpsimd.memset(ones[:, :], 1.0).then_inc(s_preset, 1)
            nc.gpsimd.memset(BV[:, :, :], 0.0).then_inc(s_preset, 1)
            nc.gpsimd.memset(ones_b[:, :], 1.0).then_inc(s_preset, 1)
            nc.gpsimd.iota(rep_i[:, :], pattern=[[1, T]], base=-NOREP, channel_multiplier=T).then_inc(s_preset, 1)
            nc.gpsimd.memset(epsc[:, :], EPS).then_inc(s_preset, 1)
            for k, semaphore in enumerate((s_o, s_ou, s_zu, s_am, s_hc, s_df, s_dr, s_xu, s_g1)):
                nc.gpsimd.memset(bcol[:, k:k + 1], 0.0).then_inc(semaphore, 1)
            nc.gpsimd.memset(ident[:, :], 0.0).then_inc(s_preset, 1)
            pool.wait_ge(s_preset, 9)
            nc.gpsimd.affine_select(out=ident[:, :], in_=ident[:, :], compare_op=ALU.not_equal, fill=1.0,
                                    base=0, pattern=[[-1, 128]], channel_multiplier=1).then_inc(s_preset, 1)
            def cut_carry_matrices():
                pool.wait_ge(s_kraw, 3)
                nc.gpsimd.affine_select(out=Kc[:, :], in_=Kc[:, :], compare_op=ALU.is_ge, fill=0.0,
                                        base=-1, pattern=[[1, P]], channel_multiplier=-1).then_inc(s_kcut, 1)
                for m in (Bm, KP):
                    nc.gpsimd.affine_select(out=m[:, :], in_=m[:, :], compare_op=ALU.is_ge, fill=0.0,
                                            base=-1, pattern=[[-1, P]], channel_multiplier=1).then_inc(s_kcut, 1)

            def gather(dst, table, rows, index, t, s):
                nc.gpsimd.indirect_dma_start(dst, None, table, bass.IndirectOffsetOnAxis(ap=index[:, t:t + 1], axis=0),
                                             bounds_check=rows - 1, oob_is_err=False).then_inc(s, 16)

            def scatter(table, rows, index, t, src, s):
                nc.gpsimd.indirect_dma_start(table, bass.IndirectOffsetOnAxis(ap=index[:, t:t + 1], axis=0), src, None,
                                             bounds_check=rows - 1, oob_is_err=False).then_inc(s, 16)

            def columns(g):
                return range(g * GC, (g + 1) * GC)

            pool.wait_ge(s_in, NLOAD)
            for g in range(G):
                for t in columns(g):
                    gather(Xs[:, t, :], a["x"], N, src_i, t, s_gx)
                if g == 1:
                    cut_carry_matrices()
                pool.wait_ge(s_gx, 16 * GC * (g + 1))
            pool.wait_ge(s_pay, 1)
            pool.wait_ge(s_ds, 32)
            for t in range(T):
                scatter(node_tab, N, sct_i, t, Tg[:, t, :], s_tab)
            pool.wait_ge(s_tab, 16 * T)
            for g in range(G):
                for t in columns(g):
                    gather(Tg[:, t, :], node_tab, N, src_i, t, s_gt)
                pool.wait_ge(s_gt, 16 * GC * (g + 1))
            for g in range(G):
                if g == 1:
                    pool.wait_ge(s_ds, 32 * (1 + chunks_before(0)))
                if g > 1:
                    pool.wait_ge(s_xs, 32 * (g - 1))
                for t in columns(g):
                    gather(xd[g % 2][:, t - g * GC, :], a["x"], N, dst_i, t, s_gd)
                pool.wait_ge(s_gd, 16 * GC * (g + 1))
            for stage in range(1, STAGES):
                pool.wait_ge(s_st, stage)
                if stage < 4:
                    pool.wait_ge(s_xs, 32 * G * stage)
                else:
                    pool.wait_ge(s_g1, 32 * G + 1)
                for g in range(G):
                    for t in columns(g):
                        if stage < 4:
                            gather(Xs[:, t, :], xt, E, rep_i, t, s_gx)
                        else:
                            gather(Y[0:P, t, :], gt, E, rep_i, t, s_gx)
                    pool.wait_ge(s_gx, 16 * GC * (stage * G + g + 1))
            pool.wait_ge(s_ds, 32 * (CHUNKS + 1))
            for g in range(G):
                pool.wait_ge(s_xu, 4 * G + g + 2)
                for t in columns(g):
                    scatter(out, N, sct_i, t, xd[g % 2][:, t - g * GC, :], s_out)
                pool.wait_ge(s_out, 16 * GC * (g + 1))

        @block.tensor
        def _(pe):
            see = Seen()

            def done(ins):
                ins.then_inc(s_pe, 1)

            pe.wait_ge(s_in, NLOAD)
            pe.wait_ge(s_preset, 10)
            done(nc.tensor.transpose(psO[0][:, 0:64], wtb.rearrange("p a b -> p (a b)"), ident[0:64, 0:64]))
            for h in range(HEADS):
                done(nc.tensor.transpose(psT[0][0:64, 128 * h:128 * h + 128], wa[:, h, :], ident[:, :]))
            done(nc.tensor.transpose(psT[1][0:64, 0:128], wg[:, :], ident[:, :]))
            pe.wait_ge(s_um, 2)
            done(nc.tensor.matmul(psS[:, 0:64], ones[0:64, :], diag[0:64, 0, 0:64], start=True, stop=True))
            done(nc.tensor.matmul(psO[1][0:1, 0:64], b1c[:, 1:2], W2[:, :], start=True, stop=True))
            done(nc.tensor.matmul(psO[1][0:1, 64:128], bgc[:, :], wwt[:, 1, :], start=True, stop=True))
            pe.wait_ge(s_act, 4)
            for h in range(HEADS):
                done(nc.tensor.matmul(psM[0][:, 64 * h:64 * h + 64], HT[0:64, 0, 128 * h:128 * h + 128],
                                      wwt[:, 0, :], start=True, stop=True))
            done(nc.tensor.matmul(psM[0][:, 256:320], HT[0:64, 1, 0:128], wwt[:, 1, :], start=True, stop=True))
            pe.wait_ge(s_ids, 2)
            done(nc.tensor.matmul(psS[0:P, 64:64 + P], ones[0:P, 0:P], diag[:, 1, :], start=True, stop=True))
            done(nc.tensor.matmul(psS[0:P, 192:192 + P], ones[0:P, 0:P], diag[:, 2, :], start=True, stop=True))
            pe.wait_ge(s_cnt, 1)
            pe.wait_ge(s_kcut, 3)
            done(nc.tensor.matmul(psS[0:P, 320:321], Kc[:, :], invdeg[:, T - 1:T], start=True, stop=True))
            done(nc.tensor.transpose(psS[0:1, 384:384 + P], c8[:, 0:1], ident[0:P, 0:P]))
            pe.wait_ge(s_c1, 1)
            done(nc.tensor.matmul(psO[1][0:P, 128:192], ones[0:1, 0:P], carry[0:1, :], start=True, stop=True))

            def transposes(src, col, bank):
                for q in range(UC // 2):
                    last = nc.tensor.transpose(psT[bank][:, q * P:(q + 1) * P], pairs(src, col + 2 * q), ident[0:P, 0:P])
                last.then_inc(s_tr, 1)

            def bias(k, r):
                nc.tensor.matmul(psO[k % 2][0:P, :], ones_b[:, :], parts_b[:, r:r + 1, :].to_broadcast([3, UC, D]),
                                 start=True, stop=False)

            def free_result(k):
                n = see.add("o") - 1
                pe.wait_ge(s_ou, n if k == 0 else n - 1)

            def lin(src, col, n, w, r):
                pe.wait_ge(s_h, see.add("h"))
                for k in range(n + 1):
                    if k < n:
                        transposes(src, col + UC * k, k % 2)
                    if k >= 1:
                        u = k - 1
                        free_result(u)
                        bias(u, r)
                        pe.wait_ge(s_ht, see.add("ht"))
                        for q in range(UC // 2):
                            last = nc.tensor.matmul(psO[u % 2][0:P, 128 * q:128 * q + 128], HT[:, u % 2, q * P:(q + 1) * P],
                                                    BW[:, w, :], start=False, stop=(q == UC // 2 - 1))
                        last.then_inc(s_o, 1)

            def score(src, n, v):
                pe.wait_ge(s_h, see.add("h"))
                for k in range(n + 1):
                    if k < n:
                        transposes(src, UC * k, k % 2)
                    if k >= 1:
                        u = k - 1
                        free_result(u)
                        pe.wait_ge(s_ht, see.add("ht"))
                        for q in range(UC // 2):
                            last = nc.tensor.matmul(psO[u % 2][0:P, 8 * q:8 * q + 8], HT[:, u % 2, q * P:(q + 1) * P],
                                                    BV[:, v, :], start=True, stop=True)
                        last.then_inc(s_o, 1)

            def back(u, r):
                free_result(u)
                pe.wait_ge(s_y, see.add("y"))
                for q in range(UC // 2):
                    last = nc.tensor.matmul(psO[u % 2][0:P, 128 * q:128 * q + 128], YT[:, u % 2, q * P:(q + 1) * P],
                                            ident[:, :], is_transpose=True, start=(q == 0), stop=(r is None and q == UC // 2 - 1))
                if r is not None:
                    last = nc.tensor.matmul(psO[u % 2][0:P, :], ones_b[:, :], parts_b[:, r:r + 1, :].to_broadcast([3, UC, D]),
                                            start=False, stop=True)
                last.then_inc(s_o, 1)

            def relu_units(src, col, n, r):
                pe.wait_ge(s_h, see.add("h"))
                for k in range(n + 2):
                    if k < n:
                        transposes(src, col + UC * k, k % 2)
                    if 1 <= k <= n:
                        u = k - 1
                        pe.wait_ge(s_ht, see.add("ht"))
                        nc.tensor.matmul(psM[u % 2][:, 0:4 * P], BW[:, W_SELF, :], HT[:, u % 2, 0:4 * P],
                                         start=True, stop=True).then_inc(s_m, 1)
                    if k >= 2:
                        back(k - 2, r)

            def neigh_units(n):
                pe.wait_ge(s_h, see.add("h"))
                for u in range(n):
                    transposes(tmpA, UC * u, 0)
                    transposes(tmpB, UC * u, 1)
                    if u >= 1:
                        back(u - 1, None)
                    pe.wait_ge(s_ht, see.add("ht", 2))
                    nc.tensor.matmul(psM[u % 2][:, 0:4 * P], BW[:, W_SELF, :], HT[:, 0, 0:4 * P], start=True, stop=False)
                    nc.tensor.matmul(psM[u % 2][:, 0:4 * P], BW[:, W_NEIGH, :], HT[:, 1, 0:4 * P],
                                     start=False, stop=True).then_inc(s_m, 1)
                back(n - 1, None)

            def mlp_units(n):
                pe.wait_ge(s_hc, see.add("hc"))
                transposes(tmpA, 0, 0)
                for u in range(n):
                    if u + 1 < n:
                        transposes(tmpA, UC * (u + 1), (u + 1) % 2)
                    pe.wait_ge(s_ht, see.add("ht"))
                    for z in range(2):
                        half = slice(64 * z, 64 * z + 64)
                        last = nc.tensor.matmul(psM[z][:, 0:4 * P], W1[half, :], HT[half, u % 2, 0:4 * P], start=True, stop=True)
                    last.then_inc(s_m, 1)
                    free_result(u)
                    bias(u, BROW_L1)
                    pe.wait_ge(s_y, see.add("y"))
                    for q in range(UC // 2):
                        for z in range(2):
                            last = nc.tensor.matmul(psO[u % 2][0:P, 128 * q + 64 * z:128 * q + 64 * z + 64],
                                                    YT[:, z, q * P:(q + 1) * P], W2[:, :], start=False,
                                                    stop=(q == UC // 2 - 1 and z == 1))
                    last.then_inc(s_o, 1)

            def messages(n):
                for u in range(n):
                    src = tmpA if u % 2 == 0 else tmpB
                    pe.wait_ge(s_h, see.add("h"))
                    for k in range(HEADS + 1):
                        if k < HEADS:
                            transposes(src, UC * k, k % 2)
                        if k >= 1:
                            h = k - 1
                            if h == 0:
                                pe.wait_ge(s_zu, see.add("zu") - 1)
                            pe.wait_ge(s_ht, see.add("ht"))
                            for q in range(UC // 2):
                                last = nc.tensor.matmul(psZ[0:P, 128 * q:128 * q + 128], HT[:, h % 2, q * P:(q + 1) * P],
                                                        BW[:, W_ATT + h, :], start=(h == 0 and q == 0),
                                                       stop=(h == HEADS - 1 and q == UC // 2 - 1))
                            last.then_inc(s_am, 1)

            def carries(kinds, stage):
                for kind in kinds:
                    pe.wait_ge(s_ct, see.add("ct"))
                    if kind == "sum":
                        last = nc.tensor.matmul(psS[0:P, 0:D], Kc[:, :], Y[0:P, T - 1, :], start=True, stop=True)
                    elif kind == "messages":
                        last = nc.tensor.matmul(psS[0:P, 0:D], Kc[:, :], Xs[:, T - 1, :], start=True, stop=True)
                    elif kind == "den":
                        last = nc.tensor.matmul(psS[0:P, 0:HEADS], Kc[:, :], Sd[:, T - 1, :], start=True, stop=True)
                    elif kind == "hold":
                        last = nc.tensor.matmul(psS[0:P, 0:HEADS], Bm[:, :], Sd[:, 0, :], start=True, stop=True)
                    else:
                        last = nc.tensor.matmul(psS[0:P, 0:HEADS * P], ones[0:P, 0:P], diag[:, :, :], start=True, stop=True)
                    last.then_inc(s_cp, 1)

            def dense():
                for half in range(2):
                    lin(dh, HC * half, HU, W_L0, BROW_DENSE)
                for half in range(2):
                    relu_units(dh, HC * half, HU, BROW_END)

            pe.wait_ge(s_parts, 48)
            CHUNK = {"h": 4, "ht": 2 * DU, "o": 2 * DU, "y": DU}

            def turn(chunk, **edge):
                return {k: edge.get(k, 0) + chunk.get(k, 0) for k in {**edge, **chunk}}

            with pe.Fori(0, G) as g:
                see.enter(g, turn(CHUNK, h=1, ht=GU, o=GU))
                lin(tmpA, 0, GU, W_L0, BROW_L0)
                dense()
                see.leave(G)
            for turns in (LONE, G):
                with pe.Fori(0, turns) as g:
                    see.enter(g, CHUNK)
                    dense()
                    see.leave(turns)

            for stage in range(STAGES):
                if stage > 0:
                    per = {1: {}, 2: {"h": 1, "ht": GU, "o": GU, "y": GU}, 3: {"h": 1, "ht": GU, "o": GU},
                           4: {"h": GU, "ht": HEADS * GU, "zu": GU}}[stage]
                    with pe.Fori(0, G) as g:
                        see.enter(g, turn(CHUNK if stage in DENSE_STAGES else {}, **per))
                        if stage == 2:
                            relu_units(tmpA, 0, GU, None)
                        elif stage == 3:
                            score(tmpA, GU, 0)
                        elif stage == 4:
                            messages(GU)
                        if stage in DENSE_STAGES:
                            dense()
                        see.leave(G)
                carries(CARRY[stage], stage)
                per = {0: {"h": 1, "ht": GU, "o": GU}, 1: {"hc": 1, "ht": GU, "y": GU, "o": GU},
                       2: {"h": 1, "ht": 2 * GU, "y": GU, "o": GU}, 3: {"h": 1, "ht": GU, "o": GU},
                       4: {"h": 1, "ht": GU, "o": GU}}[stage]
                if stage == 1:
                    see.add("hc", G)
                with pe.Fori(0, G) as g:
                    see.enter(g, per)
                    if stage == 0:
                        lin(tmpA, 0, GU, W_L0, BROW_L0)
                    elif stage == 1:
                        mlp_units(GU)
                    elif stage == 2:
                        neigh_units(GU)
                    elif stage == 3:
                        score(tmpA, GU, 1)
                    else:
                        lin(tmpA, 0, GU, W_HOP, BROW_END)
                    see.leave(G)
                if stage == 3:
                    carries(SOFTMAX, stage)

        @block.scalar
        def _(act):
            see = Seen()
            act.wait_ge(s_preset, 10)
            act.wait_ge(s_gate, 1)
            nc.scalar.activation(gsm[:, 9:11], gsm[:, 9:11], ACT.Sigmoid).then_inc(s_act, 1)
            act.wait_ge(s_gate, 2)
            nc.scalar.activation(gsm[:, 11:12], gsm[:, 11:12], ACT.Tanh).then_inc(s_act, 1)
            act.wait_ge(s_pe, 6)
            nc.scalar.activation(HT[0:64, 0, :], psT[0][0:64, :], ACT.Copy).then_inc(s_act, 1)
            nc.scalar.activation(HT[0:64, 1, 0:128], psT[1][0:64, 0:128], ACT.Copy).then_inc(s_act, 1)
            act.wait_ge(s_gate, 3)
            nc.scalar.activation(dinvd[:, :], dinvd[:, :], ACT.Sqrt).then_inc(s_act, 1)
            act.wait_ge(s_pe, 14)

            def evac(bank):
                act.wait_ge(s_tr, see.add("tr"))
                nc.scalar.activation(HT[:, bank, 0:4 * P], psT[bank][:, 0:4 * P], ACT.Copy).then_inc(s_ht, 1)

            def free_transposed(k):
                n = see.add("o") - 1
                act.wait_ge(s_o, n if k == 0 else n - 1)

            def lin(n):
                for k in range(n):
                    free_transposed(k)
                    evac(k % 2)

            def relu(u):
                act.wait_ge(s_m, see.add("m"))
                nc.scalar.activation(YT[:, u % 2, 0:4 * P], psM[u % 2][:, 0:4 * P], ACT.Relu, bias=b2c[:, 0:1]).then_inc(s_y, 1)

            def relu_units(n):
                for k in range(n + 1):
                    if k < n:
                        free_transposed(k)
                        evac(k % 2)
                    if k >= 1:
                        relu(k - 1)

            def neigh_units(n):
                for u in range(n):
                    free_transposed(u)
                    if u > 0:
                        act.wait_ge(s_m, see.value("m"))
                    evac(0)
                    evac(1)
                    relu(u)

            def mlp_units(n):
                for k in range(n + 1):
                    if k < n:
                        free_transposed(k)
                        evac(k % 2)
                    if k >= 1:
                        act.wait_ge(s_m, see.add("m"))
                        o = see.value("o") - (2 if k < n else 1)
                        act.wait_ge(s_o, o)
                        for z in range(2):
                            last = nc.scalar.activation(YT[:, z, 0:4 * P], psM[z][:, 0:4 * P], ACT.Relu, bias=b1c[:, 0:1])
                        last.then_inc(s_y, 1)

            def messages(n):
                for u in range(n):
                    for h in range(HEADS):
                        m = see.add("am") - 1
                        if u == 0 and h == 0:
                            act.wait_ge(s_o, see.value("o"))
                        act.wait_ge(s_am, m if h == 0 else m - 1)
                        evac(h % 2)

            def roots(n):
                act.wait_ge(s_var, see.add("var"))
                nc.scalar.activation(sm[:, 5, 0:n], sm[:, 2, 0:n], ACT.Sqrt, bias=epsc[:, 0:1], scale=1.0 / D).then_inc(s_std, 1)

            def copy_h(dst, src):
                nc.scalar.activation(dst, src, ACT.Copy).then_inc(s_hc, 1)

            def dense(first=True):
                if first:
                    roots(HC)
                    roots(HC)
                see.add("h", 4)
                lin(HU)
                lin(HU)
                roots(HC)
                roots(HC)
                relu_units(HU)
                relu_units(HU)

            CHUNK = {"h": 4, "tr": 2 * DU, "o": 2 * DU, "m": DU, "var": 4}

            def turn(chunk, **edge):
                return {k: edge.get(k, 0) + chunk.get(k, 0) for k in {**edge, **chunk}}

            with act.Fori(0, G) as g:
                see.enter(g, turn(CHUNK, h=1, tr=GU, o=GU, var=1))
                roots(GC)
                act.wait_ge(s_h, see.add("h"))
                copy_h(cols(Y, g), tmpA[:, :, :])
                roots(HC)
                roots(HC)
                lin(GU)
                dense(False)
                see.leave(G)
            with act.Fori(0, LONE) as g:
                see.enter(g, CHUNK)
                dense()
                see.leave(LONE)
            with act.Fori(0, G) as g:
                see.enter(g, turn(CHUNK, gt=16 * GC))
                act.wait_ge(s_gt, see.add("gt", 16 * GC))
                nc.scalar.activation(cols(dinvs, g), Tg[:, bass.ts(g, GC), 1], ACT.Sqrt, bias=ones[0:P, 0:1]).then_inc(s_std, 1)
                dense()
                see.leave(G)

            for stage in range(STAGES):
                if stage > 0:
                    per = {1: {"var": 1}, 2: {"var": 1, "h": 1, "tr": GU, "o": GU, "m": GU},
                           3: {"var": 1, "h": 1, "tr": GU, "o": GU}, 4: {"h": GU, "tr": HEADS * GU, "am": HEADS * GU}}[stage]
                    with act.Fori(0, G) as g:
                        see.enter(g, turn(CHUNK if stage in DENSE_STAGES else {}, **per))
                        if stage < 4:
                            roots(GC)
                        if stage in (2, 3):
                            act.wait_ge(s_h, see.add("h"))
                            copy_h(cols(Xs if stage == 3 else Y, g), tmpA[:, :, :])
                        if stage in DENSE_STAGES:
                            roots(HC)
                            roots(HC)
                        if stage == 2:
                            relu_units(GU)
                        elif stage == 3:
                            lin(GU)
                        elif stage == 4:
                            see.add("h", GU)
                            messages(GU)
                        if stage in DENSE_STAGES:
                            dense(False)
                        see.leave(G)
                per = {0: {"h": 1, "tr": GU, "o": GU, "var": 1}, 1: {"tr": GU, "m": GU, "o": GU},
                       2: {"h": 1, "tr": 2 * GU, "m": GU, "o": GU, "var": 1}, 3: {"h": 1, "tr": GU, "o": GU, "var": 1},
                       4: {"h": 1, "tr": GU, "o": GU}}[stage]
                if stage == 1:
                    act.wait_ge(s_sum, 2)
                with act.Fori(0, G) as g:
                    see.enter(g, per)
                    if stage in (0, 2, 3):
                        roots(GC)
                    if stage == 1:
                        act.wait_ge(s_tr, see.value("tr"))
                        copy_h(tmpA[:, :, :], cols(Y, g))
                        mlp_units(GU)
                    else:
                        see.add("h")
                        if stage == 2:
                            neigh_units(GU)
                        else:
                            lin(GU)
                    see.leave(G)
                if stage == 3:
                    act.wait_ge(s_ex, 1)
                    nc.scalar.activation(S[:, :, :], S[:, :, :], ACT.Exp).then_inc(s_exd, 1)

        @block.vector
        def _(dve):
            see = Seen()
            v = nc.vector

            def chain(ins):
                ins.then_inc(s_dve, 1)
                see.add("dve")

            def settle():
                dve.wait_ge(s_dve, see.value("dve"))

            def step(ins):
                chain(ins)
                settle()

            marks = {"gate": (0, s_gate), "set": (1, s_set), "df": (2, s_df), "dr": (3, s_dr), "ct": (4, s_ct),
                     "sum": (5, s_sum), "xu": (6, s_xu), "st": (7, s_st), "fix": (8, s_fix)}
            see.add("gate", 2)

            def mark(name):
                k, semaphore = marks[name]
                n = see.add(name)
                if not isinstance(n, int) or n > 1:
                    dve.wait_ge(semaphore, n - 1)
                v.memset(mcol[:, k:k + 1], 0.0).then_inc(semaphore, 1)

            dve.wait_ge(s_in, NLOAD)
            dve.wait_ge(s_preset, 10)
            step(v.tensor_tensor(gru[:, 0:3, :], gru[:, 0:3, :], gru[:, 3:4, :].to_broadcast([64, 3, D]), ALU.mult))
            step(v.tensor_reduce(gsm[:, 6:9], gru[:, 0:3, :], AX.X, ALU.add))
            step(v.tensor_tensor(gsm[:, 6:9], gsm[:, 6:9], gsm[:, 0:3], ALU.add))
            v.tensor_tensor(gsm[:, 9:11], gsm[:, 6:8], gsm[:, 3:5], ALU.add).then_inc(s_gate, 1)
            dve.wait_ge(s_act, 1)
            step(v.tensor_tensor(gsm[:, 11:12], gsm[:, 9:10], gsm[:, 5:6], ALU.mult))
            v.tensor_tensor(gsm[:, 11:12], gsm[:, 11:12], gsm[:, 8:9], ALU.add).then_inc(s_gate, 1)
            v.tensor_scalar(b1c[:, 1:2], b1c[:, 0:1], 0.0, None, ALU.max).then_inc(s_um, 1)
            dve.wait_ge(s_act, 2)
            step(v.tensor_scalar(gsm[:, 10:11], gsm[:, 10:11], -1.0, 1.0, ALU.mult, ALU.add))
            step(v.tensor_tensor(gsm[:, 11:12], gsm[:, 11:12], gsm[:, 10:11], ALU.mult))
            v.tensor_scalar(diag[0:64, 0, 0:64], ident[0:64, 0:64], gsm[:, 11:12], None, ALU.mult).then_inc(s_um, 1)
            chain(v.tensor_copy(dstf[:, :], dst_i[:, :]))
            chain(v.tensor_copy(nextf[:, :], next_i[:, :]))
            chain(v.memset(same[:, 0:1], 0.0))
            chain(v.memset(W8[:, :], 1.0))
            settle()
            v.tensor_scalar(diag[:, 1, :], ident[0:P, 0:P], dstf[:, 0:1], None, ALU.mult).then_inc(s_ids, 1)
            v.tensor_scalar(diag[:, 2, :], ident[0:P, 0:P], dstf[:, T - 1:T], None, ALU.mult).then_inc(s_ids, 1)
            chain(v.tensor_tensor(same[:, 1:T], dstf[:, 1:T], dstf[:, 0:T - 1], ALU.is_equal))
            chain(v.tensor_tensor(notlast[:, 0:T - 1], dstf[:, 1:T], dstf[:, 0:T - 1], ALU.is_equal))
            chain(v.tensor_tensor(notlast[:, T - 1:T], dstf[:, T - 1:T], nextf[:, :], ALU.is_equal))
            chain(v.tensor_scalar(infirst[:, :], dstf[:, :], dstf[:, 0:1], None, ALU.is_equal))
            chain(v.tensor_tensor(c8[:, 1:2], dstf[:, 0:1], nextf[:, :], ALU.not_equal))
            settle()
            chain(v.tensor_scalar(inopen[:, :], dstf[:, :], dstf[:, T - 1:T], notlast[:, T - 1:T], ALU.is_equal, ALU.mult))
            chain(v.tensor_reduce(c8[:, 0:1], infirst[:, :], AX.X, ALU.add))
            v.tensor_tensor_scan(invdeg[:, :], same[:, :], W8[:, :], 0.0, ALU.mult, ALU.add).then_inc(s_cnt, 1)
            dve.wait_ge(s_pe, 16)
            v.tensor_scalar(Kc[:, :], psS[0:P, 64:64 + P], dstf[:, T - 1:T], None, ALU.is_equal).then_inc(s_kraw, 1)
            v.tensor_scalar(KP[:, :], psS[0:P, 192:192 + P], dstf[:, 0:1], None, ALU.is_equal).then_inc(s_kraw, 1)
            v.tensor_scalar(Bm[:, :], psS[0:P, 192:192 + P], dstf[:, 0:1], c8[:, 1:2], ALU.is_equal, ALU.mult).then_inc(s_kraw, 1)
            dve.wait_ge(s_pe, 18)
            chain(v.tensor_copy(c8[:, 2:3], psS[0:P, 320:321]))
            chain(v.tensor_reduce(lmax[:, 0:1], psS[0:1, 384:384 + P], AX.X, ALU.max))
            dve.wait_ge(s_cnt, 1)
            settle()
            chain(v.scalar_tensor_tensor(invdeg[:, :], infirst[:, :], c8[:, 2:3], invdeg[:, :], ALU.mult, ALU.add))
            chain(v.tensor_copy(lmax_i[:, :], lmax[:, 0:1]))
            chain(v.tensor_copy(Tg[:, :, 0], rep_i[:, :]))
            settle()
            chain(v.tensor_copy(Tg[:, :, 1], invdeg[:, :]))
            chain(v.tensor_scalar(dinvd[:, :], invdeg[:, :], 1.0, None, ALU.add))
            settle()
            v.scalar_tensor_tensor(sct_i[:, :], notlast[:, :], float(2 * N), dstf[:, :], ALU.mult, ALU.add).then_inc(s_pay, 1)
            mark("gate")
            step(v.tensor_scalar(invdeg[:, :], invdeg[:, :], 1.0, None, ALU.max))
            dve.wait_ge(s_act, 5)
            chain(v.reciprocal(dinvd[:, :], dinvd[:, :]))
            chain(v.reciprocal(invdeg[:, :], invdeg[:, :]))
            dve.wait_ge(s_kcut, 3)
            chain(v.tensor_scalar(KP[:, :], KP[:, :], -1.0, BIG, ALU.add, ALU.mult))
            first_len = dve.value_load(lmax_i[0:1, 0:1], min_val=1, max_val=T)
            dve.wait_ge(s_pe, 14)
            chain(v.tensor_tensor(Y[:, 0:64, :], Y[:, 0:64, :], psS[:, 0:64].unsqueeze(1).to_broadcast([128, 64, D]), ALU.mult))
            for k in range(2):
                chain(v.tensor_tensor(Y[:, 64 + 4 * k:68 + 4 * k, :], wa[:, :, :], aB[:, k, :, :], ALU.mult))
            settle()
            chain(v.tensor_reduce(YT[:, 0, 0:64], Y[:, 0:64, :], AX.X, ALU.add))
            chain(v.tensor_reduce(YT[:, 1, 0:8], Y[:, 64:72, :], AX.X, ALU.add))
            chain(v.tensor_copy(brow[:, BROW_L0, :], bwr[:, 0, :]))
            chain(v.tensor_copy(brow[:, BROW_L1, :], bwr[:, 1, :]))
            chain(v.tensor_tensor(brow[:, BROW_END, :], psO[1][0:1, 64:128], bwr[:, 2, :], ALU.add))
            v.tensor_tensor(carry[0:1, :], psO[1][0:1, 0:64], bwr[:, 1, :], ALU.add).then_inc(s_c1, 1)
            dve.wait_ge(s_c1, 1)
            chain(v.tensor_tensor(brow[:, BROW_DENSE, :], carry[0:1, :], bwr[:, 0, :], ALU.add))
            settle()
            all_rows = brow[:, :, :].rearrange("p a b -> p (a b)")
            v.tensor_copy(part[:, 0, :], all_rows).then_inc(s_part, 1)
            dve.wait_ge(s_part, 1)
            step(v.tensor_tensor(rest[:, :], all_rows, part[:, 0, :], ALU.subtract))
            v.tensor_copy(part[:, 1, :], rest[:, :]).then_inc(s_part, 1)
            dve.wait_ge(s_part, 2)
            step(v.tensor_tensor(rest[:, :], rest[:, :], part[:, 1, :], ALU.subtract))
            v.tensor_copy(part[:, 2, :], rest[:, :]).then_inc(s_part, 1)
            for k in range(2):
                h = slice(64 * k, 64 * k + 64)
                chain(v.tensor_tensor(BW[h, W_L0, h], YT[h, 0, 0:64], psO[0][h, 0:64], ALU.add))
                chain(v.tensor_copy(BW[h, W_HOP, h], psM[0][h, 256:320]))
                for j in range(HEADS):
                    chain(v.tensor_scalar(BW[h, W_ATT + j, h], psM[0][h, 64 * j:64 * j + 64], 1.0 / HEADS, None, ALU.mult))
                for j in range(2):
                    chain(v.tensor_copy(BV[h, j, 4 * k:4 * k + 4], YT[h, 1, 4 * j:4 * j + 4]))
            dve.wait_ge(s_pe, 19)
            chain(v.tensor_copy(c1b[:, :], psO[1][0:P, 128:192]))
            settle()
            mark("set")

            def wide(col, n):
                return col.unsqueeze(2).to_broadcast([P, n, D])

            def norm_relu(x, dst, n, scale=None, signal=None):
                for j in range(n):
                    last = v.bn_stats(st[:, j, :], x(j))
                step(last)
                k = sm[:, :, 0:n]
                chain(v.tensor_tensor(k[:, 0, :], st[:, 0:n, 1], st[:, 0:n, 4], ALU.add))
                chain(v.tensor_tensor(k[:, 1, :], st[:, 0:n, 1], st[:, 0:n, 4], ALU.subtract))
                chain(v.tensor_tensor(k[:, 2, :], st[:, 0:n, 2], st[:, 0:n, 5], ALU.add))
                settle()
                chain(v.tensor_scalar(k[:, 4, :], k[:, 0, :], 0.5, None, ALU.mult))
                chain(v.scalar_tensor_tensor(k[:, 3, :], k[:, 1, :], D / 4.0, k[:, 1, :], ALU.mult, ALU.mult))
                settle()
                v.tensor_tensor(k[:, 2, :], k[:, 2, :], k[:, 3, :], ALU.add).then_inc(s_var, 1)
                chain(v.tensor_tensor(dst, x(None), wide(k[:, 4, :], n), ALU.subtract))
                dve.wait_ge(s_std, see.add("std"))
                step(v.reciprocal(k[:, 5, :], k[:, 5, :]))
                if scale is not None:
                    step(v.tensor_tensor(k[:, 5, :], k[:, 5, :], scale, ALU.mult))
                ins = v.scalar_tensor_tensor(dst, dst, 0.0, wide(k[:, 5, :], n), ALU.max, ALU.mult)
                if signal is None:
                    step(ins)
                else:
                    ins.then_inc(signal, 1)

            def group_cols(t, g):
                return lambda j: cols(t, g) if j is None else t[0:P, g * GC + j, :]

            def buffer_cols(t):
                return lambda j: t[:, :, :] if j is None else t[:, j, :]

            def add_units(at, n, base=None, free=None):
                for k in range(n):
                    dve.wait_ge(s_o, see.add("o"))
                    v.tensor_tensor(at(k), (base or at)(k), unit_rows(psO[k % 2]), ALU.add).then_inc(s_ou, 1)
                dve.wait_ge(s_ou, see.value("o"))

            def half(t, z):
                return lambda j: t[:, HC * z:HC * z + HC, :] if j is None else t[:, HC * z + j, :]

            def half_units(t, z):
                return lambda k: t[:, HC * z + UC * k:HC * z + UC * k + UC, :]

            def dense_first():
                dve.wait_ge(s_dl, see.add("dl", 32))
                for z in range(2):
                    norm_relu(half(din, z), half(dh, z)(None), HC, signal=s_h)

            def dense_rest():
                dve.wait_ge(s_ds, see.add("ds", 32))
                for z in range(2):
                    add_units(half_units(dout, z), HU, base=half_units(din, z))
                    if z == 1:
                        mark("df")
                    norm_relu(half(dout, z), half(dh, z)(None), HC, signal=s_h)
                for z in range(2):
                    add_units(half_units(dout, z), HU)
                mark("dr")

            def scan_sums(dst, src):
                with dve.Fori(0, D // 4) as f:
                    for k in range(4):
                        v.tensor_tensor_scan(dst[0:P, :, f * 4 + k], same[:, :], src[0:P, :, f * 4 + k], 0.0, ALU.mult, ALU.add)

            def carry_sums(dst):
                mark("ct")
                dve.wait_ge(s_ct, see.value("ct"))
                dve.wait_ge(s_cp, see.add("cp"))
                step(v.tensor_copy(carry[:, :], psS[0:P, 0:D]))
                with dve.Fori(0, first_len) as t:
                    v.scalar_tensor_tensor(dst[0:P, t, :], carry[:, :], infirst[:, bass.ts(t, 1)], dst[0:P, t, :], ALU.mult, ALU.add)
                mark("fix")
                dve.wait_ge(s_fix, see.value("fix"))

            def carry_heads(mask):
                dve.wait_ge(s_cp, see.add("cp"))
                step(v.tensor_copy(carry[:, 0:HEADS], psS[0:P, 0:HEADS]))
                for h in range(HEADS):
                    chain(v.scalar_tensor_tensor(Sd[:, :, h], mask[:, :], carry[:, h:h + 1], Sd[:, :, h], ALU.mult, ALU.add))
                settle()

            def tails_out():
                mark("ct")

            def hold():
                step(v.tensor_scalar(W8[:, :], notlast[:, :], -1.0, 1.0, ALU.mult, ALU.add))
                step(v.tensor_tensor(Sd[:, :, :], Sd[:, :, :], W8[:, :].unsqueeze(2).to_broadcast([P, T, HEADS]), ALU.mult))
                for h in range(HEADS):
                    chain(v.tensor_tensor_scan(Sd[:, ::-1, h], notlast[:, ::-1], Sd[:, ::-1, h], 0.0, ALU.mult, ALU.add))
                settle()
                tails_out()
                carry_heads(inopen)

            def softmax():
                hold()
                step(v.tensor_tensor(S[:, :, :], S[:, :, :], Sd[:, :, :], ALU.add))
                step(v.scalar_tensor_tensor(S[:, :, :], S[:, :, :], SLOPE, S[:, :, :], ALU.mult, ALU.max))
                step(v.tensor_scalar(W8[:, :], same[:, :], -1.0, BIG, ALU.add, ALU.mult))
                for h in range(HEADS):
                    chain(v.tensor_tensor_scan(Sd[:, :, h], W8[:, :], S[:, :, h], -BIG, ALU.add, ALU.max))
                settle()
                for h in range(HEADS):
                    chain(v.tensor_scalar(diag[:, h, :], ident[0:P, 0:P], Sd[:, T - 1, h:h + 1], None, ALU.mult))
                settle()
                tails_out()
                dve.wait_ge(s_cp, see.add("cp"))
                tails = psS[0:P, 0:HEADS * P].rearrange("p (h q) -> p h q", h=HEADS)
                step(v.tensor_tensor(diag[:, :, :], tails, KP[:, :].unsqueeze(1).to_broadcast([P, HEADS, P]), ALU.add))
                chain(v.tensor_reduce(carry[:, 0:HEADS], diag[:, :, :], AX.X, ALU.max))
                chain(v.tensor_scalar(W8[:, :], infirst[:, :], -1.0, BIG, ALU.add, ALU.mult))
                settle()
                for h in range(HEADS):
                    chain(v.scalar_tensor_tensor(Sd[:, :, h], W8[:, :], carry[:, h:h + 1], Sd[:, :, h], ALU.add, ALU.max))
                settle()
                hold()
                v.tensor_tensor(S[:, :, :], S[:, :, :], Sd[:, :, :], ALU.subtract).then_inc(s_ex, 1)
                dve.wait_ge(s_exd, 1)
                for h in range(HEADS):
                    chain(v.tensor_tensor_scan(Sd[:, :, h], same[:, :], S[:, :, h], 0.0, ALU.mult, ALU.add))
                settle()
                tails_out()
                carry_heads(infirst)
                hold()
                step(v.tensor_scalar(Sd[:, :, :], Sd[:, :, :], 1e-16, None, ALU.max))
                step(v.reciprocal(Sd[:, :, :], Sd[:, :, :]))
                step(v.tensor_tensor(S[:, :, :], S[:, :, :], Sd[:, :, :], ALU.mult))

            def weighted(g, u):
                dst = (tmpA if u % 2 == 0 else tmpB)[:, 0:HEADS * UC, :].rearrange("p (h c) d -> p h c d", h=HEADS)
                for h in range(HEADS):
                    last = v.tensor_tensor(dst[:, h, :, :], cols(Xs, g, UC * u, UC),
                                           S[:, bass.ds(g * GC + UC * u, UC), h:h + 1].to_broadcast([P, UC, D]), ALU.mult)
                last.then_inc(s_h, 1)

            def take_messages(g, u):
                dve.wait_ge(s_am, see.add("am", HEADS))
                v.tensor_scalar(cols(Xs, g, UC * u, UC), unit_rows(psZ), 1.0, None, ALU.mult).then_inc(s_zu, 1)

            def src_norm(stage, g):
                dve.wait_ge(s_gx, see.add("gx", 16 * GC))
                rows = group_cols(Xs, g)
                if stage == 1:
                    norm_relu(rows, tmpA[:, :, :], GC)
                    chain(v.tensor_tensor(cols(Xs, g), cols(Xs, g), c1b[:, :].unsqueeze(1).to_broadcast([P, GC, D]), ALU.add))
                    step(v.tensor_tensor(cols(Y, g), cols(Y, g), tmpA[:, :, :], ALU.add))
                else:
                    dve.wait_ge(s_hc, see.add("hc") - 1)
                    norm_relu(rows, tmpA[:, :, :], GC, signal=s_h)

            def src_units(g):
                add_units(lambda k: cols(Xs, g, UC * k, UC), GU)

            def table_rows(g):
                dve.wait_ge(s_gt, see.add("gt", 16 * GC))
                chain(v.tensor_scalar(cols(rep_i, g), Tg[:, bass.ts(g, GC), 0], float(NOREP), None, ALU.add))
                dve.wait_ge(s_std, see.add("std"))
                step(v.reciprocal(cols(dinvs, g), cols(dinvs, g)))
                chain(v.tensor_tensor(cols(Y, g), cols(Y, g), wide(cols(dinvs, g), GC), ALU.mult))

            def all_messages(g):
                for u in range(GU + 1):
                    if u < GU:
                        weighted(g, u)
                    if u >= 1:
                        take_messages(g, u - 1)

            def take_scores(dst, g):
                for k in range(GU):
                    dve.wait_ge(s_o, see.add("o"))
                    v.tensor_scalar(cols(dst, g, UC * k, UC), psO[k % 2][0:P, 0:UC * HEADS].rearrange("p (c h) -> p c h", h=HEADS),
                                    1.0, None, ALU.mult).then_inc(s_ou, 1)
                dve.wait_ge(s_ou, see.value("o"))

            def dst_work(stage, g, b):
                rows = xd[b]
                at = lambda k: rows[:, UC * k:UC * k + UC, :]
                if stage == 0:
                    dve.wait_ge(s_gd, see.add("gd", 16 * GC))
                else:
                    dve.wait_ge(s_xl[b], see.add(f"xl{b}", 32))
                if stage == 0:
                    norm_relu(buffer_cols(rows), tmpA[:, :, :], GC, scale=cols(dinvd, g))
                    step(v.tensor_tensor(tmpA[:, :, :], tmpA[:, :, :], cols(Y, g), ALU.add))
                    v.tensor_tensor(tmpA[:, :, :], tmpA[:, :, :], wide(cols(dinvd, g), GC), ALU.mult).then_inc(s_h, 1)
                    add_units(at, GU)
                elif stage == 1:
                    add_units(at, GU)
                elif stage == 2:
                    chain(v.tensor_tensor(tmpB[:, :, :], cols(Y, g), wide(cols(invdeg, g), GC), ALU.mult))
                    norm_relu(buffer_cols(rows), tmpA[:, :, :], GC, signal=s_h)
                    add_units(at, GU)
                elif stage == 3:
                    norm_relu(buffer_cols(rows), tmpA[:, :, :], GC, signal=s_h)
                    dve.wait_ge(s_g1, see.add("g1", 32) - 32)
                    chain(v.tensor_tensor(tmpB[:, :, :], cols(Y, g), wide(cols(invdeg, g), GC), ALU.mult))
                    take_scores(Sd, g)
                else:
                    v.tensor_tensor(tmpA[:, :, :], cols(Y, g), wide(cols(invdeg, g), GC), ALU.mult).then_inc(s_h, 1)
                    step(v.tensor_tensor(rows[:, :, :], rows[:, :, :], cols(Xs, g), ALU.add))
                    add_units(at, GU)
                mark("xu")

            dve.wait_ge(s_ds, 32)
            with dve.Fori(0, G) as g:
                see.enter(g, TURN["rows"])
                src_norm(0, g)
                dense_first()
                src_units(g)
                dense_rest()
                see.leave(G)
            with dve.Fori(0, LONE) as g:
                see.enter(g, TURN["lone"])
                dense_first()
                dense_rest()
                see.leave(LONE)
            dve.wait_ge(s_hc, see.value("hc"))
            with dve.Fori(0, G) as g:
                see.enter(g, TURN["table"])
                table_rows(g)
                dense_first()
                dense_rest()
                see.leave(G)

            for stage in range(STAGES):
                if stage == 1:
                    dve.wait_ge(s_ea, 32 * G)
                if stage == 4:
                    dve.wait_ge(s_g1, 32 * G + 1)
                if stage in DENSE_STAGES:
                    dve.wait_ge(s_xs, 32 * G * min(stage, 3))
                if stage > 0:
                    with dve.Fori(0, G) as g:
                        see.enter(g, TURN[stage])
                        if stage < 4:
                            src_norm(stage, g)
                        if stage in DENSE_STAGES:
                            dense_first()
                        if stage == 2:
                            src_units(g)
                        elif stage == 3:
                            take_scores(S, g)
                        elif stage == 4:
                            all_messages(g)
                        if stage in DENSE_STAGES:
                            dense_rest()
                        see.leave(G)
                if stage in (0, 2, 3):
                    dve.wait_ge(s_hc, see.value("hc"))
                settle()
                if stage == 4:
                    dve.wait_ge(s_gx, 16 * T * 5)
                    dve.wait_ge(s_zu, GU * G + 1)
                scan_sums(Y, Xs if stage == 3 else Y)
                carry_sums(Y)
                if stage == 4:
                    scan_sums(Xs, Xs)
                    carry_sums(Xs)
                mark("sum")
                if stage == 1:
                    see.add("hc", G)
                see.by_pairs(dve, DST_TURN[stage], lambda g, b: dst_work(stage, g, b))
                if stage == 3:
                    step(v.memset(Y[:, :, :], 0.0))
                mark("st")
                if stage == 3:
                    softmax()


_INS = ['x', 'src', 'dst', 'edge_attr_64', 'L0_gnn_memory_weights', 'L0_gnn_gru_w_ih', 'L0_gnn_gru_b_ih',
        'L0_gnn_gru_b_hh', 'L0_gnn_wt_w', 'L0_gnn_wt_b', 'L0_gnn_gcn_bias', 'L1_gnn_W1', 'L1_gnn_b1', 'L1_gnn_W2',
        'L1_gnn_b2', 'L2_gnn_W_self', 'L2_gnn_W_neigh', 'L2_gnn_bias', 'L3_gnn_W_att', 'L3_gnn_a_src', 'L3_gnn_a_dst',
        'L3_gnn_W_g', 'L3_gnn_b_g', 'L3_gnn_W_w', 'L3_gnn_b_w']


def kernel(**inputs):
    import concourse.bacc as _bacc
    from concourse.bass_utils import run_bass_kernel_spmd as _run

    nc = _bacc.Bacc("TRN2", target_bir_lowering=False, num_devices=1)
    arrays, args = {}, {}
    for name in _INS:
        v = np.ascontiguousarray(inputs[name])
        arrays[f"in_{name}"] = v
        args[name] = nc.dram_tensor(f"in_{name}", v.shape, mybir.dt.from_np(v.dtype), kind="ExternalInput").ap()
    out = nc.dram_tensor("out_0", (N, D), F32, kind="ExternalOutput").ap()
    gnn_kernel(nc, args, out)
    return _run(nc, [arrays], core_ids=[0]).results[0]["out_0"]
```

```python
import numpy as np
import concourse.bass as bass
from concourse import mybir

F32 = mybir.dt.float32
I32 = mybir.dt.int32
ALU = mybir.AluOpType
ACT = mybir.ActivationFunctionType
AX = mybir.AxisListType

N, E, D = 100000, 25000, 64
P = 125
T = E // P
G = 5
GC = T // G
UC = 8
GU = GC // UC
HALF = GC // 2
NODES = N // P
STAGES = 5
DC = 32
DU = DC // UC
HC, HU = DC // 2, DU // 2
LONE = 5
DENSE_STAGES = (1,)
RK = 4
HEADS = 4
HID = 2 * D
EPS = 1e-5
SLOPE = 0.2
BIG = 1e30
NOREP = 32768


_NORM, _MOMENTS = 8, 7


def _turn(dense=False, **edge):
    chunk = {"dl": 32, "ds0": 32, "ds1": 32, "df": 1, "dr": 2, "std": 3, "o": 2 * DU,
             "dve": 2 * _NORM + _MOMENTS + 2} if dense else {}
    return {k: edge.get(k, 0) + chunk.get(k, 0) for k in {**edge, **chunk}}


TURN = {
    "rows": _turn(True, gx=16 * HALF, hc=1, std=1, o=GU, dve=_NORM),
    "lone": _turn(True),
    "table": _turn(True, gt=16 * HALF, std=1, dve=3),
    1: _turn(1 in DENSE_STAGES, gx=16 * HALF, std=1, dve=_NORM + 3),
    2: _turn(2 in DENSE_STAGES, gx=16 * HALF, hc=1, std=2, o=2 * GU, dve=2 * _NORM, xl0=32, xu=1, zs=32),
    3: _turn(3 in DENSE_STAGES, gx=16 * HALF, hc=1, std=2, o=2 * GU, dve=2 * _NORM, xl0=32, xu=1),
    4: _turn(am=HEADS * GU),
}
BY_BUFFER = {"xl0": 32, "xl1": 32}
DST_TURN = [
    _turn(True, gd=16 * HALF, xu=1, o=GU, dve=_NORM + 3, std=1),
    {**BY_BUFFER, "xu": 1, "o": GU},
    {**BY_BUFFER, "zl": 32, "xu": 1, "o": GU},
    {"dve": 1, "xu": 1},
    {**BY_BUFFER, "xu": 1, "o": GU, "dve": 1},
]


class Seen:

    def __init__(self):
        self.n, self.g, self.per, self.start = {name: 1 for name in COUNT_FROM_ONE}, None, {}, {}

    def add(self, name, k=1):
        self.n[name] = self.n.get(name, 0) + k
        return self.value(name)

    def value(self, name):
        v = self.n.get(name, 0)
        return v if self.g is None else self.g * self.per.get(name, 0) + v

    def by_pairs(self, engine, per, body):
        with engine.Fori(0, G // 2) as k:
            self.enter(k, {name: v if name in ("xl0", "xl1") else 2 * v for name, v in per.items()})
            body(k * 2, 0)
            body(k * 2 + 1, 1)
            self.leave(G // 2)
        body(G - 1, 0)

    def enter(self, g, per):
        self.g, self.per, self.start = g, per, dict(self.n)

    def leave(self, turns):
        got = {k: v - self.start.get(k, 0) for k, v in self.n.items() if v != self.start.get(k, 0)}
        assert got == {k: v for k, v in self.per.items() if v}, (got, self.per)
        for k, v in got.items():
            self.n[k] += v * (turns - 1)
        self.g, self.per = None, {}


COUNT_FROM_ONE = ("o", "zu", "am", "hc", "df", "dr", "xu", "ds1")


def gnn_kernel(nc, a, out):
    def sb(name, shape, dt=F32):
        return nc.alloc_sbuf_tensor(name, shape, dt)

    def sem(name):
        return nc.alloc_semaphore(name)

    src_s = nc.dram_tensor("src_s", (E, 1), I32, kind="Internal").ap()
    dst_s = nc.dram_tensor("dst_s", (E, 1), I32, kind="Internal").ap()
    ea_s = nc.dram_tensor("ea_s", (E, D), F32, kind="Internal").ap()
    rank_d = nc.dram_tensor("rank_d", (E, 1), I32, kind="Internal").ap()
    node_tab = nc.dram_tensor("node_tab", (N, 2), F32, kind="Internal").ap()
    xt = nc.dram_tensor("xt", (E, D), F32, kind="Internal").ap()
    gt = nc.dram_tensor("gt", (E, D), F32, kind="Internal").ap()
    zt = nc.dram_tensor("zt", (E, D), F32, kind="Internal").ap()
    xt_v = xt.rearrange("(p t) d -> p t d", p=P)
    zt_v = zt.rearrange("(p t) d -> p t d", p=P)
    gt_v = gt.rearrange("(p t) d -> p t d", p=P)
    src_v, dst_v, rank_v = (t.rearrange("(p t) a -> p (t a)", p=P) for t in (src_s, dst_s, rank_d))
    src_in, dst_in = (a[name].rearrange("(p t) -> p t", p=P) for name in ("src", "dst"))
    ea_in = a["edge_attr_64"].rearrange("(p t) d -> p t d", p=P)
    ea_v = ea_s.rearrange("(p t) d -> p t d", p=P)
    x_v = a["x"].rearrange("(p t) d -> p t d", p=P)
    out_v = out.rearrange("(p t) d -> p t d", p=P)

    Xs = sb("Xs", [P, T, D])
    Y = sb("Y", [128, T, D])
    tmpA = sb("tmpA", [P, GC, D])
    tmpB = sb("tmpB", [P, GC, D])
    xdg = sb("xdg", [P, GC, D])
    din = sb("din", [P, DC, D])
    dbuf = sb("dbuf", [P, 2 * DC, D])
    dout = dbuf[:, 0:DC, :]
    dh = dbuf[:, DC:2 * DC, :]
    xd = [xdg, dbuf[:, 0:GC, :]]
    xd0 = [xdg, tmpB]
    HT = sb("HT", [128, 2, 512])
    YT = sb("YT", [128, 2, 512])
    src_i = sb("src_i", [P, T], I32)
    dst_i = sb("dst_i", [P, T], I32)
    rep_i = sb("rep_i", [P, T], I32)
    sct_i = sb("sct_i", [P, T], I32)
    dstf = sb("dstf", [P, T])
    nextf = sb("nextf", [P, 1])
    next_i = sb("next_i", [P, 1], I32)
    same = sb("same", [P, T])
    notlast = sb("notlast", [P, T])
    infirst = sb("infirst", [P, T])
    inopen = sb("inopen", [P, T])
    dinvd = sb("dinvd", [P, T])
    dinvs = sb("dinvs", [P, T])
    invdeg = sb("invdeg", [P, T])
    S = sb("S", [P, T, HEADS])
    Sd = sb("Sd", [P, T, HEADS])
    Tg = sb("Tg", [P, T, 2])
    W8 = sb("W8", [P, T])
    st = sb("st", [P, GC, 6])
    sm = sb("sm", [P, 6, GC])
    smd = sb("smd", [P, 6, DC])
    ident = sb("ident", [128, 128])
    ones = sb("ones", [128, 128])
    Kc = sb("Kc", [P, P])
    KP = sb("KP", [P, P])
    Bm = sb("Bm", [P, P])
    diag = sb("diag", [P, HEADS, P])
    BW = sb("BW", [128, 8, 128])
    BV = sb("BV", [128, 2, 2 * HEADS])
    W1 = sb("W1", [128, HID])
    W2 = sb("W2", [HID, D])
    brow = sb("brow", [1, 5, D])
    c1b = sb("c1b", [P, D])
    b1c = sb("b1c", [128, 2])
    b2c = sb("b2c", [128, 1])
    carry = sb("carry", [P, D])
    near_i = sb("near_i", [P, RK], I32)
    near = sb("near", [P, RK])
    place = sb("place", [P, RK])
    own = sb("own", [P, T])
    rank = sb("rank", [P, T])
    rank_i = sb("rank_i", [P, T], I32)
    bad = sb("bad", [P, 4])
    turns_i = sb("turns_i", [1, 2], I32)
    move_rank = sb("move_rank", [P, 1], I32)
    move_src = sb("move_src", [P, 1], I32)
    move_dst = sb("move_dst", [P, 1], I32)
    move_ea = sb("move_ea", [P, D])
    lmax = sb("lmax", [1, 2])
    lmax_i = sb("lmax_i", [1, 1], I32)
    c8 = sb("c8", [P, 4])
    gru = tmpB[0:64, 0:4, :]
    gsm = sb("gsm", [64, 12])
    wtb = din[0:64, 0:2, :]
    BROW_L0, BROW_DENSE, BROW_L1, BROW_L2, BROW_END = range(5)
    W_L0, W_SELF, W_NEIGH, W_ATT, W_HOP = 0, 1, 2, 3, 7

    wa = sb("wa", [128, 4, D])
    aB = sb("aB", [128, 2, 4, D])
    wg = sb("wg", [128, D])
    wwt = sb("wwt", [64, 2, D])
    bgc = sb("bgc", [64, 1])
    bwr = sb("bwr", [1, 4, D])


    epsc = sb("epsc", [P, 1])
    BF16 = mybir.dt.bfloat16
    ones_b = sb("ones_b", [3, P], BF16)
    parts_b = sb("parts_b", [3, 5, D], BF16)
    part = sb("part", [1, 3, 5 * D], BF16)
    rest = sb("rest", [1, 5 * D])
    bcol = sb("bcol", [P, 12])
    mcol = sb("mcol", [P, 16])
    psT = [nc.alloc_psum_tensor(f"psT{i}", [128, 512], F32) for i in range(2)]
    psM = [nc.alloc_psum_tensor(f"psM{i}", [128, 512], F32) for i in range(2)]
    psO = [nc.alloc_psum_tensor(f"psO{i}", [128, 512], F32) for i in range(2)]
    psZ = nc.alloc_psum_tensor("psZ", [128, 512], F32)
    psS = nc.alloc_psum_tensor("psS", [128, 512], F32)
    ring = psO + [psZ, psS]

    s_raw = sem("edges_loaded")
    s_rawc = sem("edges_copied")
    s_eac = sem("edge_attr_copied")
    s_rl = sem("rank_dst_loaded")
    s_ru = sem("rank_dst_used")
    s_rc = sem("rank_chain")
    s_bad = sem("disorder_counted")
    s_nb = sem("disorder_summed")
    s_turns = sem("turns_ready")
    s_rank = sem("ranks_ready")
    s_rs = sem("ranks_stored")
    s_ml = sem("edge_column_loaded")
    s_mo = sem("edge_column_moved")
    s_al = sem("attr_column_loaded")
    s_ao = sem("attr_column_moved")
    s_perm = sem("edges_in_order")
    s_edges = sem("ordered_edges_loaded")
    s_in = sem("inputs_loaded")
    s_preset = sem("constants_preset")
    s_kcut = sem("carry_matrices_cut")
    s_dve = sem("dve_chain")
    s_gate = sem("gates_summed")
    s_act = sem("act_setup")
    s_um = sem("memory_updated")
    s_c1 = sem("c1_row_ready")
    s_ids = sem("ids_on_diagonals")
    s_kraw = sem("carry_matrices_raw")
    s_cnt = sem("counts_scanned")
    s_pay = sem("payload_ready")
    s_set = sem("setup_done")
    s_pe = sem("setup_product")
    s_part = sem("bias_parts_split")
    s_parts = sem("bias_parts_spread")
    s_tab = sem("node_table_written")
    s_gx = [sem("src_rows_gathered_{z}".format(z=z)) for z in "ab"]
    s_gt = [sem("table_rows_gathered_{z}".format(z=z)) for z in "ab"]
    s_gd = [sem("dst_rows_gathered_{z}".format(z=z)) for z in "ab"]
    s_xs = sem("dst_rows_stored")
    s_xl = [sem("dst_rows_loaded"), sem("dst_rows_loaded_ahead")]
    s_xu = sem("dst_rows_updated")
    s_zs = sem("self_parts_stored")
    s_zl = sem("self_parts_loaded")
    s_ea = sem("edge_attr_loaded")
    s_var = sem("variances_ready")
    s_std = sem("roots_ready")
    s_h = sem("h_ready")
    s_hc = sem("h_copied")
    s_tr = sem("transposed")
    s_ht = sem("transposed_evacuated")
    s_m = sem("mid_ready")
    s_y = sem("mid_evacuated")
    s_o = sem("unit_ready")
    s_ou = sem("unit_used")
    s_am = sem("head_done")
    s_zu = sem("messages_used")
    s_dl = sem("dense_loaded")
    s_df = sem("dense_input_free")
    s_dr = sem("dense_result_ready")
    s_ds = [sem("dense_result_stored_a"), sem("dense_result_stored_b")]
    s_sum = sem("stage_sums_ready")
    s_st = sem("stage_done")
    s_fix = sem("carries_added")
    s_ct = sem("tails_ready")
    s_cp = sem("carries_ready")
    s_ex = sem("exp_input_ready")
    s_exd = sem("exp_done")
    s_g1 = sem("hop_rows_stored")
    s_out = [sem("rows_scattered_{z}".format(z=z)) for z in "ab"]

    PARTS = [(0, 120), (120, P)]

    def row(v):
        return v.rearrange("(a m) -> a m", a=1)

    def column(v):
        return v.rearrange("(p a) -> p a", a=1)

    loads = [
        (gru[:, 0:3, :], a["L0_gnn_gru_w_ih"].rearrange("(g j) m -> j g m", g=3)),
        (gru[:, 3, :], row(a["L0_gnn_memory_weights"]).to_broadcast([64, D])),
        (gsm[:, 0:3], a["L0_gnn_gru_b_ih"].rearrange("(g j) -> j g", g=3)),
        (gsm[:, 3:6], a["L0_gnn_gru_b_hh"].rearrange("(g j) -> j g", g=3)),
        (W2[:, :], a["L1_gnn_W2"]),
        (b1c[:, 0:1], column(a["L1_gnn_b1"])),
        (bwr[:, 0, :], row(a["L0_gnn_gcn_bias"])),
        (bwr[:, 1, :], row(a["L1_gnn_b2"])),
        (bwr[:, 2, :], row(a["L3_gnn_b_w"])),
        (bwr[:, 3, :], row(a["L2_gnn_bias"])),
        (wwt[:, :, :], a["L3_gnn_W_w"].rearrange("(a i) o -> i a o", a=2)),
        (bgc[:, :], column(a["L3_gnn_b_g"])),
    ]
    for k, name in enumerate(("L3_gnn_a_src", "L3_gnn_a_dst")):
        loads.append((aB[:, k, :, :].rearrange("p h o -> p (h o)"),
                      a[name].rearrange("(a h) o -> a (h o)", a=1).to_broadcast([128, HEADS * D])))
    for k in range(2):
        h = slice(64 * k, 64 * k + 64)
        loads += [
            (Y[h, 0:64, :], a["L0_gnn_wt_w"].rearrange("(o i) m -> i o m", i=D)),
            (wtb[:, k, :], a["L0_gnn_wt_b"].rearrange("(o i) -> o i", i=D)),
            (W1[h, :], a["L1_gnn_W1"]),
            (b2c[h, :], column(a["L2_gnn_bias"])),
            (wa[h, :, :], a["L3_gnn_W_att"].rearrange("h i o -> i h o")),
            (wg[h, :], a["L3_gnn_W_g"]),
            (BW[h, W_SELF, h], a["L2_gnn_W_self"]),
            (BW[h, W_NEIGH, h], a["L2_gnn_W_neigh"]),
        ]
    NLOAD = 16 * len(loads)
    CHUNKS = NODES // DC
    FIRST_CHUNK = {"rows": 0, "lone": G, "table": G + LONE,
                   "dst": 2 * G + LONE,
                   **{stage: (3 + i) * G + LONE for i, stage in enumerate(DENSE_STAGES)}}
    assert (3 + len(DENSE_STAGES)) * G + LONE == CHUNKS

    def chunks_before(stage):
        return 3 * G + LONE + G * sum(s <= stage for s in DENSE_STAGES)

    CARRY = {0: ["sum"], 1: ["sum"], 2: ["sum"], 3: ["sum"], 4: ["sum", "messages"]}
    SOFTMAX = ["hold", "max", "hold", "den", "hold"]

    def cols(t, g, lo=0, n=GC):
        return t[0:P, bass.ds(g * GC + lo, n)] if len(t.shape) == 2 else t[0:P, bass.ds(g * GC + lo, n), :]

    def both(engine, semaphores, count):
        for semaphore in semaphores:
            engine.wait_ge(semaphore, count)

    def pairs(t, c):
        return t[0:P, c:c + 2, :].rearrange("p a b -> p (a b)")

    def unit_rows(ps):
        return ps[0:P, :].rearrange("p (c d) -> p c d", d=D)

    with nc.Block() as block:

        @block.sync
        def _(sp):
            see = Seen()

            def await_(semaphore, count):
                sp.wait_ge(semaphore, count)
                sp.nop(nofuse=True)

            def await_both(semaphores, count):
                for semaphore in semaphores:
                    await_(semaphore, count)

            def dense_load(c):
                for lo, hi in PARTS:
                    sp.dma_start(din[lo:hi, :, :], x_v[lo:hi, bass.ts(c, DC), :]).then_inc(s_dl, 16)

            def dense_store(c):
                for z in range(2):
                    await_(s_dr, see.add("dr"))
                    for lo, hi in PARTS:
                        sp.dma_start(out_v[lo:hi, bass.ds(c * DC + HC * z, HC), :], dout[lo:hi, HC * z:HC * z + HC, :]).then_inc(s_ds[z], 16)

            def dense_stored(chunks):
                for z in range(2):
                    await_(s_ds[z], 32 * (chunks + 1) if z == 0 else 32 * chunks + 1)

            def x_load(g, b):
                for lo, hi in PARTS:
                    sp.dma_start(xd[b][lo:hi, :, :], xt_v[lo:hi, bass.ts(g, GC), :]).then_inc(s_xl[b], 16)

            def x_store(g, b, buffers=xd):
                for lo, hi in PARTS:
                    sp.dma_start(xt_v[lo:hi, bass.ts(g, GC), :], buffers[b][lo:hi, :, :]).then_inc(s_xs, 16)
                await_(s_xs, see.add("xs", 32))

            for lo, hi in PARTS:
                sp.dma_start(dst_i[lo:hi, :], dst_in[lo:hi, :]).then_inc(s_raw, 16)
                sp.dma_start(src_i[lo:hi, :], src_in[lo:hi, :]).then_inc(s_raw, 16)
            sp.wait_ge(s_preset, 3)
            sp.dma_start(next_i[0:P - 1, :], dst_in[1:P, 0:1], allow_slow_non_contiguous=True).then_inc(s_raw, 16)
            for dst, src in loads:
                sp.dma_start(dst, src, allow_slow_non_contiguous=True).then_inc(s_in, 16)
            for lo, hi in PARTS:
                sp.dma_start(node_tab.rearrange("(p n) c -> p (n c)", p=P)[lo:hi, :],
                             tmpA[lo:hi, 0:25, :].rearrange("p a b -> p (a b)")).then_inc(s_ds[0], 16)
            sp.wait_ge(s_raw, 80)
            for lo, hi in PARTS:
                sp.dma_start(src_v[lo:hi, :], src_i[lo:hi, :]).then_inc(s_rawc, 16)
                sp.dma_start(dst_v[lo:hi, :], dst_i[lo:hi, :]).then_inc(s_rawc, 16)
            sp.wait_ge(s_turns, 1)
            rank_turns = sp.value_load(turns_i[0:1, 0:1], min_val=1, max_val=E // RK)
            with sp.Fori(0, rank_turns) as k:
                await_(s_ru, k + 1)
                sp.dma_start(near_i[:, :], a["dst"].rearrange("(a m) -> a m", a=1)[:, bass.ts(k, RK)].to_broadcast([P, RK])).then_inc(s_rl, 16)
            sp.wait_ge(s_rank, 1)
            for lo, hi in PARTS:
                sp.dma_start(rank_v[lo:hi, :], rank_i[lo:hi, :]).then_inc(s_rs, 16)
            sp.wait_ge(s_perm, 1)
            for lo, hi in PARTS:
                sp.dma_start(src_i[lo:hi, :], src_v[lo:hi, :]).then_inc(s_edges, 16)
                sp.dma_start(dst_i[lo:hi, :], dst_v[lo:hi, :]).then_inc(s_edges, 16)
            sp.dma_start(next_i[0:P - 1, :], dst_v[1:P, 0:1], allow_slow_non_contiguous=True).then_inc(s_edges, 16)
            sp.dma_start(ea_s, a["edge_attr_64"]).then_inc(s_eac, 16)
            sp.wait_ge(s_part, 3)
            for k in range(3):
                sp.dma_start(parts_b[k:k + 1, :, :].rearrange("p a b -> p (a b)"), part[:, k, :]).then_inc(s_parts, 16)
            sp.wait_ge(s_set, 1)
            dense_load(0)

            def chunk(c, last=False):
                await_(s_df, see.add("df"))
                if not last:
                    dense_load(c + 1)
                dense_store(c)

            for phase, turns in (("rows", G), ("lone", LONE), ("table", G)):
                with sp.Fori(0, turns) as g:
                    see.enter(g, {"df": 1, "dr": 2})
                    chunk(g + FIRST_CHUNK[phase])
                    see.leave(turns)

            for stage in range(STAGES):
                if stage == 1:
                    sp.wait_ge(s_st, 1)
                    sp.wait_ge(s_perm, 2)
                    for g in range(G):
                        for lo, hi in PARTS:
                            sp.dma_start(Y[lo:hi, g * GC:(g + 1) * GC, :], ea_v[lo:hi, g * GC:(g + 1) * GC, :]).then_inc(s_ea, 16)
                src_turn = {**({"df": 1, "dr": 2} if stage in DENSE_STAGES else {}), **({"xu": 1} if stage in (2, 3) else {})}

                def src_work(g, last=False):
                    if stage == 2:
                        await_(s_xu, see.add("xu"))
                        for lo, hi in PARTS:
                            sp.dma_start(zt_v[lo:hi, bass.ts(g, GC), :], tmpB[lo:hi, :, :]).then_inc(s_zs, 16)
                        if not last:
                            x_load(g + 1, 0)
                    elif stage == 3:
                        x_load(g, 0)
                        await_(s_xu, see.add("xu"))
                    if stage in DENSE_STAGES:
                        chunk(g + FIRST_CHUNK[stage], last)

                if stage == 2:
                    x_load(0, 0)
                if src_turn:
                    with sp.Fori(0, G - 1) as g:
                        see.enter(g, src_turn)
                        src_work(g)
                        see.leave(G - 1)
                    src_work(G - 1, last=stage in (2, DENSE_STAGES[-1]))
                if stage == 2:
                    sp.wait_ge(s_zs, 32 * G)

                def z_load(g):
                    for lo, hi in PARTS:
                        sp.dma_start(tmpA[lo:hi, :, :], zt_v[lo:hi, bass.ts(g, GC), :]).then_inc(s_zl, 16)

                def dst_rows(g, b):
                    last = isinstance(g, int) and g == G - 1
                    if stage > 0 and not last:
                        x_load(g + 1, 1 - b)
                    await_(s_xu, see.add("xu"))
                    if stage == 2 and not last:
                        z_load(g + 1)
                    if stage < 3:
                        x_store(g, b)
                    else:
                        await_both(s_out, see.add("out", 16 * HALF))

                if stage == 3:
                    for g in range(G):
                        sp.wait_ge(s_xu, see.add("xu"))
                        for lo, hi in PARTS:
                            sp.dma_start(gt_v[lo:hi, g * GC:(g + 1) * GC, :], Y[lo:hi, g * GC:(g + 1) * GC, :]).then_inc(s_g1, 16)
                    continue
                if stage == 0:
                    def first_rows(g, b):
                        await_(s_df, see.add("df"))
                        dense_load(g + FIRST_CHUNK["dst"] + 1)
                        await_(s_xu, see.add("xu"))
                        x_store(g, b, xd0)
                        dense_store(g + FIRST_CHUNK["dst"])

                    see.by_pairs(sp, {"xu": 1, "xs": 32, "df": 1, "dr": 2}, first_rows)
                    continue
                if stage > 0:
                    dense_stored(chunks_before(stage))
                    x_load(0, 0)
                if stage == 2:
                    sp.wait_ge(s_sum, 3)
                    z_load(0)
                see.by_pairs(sp, {"xu": 1, **({"xs": 32} if stage < 3 else {"out": 16 * HALF})}, dst_rows)
            dense_stored(CHUNKS)

        @block.gpsimd
        def _(pool):
            see = Seen()
            nc.gpsimd.memset(BW[:, :, :], 0.0).then_inc(s_preset, 1)
            nc.gpsimd.memset(next_i[:, :], -1).then_inc(s_preset, 1)
            nc.gpsimd.memset(tmpA[:, :, :], 0.0).then_inc(s_preset, 1)
            nc.gpsimd.memset(ones[:, :], 1.0).then_inc(s_preset, 1)
            nc.gpsimd.memset(BV[:, :, :], 0.0).then_inc(s_preset, 1)
            nc.gpsimd.memset(ones_b[:, :], 1.0).then_inc(s_preset, 1)
            nc.gpsimd.iota(rep_i[:, :], pattern=[[1, T]], base=-NOREP, channel_multiplier=T).then_inc(s_preset, 1)
            nc.gpsimd.memset(epsc[:, :], EPS).then_inc(s_preset, 1)
            for k, semaphore in enumerate((s_o, s_ou, s_zu, s_am, s_hc, s_df, s_dr, s_xu, s_ru, s_ds[1])):
                nc.gpsimd.memset(bcol[:, k:k + 1], 0.0).then_inc(semaphore, 1)
            nc.gpsimd.memset(ident[:, :], 0.0).then_inc(s_preset, 1)
            pool.wait_ge(s_preset, 9)
            nc.gpsimd.affine_select(out=ident[:, :], in_=ident[:, :], compare_op=ALU.not_equal, fill=1.0,
                                    base=0, pattern=[[-1, 128]], channel_multiplier=1).then_inc(s_preset, 1)
            def cut_carry_matrices():
                pool.wait_ge(s_kraw, 3)
                nc.gpsimd.affine_select(out=Kc[:, :], in_=Kc[:, :], compare_op=ALU.is_ge, fill=0.0,
                                        base=-1, pattern=[[1, P]], channel_multiplier=-1).then_inc(s_kcut, 1)
                for m in (Bm, KP):
                    nc.gpsimd.affine_select(out=m[:, :], in_=m[:, :], compare_op=ALU.is_ge, fill=0.0,
                                            base=-1, pattern=[[-1, P]], channel_multiplier=1).then_inc(s_kcut, 1)

            def gather(dst, table, rows, index, t, s):
                nc.gpsimd.indirect_dma_start(dst, None, table, bass.IndirectOffsetOnAxis(ap=index[:, t:t + 1], axis=0),
                                             bounds_check=rows - 1, oob_is_err=False).then_inc(s, 16)

            def scatter(table, rows, index, t, src, s):
                nc.gpsimd.indirect_dma_start(table, bass.IndirectOffsetOnAxis(ap=index[:, t:t + 1], axis=0), src, None,
                                             bounds_check=rows - 1, oob_is_err=False).then_inc(s, 16)

            def group(g, before, semaphores, issue):
                for z in range(2):
                    if before > 0:
                        pool.wait_ge(semaphores[z], 16 * HALF * before)
                    for t in range(g * GC + z * HALF, g * GC + (z + 1) * HALF):
                        issue(t, semaphores[z])

            def await_(semaphore, count):
                pool.wait_ge(semaphore, count)
                pool.nop(nofuse=True)

            pool.wait_ge(s_turns, 1)
            move_turns = pool.value_load(turns_i[0:1, 1:2], min_val=1, max_val=T)
            pool.wait_ge(s_rs, 32)
            pool.wait_ge(s_rawc, 64)
            with pool.Fori(0, move_turns) as t:
                for dst, src in ((move_rank, rank_v), (move_src, src_in), (move_dst, dst_in)):
                    nc.gpsimd.dma_start(dst[:, :], src[:, bass.ts(t, 1)], allow_slow_non_contiguous=True).then_inc(s_ml, 16)
                await_(s_ml, t * 48 + 48)
                scatter(src_s, E, move_rank, 0, move_src[:, :], s_mo)
                scatter(dst_s, E, move_rank, 0, move_dst[:, :], s_mo)
                await_(s_mo, t * 32 + 32)
            nc.gpsimd.memset(bcol[:, 11:12], 0.0).then_inc(s_perm, 1)

            def permute_attr():
                pool.wait_ge(s_eac, 16)
                with pool.Fori(0, move_turns) as t:
                    nc.gpsimd.dma_start(move_rank[:, :], rank_v[:, bass.ts(t, 1)], allow_slow_non_contiguous=True).then_inc(s_al, 16)
                    nc.gpsimd.dma_start(move_ea[:, :], ea_in[:, bass.ts(t, 1), :].rearrange("p a d -> p (a d)")).then_inc(s_al, 16)
                    await_(s_al, t * 32 + 32)
                    scatter(ea_s, E, move_rank, 0, move_ea[:, :], s_ao)
                    await_(s_ao, t * 16 + 16)
                nc.gpsimd.memset(bcol[:, 10:11], 0.0).then_inc(s_perm, 1)

            pool.wait_ge(s_edges, 80)
            pool.wait_ge(s_in, NLOAD)
            for z in range(2):
                for t in range(z * HALF, (z + 1) * HALF):
                    gather(Xs[:, t, :], a["x"], N, src_i, t, s_gx[z])
                if z == 0:
                    cut_carry_matrices()
            for g in range(1, G):
                group(g, g, s_gx, lambda t, s: gather(Xs[:, t, :], a["x"], N, src_i, t, s))
            permute_attr()
            pool.wait_ge(s_pay, 1)
            pool.wait_ge(s_ds[0], 32)
            for t in range(T):
                scatter(node_tab, N, sct_i, t, Tg[:, t, :], s_tab)
            pool.wait_ge(s_tab, 16 * T)
            for g in range(G):
                group(g, g, s_gt, lambda t, s: gather(Tg[:, t, :], node_tab, N, src_i, t, s))
            for g in range(G):
                if g == 1:
                    pool.wait_ge(s_hc, G + 1)
                if g > 1:
                    pool.wait_ge(s_xs, 32 * (g - 1))
                group(g, g, s_gd, lambda t, s: gather(xd0[g % 2][:, t - g * GC, :], a["x"], N, dst_i, t, s))
            for stage in range(1, STAGES):
                pool.wait_ge(s_st, stage)
                if stage < 4:
                    pool.wait_ge(s_xs, 32 * G * stage)
                else:
                    pool.wait_ge(s_g1, 32 * G)
                for g in range(G):
                    if stage < 4:
                        group(g, stage * G + g, s_gx, lambda t, s: gather(Xs[:, t, :], xt, E, rep_i, t, s))
                    else:
                        group(g, stage * G + g, s_gx, lambda t, s: gather(Y[0:P, t, :], gt, E, rep_i, t, s))
            pool.wait_ge(s_ds[0], 32 * (CHUNKS + 1))
            pool.wait_ge(s_ds[1], 32 * CHUNKS + 1)
            for g in range(G):
                pool.wait_ge(s_xu, 6 * G + g + 2)
                group(g, g, s_out, lambda t, s: scatter(out, N, sct_i, t, xd[g % 2][:, t - g * GC, :], s))
            for z in range(2):
                pool.wait_ge(s_out[z], 16 * HALF * G)

        @block.tensor
        def _(pe):
            see = Seen()

            def done(ins):
                ins.then_inc(s_pe, 1)

            pe.wait_ge(s_bad, 1)
            pe.wait_ge(s_preset, 10)
            nc.tensor.matmul(psS[0:P, 0:1], ones[0:P, 0:P], bad[:, 0:1], start=True, stop=True).then_inc(s_nb, 1)
            pe.wait_ge(s_in, NLOAD)
            pe.wait_ge(s_preset, 10)
            done(nc.tensor.transpose(psO[0][:, 0:64], wtb.rearrange("p a b -> p (a b)"), ident[0:64, 0:64]))
            for h in range(HEADS):
                done(nc.tensor.transpose(psT[0][0:64, 128 * h:128 * h + 128], wa[:, h, :], ident[:, :]))
            done(nc.tensor.transpose(psT[1][0:64, 0:128], wg[:, :], ident[:, :]))
            pe.wait_ge(s_um, 2)
            done(nc.tensor.matmul(psS[:, 0:64], ones[0:64, :], diag[0:64, 0, 0:64], start=True, stop=True))
            done(nc.tensor.matmul(psO[1][0:1, 0:64], b1c[:, 1:2], W2[:, :], start=True, stop=True))
            done(nc.tensor.matmul(psO[1][0:1, 64:128], bgc[:, :], wwt[:, 1, :], start=True, stop=True))
            pe.wait_ge(s_act, 4)
            for h in range(HEADS):
                done(nc.tensor.matmul(psM[0][:, 64 * h:64 * h + 64], HT[0:64, 0, 128 * h:128 * h + 128],
                                      wwt[:, 0, :], start=True, stop=True))
            done(nc.tensor.matmul(psM[0][:, 256:320], HT[0:64, 1, 0:128], wwt[:, 1, :], start=True, stop=True))
            pe.wait_ge(s_c1, 1)
            done(nc.tensor.matmul(psO[1][0:P, 128:192], ones[0:1, 0:P], carry[0:1, :], start=True, stop=True))
            pe.wait_ge(s_ids, 2)
            done(nc.tensor.matmul(psS[0:P, 64:64 + P], ones[0:P, 0:P], diag[:, 1, :], start=True, stop=True))
            done(nc.tensor.matmul(psS[0:P, 192:192 + P], ones[0:P, 0:P], diag[:, 2, :], start=True, stop=True))
            pe.wait_ge(s_cnt, 1)
            pe.wait_ge(s_kcut, 3)
            done(nc.tensor.matmul(psS[0:P, 320:321], Kc[:, :], invdeg[:, T - 1:T], start=True, stop=True))
            done(nc.tensor.transpose(psS[0:1, 384:384 + P], c8[:, 0:1], ident[0:P, 0:P]))

            def transposes(src, col, bank):
                for q in range(UC // 2):
                    last = nc.tensor.transpose(psT[bank][:, q * P:(q + 1) * P], pairs(src, col + 2 * q), ident[0:P, 0:P])
                last.then_inc(s_tr, 1)

            def bias(bank, r):
                if r is not None:
                    nc.tensor.matmul(bank[0:P, :], ones_b[:, :], parts_b[:, r:r + 1, :].to_broadcast([3, UC, D]),
                                     start=True, stop=False)

            def free_result(k, banks=2):
                n = see.add("o") - 1
                pe.wait_ge(s_ou, n if k == 0 else n - (banks - 1))

            def lin(src, col, n, w, r, at=0, banks=psO):
                pe.wait_ge(s_h, see.add("h"))
                for k in range(n + 1):
                    if k < n:
                        transposes(src, col + UC * k, k % 2)
                    if k >= 1:
                        u = k - 1
                        bank = banks[(at + u) % len(banks)]
                        free_result(at + u, len(banks))
                        bias(bank, r)
                        pe.wait_ge(s_ht, see.add("ht"))
                        for q in range(UC // 2):
                            last = nc.tensor.matmul(bank[0:P, 128 * q:128 * q + 128], HT[:, u % 2, q * P:(q + 1) * P],
                                                    BW[:, w, :], start=(r is None and q == 0), stop=(q == UC // 2 - 1))
                        last.then_inc(s_o, 1)

            def score(src, n, v):
                pe.wait_ge(s_h, see.add("h"))
                for k in range(n + 1):
                    if k < n:
                        transposes(src, UC * k, k % 2)
                    if k >= 1:
                        u = k - 1
                        free_result(u)
                        pe.wait_ge(s_ht, see.add("ht"))
                        for q in range(UC // 2):
                            last = nc.tensor.matmul(psO[u % 2][0:P, 8 * q:8 * q + 8], HT[:, u % 2, q * P:(q + 1) * P],
                                                    BV[:, v, :], start=True, stop=True)
                        last.then_inc(s_o, 1)

            def back(u, r, at, banks):
                bank = banks[(at + u) % len(banks)]
                free_result(at + u, len(banks))
                pe.wait_ge(s_y, see.add("y"))
                for q in range(UC // 2):
                    last = nc.tensor.matmul(bank[0:P, 128 * q:128 * q + 128], YT[:, u % 2, q * P:(q + 1) * P],
                                            ident[:, :], is_transpose=True, start=(q == 0), stop=(r is None and q == UC // 2 - 1))
                if r is not None:
                    last = nc.tensor.matmul(bank[0:P, :], ones_b[:, :], parts_b[:, r:r + 1, :].to_broadcast([3, UC, D]),
                                            start=False, stop=True)
                last.then_inc(s_o, 1)

            def relu_units(src, col, n, r, at=0, banks=psO):
                pe.wait_ge(s_h, see.add("h"))
                for k in range(n + 2):
                    if k < n:
                        transposes(src, col + UC * k, k % 2)
                    if 1 <= k <= n:
                        u = k - 1
                        pe.wait_ge(s_ht, see.add("ht"))
                        nc.tensor.matmul(psM[u % 2][:, 0:4 * P], BW[:, W_SELF, :], HT[:, u % 2, 0:4 * P],
                                         start=True, stop=True).then_inc(s_m, 1)
                    if k >= 2:
                        back(k - 2, r, at, banks)

            def mlp_units(src, n):
                pe.wait_ge(s_h, see.add("h"))
                transposes(src, 0, 0)
                for u in range(n):
                    if u + 1 < n:
                        transposes(src, UC * (u + 1), (u + 1) % 2)
                    pe.wait_ge(s_ht, see.add("ht"))
                    for z in range(2):
                        half = slice(64 * z, 64 * z + 64)
                        nc.tensor.matmul(psM[z][:, 0:4 * P], W1[half, :], HT[half, u % 2, 0:4 * P],
                                         start=True, stop=True).then_inc(s_m, 1)
                    free_result(u)
                    bias(psO[u % 2], BROW_L1)
                    for z in range(2):
                        pe.wait_ge(s_y, see.add("y"))
                        for q in range(UC // 2):
                            last = nc.tensor.matmul(psO[u % 2][0:P, 128 * q + 64 * z:128 * q + 64 * z + 64],
                                                    YT[:, z, q * P:(q + 1) * P], W2[:, :], start=False,
                                                    stop=(q == UC // 2 - 1 and z == 1))
                    last.then_inc(s_o, 1)

            def messages(n):
                for u in range(n):
                    src = tmpA if u % 2 == 0 else tmpB
                    pe.wait_ge(s_h, see.add("h"))
                    for k in range(HEADS + 1):
                        if k < HEADS:
                            transposes(src, UC * k, k % 2)
                        if k >= 1:
                            h = k - 1
                            if h == 0:
                                pe.wait_ge(s_zu, see.add("zu") - 1)
                            pe.wait_ge(s_ht, see.add("ht"))
                            for q in range(UC // 2):
                                last = nc.tensor.matmul(psZ[0:P, 128 * q:128 * q + 128], HT[:, h % 2, q * P:(q + 1) * P],
                                                        BW[:, W_ATT + h, :], start=(h == 0 and q == 0),
                                                       stop=(h == HEADS - 1 and q == UC // 2 - 1))
                            last.then_inc(s_am, 1)

            def carries(kinds):
                for kind in kinds:
                    pe.wait_ge(s_ct, see.add("ct"))
                    if kind == "sum":
                        last = nc.tensor.matmul(psS[0:P, 0:D], Kc[:, :], Y[0:P, T - 1, :], start=True, stop=True)
                    elif kind == "messages":
                        last = nc.tensor.matmul(psS[0:P, 0:D], Kc[:, :], Xs[:, T - 1, :], start=True, stop=True)
                    elif kind == "den":
                        last = nc.tensor.matmul(psS[0:P, 0:HEADS], Kc[:, :], Sd[:, T - 1, :], start=True, stop=True)
                    elif kind == "hold":
                        last = nc.tensor.matmul(psS[0:P, 0:HEADS], Bm[:, :], Sd[:, 0, :], start=True, stop=True)
                    else:
                        last = nc.tensor.matmul(psS[0:P, 0:HEADS * P], ones[0:P, 0:P], diag[:, :, :], start=True, stop=True)
                    last.then_inc(s_cp, 1)

            def dense_lin():
                for half in range(2):
                    lin(dh, HC * half, HU, W_L0, BROW_DENSE)

            def dense_relu():
                for half in range(2):
                    relu_units(dh, HC * half, HU, BROW_END)

            pe.wait_ge(s_parts, 48)
            CHUNK = {"h": 4, "ht": 2 * DU, "o": 2 * DU, "y": DU}

            def turn(chunk, **edge):
                return {k: edge.get(k, 0) + chunk.get(k, 0) for k in {**edge, **chunk}}

            with pe.Fori(0, G) as g:
                see.enter(g, turn(CHUNK, h=1, ht=GU, o=GU))
                dense_lin()
                lin(tmpA, 0, GU, W_L0, BROW_L0)
                dense_relu()
                see.leave(G)
            for turns in (LONE, G):
                with pe.Fori(0, turns) as g:
                    see.enter(g, CHUNK)
                    dense_lin()
                    dense_relu()
                    see.leave(turns)

            for stage in range(STAGES):
                if stage > 0:
                    per = {1: {}, 2: {"h": 2, "ht": 2 * GU, "o": 2 * GU, "y": GU}, 3: {"h": 2, "ht": 2 * GU, "o": 2 * GU},
                           4: {"h": GU, "ht": HEADS * GU, "zu": GU}}[stage]
                    with pe.Fori(0, G) as g:
                        see.enter(g, turn(CHUNK if stage in DENSE_STAGES else {}, **per))
                        if stage in DENSE_STAGES:
                            dense_lin()
                            dense_relu()
                        if stage == 2:
                            lin(tmpB, 0, GU, W_SELF, BROW_L2, 0, ring)
                            relu_units(tmpA, 0, GU, None, GU, ring)
                        elif stage == 3:
                            score(tmpB, GU, 1)
                            score(tmpA, GU, 0)
                        elif stage == 4:
                            messages(GU)
                        see.leave(G)
                carries(CARRY[stage])
                if stage == 1:
                    see.by_pairs(pe, {"h": 1, "ht": GU, "y": 2 * GU, "o": GU}, lambda g, b: mlp_units((tmpA, tmpB)[b], GU))
                elif stage != 3:
                    with pe.Fori(0, G) as g:
                        see.enter(g, turn(CHUNK if stage == 0 else {}, h=1, ht=GU, o=GU))
                        if stage == 0:
                            dense_lin()
                            lin(tmpA, 0, GU, W_L0, BROW_L0)
                            dense_relu()
                        elif stage == 2:
                            lin(tmpB, 0, GU, W_NEIGH, None)
                        else:
                            lin(tmpA, 0, GU, W_HOP, BROW_END)
                        see.leave(G)
                if stage == 3:
                    carries(SOFTMAX)

        @block.scalar
        def _(act):
            see = Seen()
            act.wait_ge(s_preset, 10)
            act.wait_ge(s_gate, 1)
            nc.scalar.activation(gsm[:, 9:11], gsm[:, 9:11], ACT.Sigmoid).then_inc(s_act, 1)
            act.wait_ge(s_gate, 2)
            nc.scalar.activation(gsm[:, 11:12], gsm[:, 11:12], ACT.Tanh).then_inc(s_act, 1)
            act.wait_ge(s_pe, 6)
            nc.scalar.activation(HT[0:64, 0, :], psT[0][0:64, :], ACT.Copy).then_inc(s_act, 1)
            nc.scalar.activation(HT[0:64, 1, 0:128], psT[1][0:64, 0:128], ACT.Copy).then_inc(s_act, 1)
            act.wait_ge(s_gate, 3)
            nc.scalar.activation(dinvd[:, :], dinvd[:, :], ACT.Sqrt).then_inc(s_act, 1)
            act.wait_ge(s_pe, 14)

            def evac(bank):
                act.wait_ge(s_tr, see.add("tr"))
                nc.scalar.activation(HT[:, bank, 0:4 * P], psT[bank][:, 0:4 * P], ACT.Copy).then_inc(s_ht, 1)

            def free_transposed(k):
                n = see.add("o") - 1
                act.wait_ge(s_o, n if k == 0 else n - 1)

            def lin(n, between=None):
                for k in range(n):
                    if k == 2 and between:
                        between()
                    free_transposed(k)
                    evac(k % 2)

            def relu(u):
                act.wait_ge(s_m, see.add("m"))
                nc.scalar.activation(YT[:, u % 2, 0:4 * P], psM[u % 2][:, 0:4 * P], ACT.Relu, bias=b2c[:, 0:1]).then_inc(s_y, 1)

            def relu_units(n, between=None):
                for k in range(n + 1):
                    if k == 2 and between:
                        between()
                    if k < n:
                        free_transposed(k)
                        evac(k % 2)
                    if k >= 1:
                        relu(k - 1)

            def mlp_units(n):
                for k in range(n + 1):
                    if k < n:
                        free_transposed(k)
                        evac(k % 2)
                    if k >= 1:
                        o = see.value("o") - (2 if k < n else 1)
                        act.wait_ge(s_o, o)
                        for z in range(2):
                            act.wait_ge(s_m, see.add("m"))
                            nc.scalar.activation(YT[:, z, 0:4 * P], psM[z][:, 0:4 * P], ACT.Relu, bias=b1c[:, 0:1]).then_inc(s_y, 1)

            def messages(n):
                for u in range(n):
                    for h in range(HEADS):
                        m = see.add("am") - 1
                        if u == 0 and h == 0:
                            act.wait_ge(s_o, see.value("o"))
                        act.wait_ge(s_am, m if h == 0 else m - 1)
                        evac(h % 2)

            def roots(n, k=sm):
                act.wait_ge(s_var, see.add("var"))
                nc.scalar.activation(k[:, 5, 0:n], k[:, 2, 0:n], ACT.Sqrt, bias=epsc[:, 0:1], scale=1.0 / D).then_inc(s_std, 1)

            def copy_h(dst, src):
                nc.scalar.activation(dst, src, ACT.Copy).then_inc(s_hc, 1)

            def dense_lin():
                see.add("h", 4)
                lin(HU)
                lin(HU)

            def dense_relu(last):
                relu_units(HU)
                if not last:
                    roots(DC, smd)
                relu_units(HU)

            def dense(last=False):
                dense_lin()
                roots(HC)
                roots(HC)
                dense_relu(last)

            CHUNK = {"h": 4, "tr": 2 * DU, "o": 2 * DU, "m": DU, "var": 3}

            def turn(chunk, **edge):
                return {k: edge.get(k, 0) + chunk.get(k, 0) for k in {**edge, **chunk}}

            roots(DC, smd)
            with act.Fori(0, G) as g:
                see.enter(g, turn(CHUNK, h=1, tr=GU, o=GU, var=1))
                dense_lin()
                roots(GC)
                act.wait_ge(s_h, see.value("h") - 1)
                see.add("h")
                copy_h(cols(Y, g), tmpA[:, :, :])
                roots(HC)
                lin(GU)
                roots(HC)
                dense_relu(False)
                see.leave(G)
            with act.Fori(0, LONE) as g:
                see.enter(g, CHUNK)
                dense()
                see.leave(LONE)
            with act.Fori(0, G) as g:
                see.enter(g, turn(CHUNK, gt=16 * HALF))
                dense()
                both(act, s_gt, see.add("gt", 16 * HALF))
                nc.scalar.activation(cols(dinvs, g), Tg[:, bass.ts(g, GC), 1], ACT.Sqrt, bias=ones[0:P, 0:1]).then_inc(s_std, 1)
                see.leave(G)

            for stage in range(STAGES):
                if stage > 0:
                    per = {1: {"var": 1}, 2: {"var": 2, "h": 2, "tr": 2 * GU, "o": 2 * GU, "m": GU},
                           3: {"var": 2, "h": 2, "tr": 2 * GU, "o": 2 * GU}, 4: {"h": GU, "tr": HEADS * GU, "am": HEADS * GU}}[stage]
                    def src_work(g, last=False):
                        if stage in DENSE_STAGES:
                            dense(last)
                        if stage == 2:
                            lin(GU, lambda: roots(GC))
                        elif stage < 4:
                            roots(GC)
                        if stage == 3:
                            see.add("h")
                            roots(GC)
                            lin(GU)
                        if stage in (2, 3):
                            act.wait_ge(s_h, see.add("h"))
                            copy_h(cols(Xs if stage == 3 else Y, g), tmpA[:, :, :])
                        if stage == 2:
                            if not last:
                                see.add("h")
                            relu_units(GU, None if last else lambda: roots(GC))
                        elif stage == 3:
                            lin(GU)
                        elif stage == 4:
                            see.add("h", GU)
                            messages(GU)

                    end = stage in (2, DENSE_STAGES[-1])
                    if stage == 2:
                        roots(GC)
                        see.add("h")
                    with act.Fori(0, G - end) as g:
                        see.enter(g, turn(CHUNK if stage in DENSE_STAGES else {}, **per))
                        src_work(g)
                        see.leave(G - end)
                    if end:
                        src_work(G - 1, last=True)
                if stage != 3:
                    with act.Fori(0, G) as g:
                        see.enter(g, turn(CHUNK if stage == 0 else {}, h=1, tr=GU, o=GU, **({"m": 2 * GU} if stage == 1 else {"var": 1} if stage == 0 else {})))
                        see.add("h")
                        if stage == 0:
                            dense_lin()
                            roots(GC)
                            roots(HC)
                            lin(GU)
                            roots(HC)
                            dense_relu(False)
                        elif stage == 1:
                            mlp_units(GU)
                        else:
                            lin(GU)
                        see.leave(G)
                if stage == 3:
                    act.wait_ge(s_ex, 1)
                    nc.scalar.activation(S[:, :, :], S[:, :, :], ACT.Exp).then_inc(s_exd, 1)

        @block.vector
        def _(dve):
            see = Seen()
            v = nc.vector

            def chain(ins):
                ins.then_inc(s_dve, 1)
                see.add("dve")

            def settle():
                dve.wait_ge(s_dve, see.value("dve"))

            def step(ins):
                chain(ins)
                settle()

            marks = {"gate": (0, s_gate), "set": (1, s_set), "df": (2, s_df), "dr": (3, s_dr), "ct": (4, s_ct),
                     "sum": (5, s_sum), "xu": (6, s_xu), "st": (7, s_st), "fix": (8, s_fix)}
            see.add("gate", 2)

            def mark(name):
                k, semaphore = marks[name]
                n = see.add(name)
                if not isinstance(n, int) or n > 1:
                    dve.wait_ge(semaphore, n - 1)
                v.memset(mcol[:, k:k + 1], 0.0).then_inc(semaphore, 1)

            dve.wait_ge(s_preset, 10)
            dve.wait_ge(s_raw, 80)
            chain(v.tensor_copy(dstf[:, :], dst_i[:, :]))
            chain(v.tensor_copy(nextf[:, :], next_i[:, :]))
            chain(v.tensor_scalar(own[:, :], rep_i[:, :], float(NOREP), None, ALU.add))
            chain(v.memset(rank[:, :], 0.0))
            settle()
            chain(v.tensor_scalar(place[:, :], own[:, 0:RK], own[:, 0:1], None, ALU.subtract))
            chain(v.tensor_tensor(W8[:, 0:T - 1], dstf[:, 1:T], dstf[:, 0:T - 1], ALU.is_lt))
            chain(v.tensor_tensor(bad[:, 1:2], nextf[:, :], dstf[:, T - 1:T], ALU.is_lt))
            chain(v.tensor_scalar(bad[:, 2:3], nextf[:, :], 0.0, None, ALU.is_ge))
            settle()
            chain(v.tensor_reduce(bad[:, 0:1], W8[:, 0:T - 1], AX.X, ALU.add))
            chain(v.tensor_tensor(bad[:, 1:2], bad[:, 1:2], bad[:, 2:3], ALU.mult))
            settle()
            v.tensor_tensor(bad[:, 0:1], bad[:, 0:1], bad[:, 1:2], ALU.add).then_inc(s_bad, 1)
            dve.wait_ge(s_nb, 1)
            step(v.tensor_scalar(bad[:, 3:4], psS[0:P, 0:1], 0.0, None, ALU.is_gt))
            chain(v.tensor_scalar(bad[:, 1:2], bad[:, 3:4], float(E // RK - 1), 1.0, ALU.mult, ALU.add))
            chain(v.tensor_scalar(bad[:, 2:3], bad[:, 3:4], float(T - 1), 1.0, ALU.mult, ALU.add))
            settle()
            v.tensor_copy(turns_i[:, :], bad[0:1, 1:3]).then_inc(s_turns, 1)
            dve.wait_ge(s_turns, 1)
            rank_turns = dve.value_load(turns_i[0:1, 0:1], min_val=1, max_val=E // RK)
            shape = [P, T, RK]
            xs_row = Xs[:, :, :].rearrange("p a b -> p (a b)")
            equal, less = (xs_row[:, z * T * RK:(z + 1) * T * RK].rearrange("p (t k) -> p t k", k=RK) for z in range(2))

            def by_slot(t):
                return t[:, :].unsqueeze(2).to_broadcast(shape)

            def by_near(t):
                return t[:, :].unsqueeze(1).to_broadcast(shape)

            RANK_STEPS = 9
            with dve.Fori(0, rank_turns) as k:
                dve.wait_ge(s_rl, k * 16 + 16)
                v.tensor_scalar(near[:, :], near_i[:, :], 1.0, None, ALU.mult).then_inc(s_rc, 1)
                v.tensor_tensor(less, by_slot(own), by_near(place), ALU.is_gt).then_inc(s_rc, 1)
                dve.wait_ge(s_rc, k * RANK_STEPS + 2)
                v.tensor_tensor(equal, by_slot(dstf), by_near(near), ALU.is_equal).then_inc(s_rc, 1)
                dve.wait_ge(s_rc, k * RANK_STEPS + 3)
                v.tensor_tensor(equal, equal, less, ALU.mult).then_inc(s_rc, 1)
                dve.wait_ge(s_rc, k * RANK_STEPS + 4)
                v.tensor_tensor(less, by_slot(dstf), by_near(near), ALU.is_gt).then_inc(s_rc, 1)
                dve.wait_ge(s_rc, k * RANK_STEPS + 5)
                v.tensor_tensor(equal, equal, less, ALU.add).then_inc(s_rc, 1)
                dve.wait_ge(s_rc, k * RANK_STEPS + 6)
                v.tensor_reduce(W8[:, :], equal, AX.X, ALU.add).then_inc(s_rc, 1)
                v.tensor_scalar(own[:, :], own[:, :], -float(RK), None, ALU.add).then_inc(s_rc, 1)
                dve.wait_ge(s_rc, k * RANK_STEPS + 8)
                v.tensor_tensor(rank[:, :], rank[:, :], W8[:, :], ALU.add).then_inc(s_rc, 1)
                dve.wait_ge(s_rc, k * RANK_STEPS + 9)
                v.memset(mcol[:, 9:10], 0.0).then_inc(s_ru, 1)
            step(v.tensor_scalar(own[:, :], rep_i[:, :], float(NOREP), None, ALU.add))
            step(v.tensor_tensor(rank[:, :], rank[:, :], own[:, :], ALU.subtract))
            step(v.scalar_tensor_tensor(rank[:, :], rank[:, :], bad[:, 3:4], own[:, :], ALU.mult, ALU.add))
            v.tensor_copy(rank_i[:, :], rank[:, :]).then_inc(s_rank, 1)
            dve.wait_ge(s_in, NLOAD)
            dve.wait_ge(s_preset, 10)
            step(v.tensor_tensor(gru[:, 0:3, :], gru[:, 0:3, :], gru[:, 3:4, :].to_broadcast([64, 3, D]), ALU.mult))
            step(v.tensor_reduce(gsm[:, 6:9], gru[:, 0:3, :], AX.X, ALU.add))
            step(v.tensor_tensor(gsm[:, 6:9], gsm[:, 6:9], gsm[:, 0:3], ALU.add))
            v.tensor_tensor(gsm[:, 9:11], gsm[:, 6:8], gsm[:, 3:5], ALU.add).then_inc(s_gate, 1)
            dve.wait_ge(s_act, 1)
            step(v.tensor_tensor(gsm[:, 11:12], gsm[:, 9:10], gsm[:, 5:6], ALU.mult))
            v.tensor_tensor(gsm[:, 11:12], gsm[:, 11:12], gsm[:, 8:9], ALU.add).then_inc(s_gate, 1)
            v.tensor_scalar(b1c[:, 1:2], b1c[:, 0:1], 0.0, None, ALU.max).then_inc(s_um, 1)
            dve.wait_ge(s_act, 2)
            step(v.tensor_scalar(gsm[:, 10:11], gsm[:, 10:11], -1.0, 1.0, ALU.mult, ALU.add))
            step(v.tensor_tensor(gsm[:, 11:12], gsm[:, 11:12], gsm[:, 10:11], ALU.mult))
            v.tensor_scalar(diag[0:64, 0, 0:64], ident[0:64, 0:64], gsm[:, 11:12], None, ALU.mult).then_inc(s_um, 1)
            dve.wait_ge(s_pe, 14)
            chain(v.tensor_tensor(Y[:, 0:64, :], Y[:, 0:64, :], psS[:, 0:64].unsqueeze(1).to_broadcast([128, 64, D]), ALU.mult))
            for k in range(2):
                chain(v.tensor_tensor(Y[:, 64 + 4 * k:68 + 4 * k, :], wa[:, :, :], aB[:, k, :, :], ALU.mult))
            settle()
            chain(v.tensor_reduce(YT[:, 0, 0:64], Y[:, 0:64, :], AX.X, ALU.add))
            chain(v.tensor_reduce(YT[:, 1, 0:8], Y[:, 64:72, :], AX.X, ALU.add))
            chain(v.tensor_copy(brow[:, BROW_L0, :], bwr[:, 0, :]))
            chain(v.tensor_copy(brow[:, BROW_L1, :], bwr[:, 1, :]))
            chain(v.tensor_copy(brow[:, BROW_L2, :], bwr[:, 3, :]))
            chain(v.tensor_tensor(brow[:, BROW_END, :], psO[1][0:1, 64:128], bwr[:, 2, :], ALU.add))
            v.tensor_tensor(carry[0:1, :], psO[1][0:1, 0:64], bwr[:, 1, :], ALU.add).then_inc(s_c1, 1)
            dve.wait_ge(s_c1, 1)
            chain(v.tensor_tensor(brow[:, BROW_DENSE, :], carry[0:1, :], bwr[:, 0, :], ALU.add))
            settle()
            all_rows = brow[:, :, :].rearrange("p a b -> p (a b)")
            v.tensor_copy(part[:, 0, :], all_rows).then_inc(s_part, 1)
            dve.wait_ge(s_part, 1)
            step(v.tensor_tensor(rest[:, :], all_rows, part[:, 0, :], ALU.subtract))
            v.tensor_copy(part[:, 1, :], rest[:, :]).then_inc(s_part, 1)
            dve.wait_ge(s_part, 2)
            step(v.tensor_tensor(rest[:, :], rest[:, :], part[:, 1, :], ALU.subtract))
            v.tensor_copy(part[:, 2, :], rest[:, :]).then_inc(s_part, 1)
            for k in range(2):
                h = slice(64 * k, 64 * k + 64)
                chain(v.tensor_tensor(BW[h, W_L0, h], YT[h, 0, 0:64], psO[0][h, 0:64], ALU.add))
                chain(v.tensor_copy(BW[h, W_HOP, h], psM[0][h, 256:320]))
                for j in range(HEADS):
                    chain(v.tensor_scalar(BW[h, W_ATT + j, h], psM[0][h, 64 * j:64 * j + 64], 1.0 / HEADS, None, ALU.mult))
                for j in range(2):
                    chain(v.tensor_copy(BV[h, j, 4 * k:4 * k + 4], YT[h, 1, 4 * j:4 * j + 4]))
            dve.wait_ge(s_pe, 15)
            chain(v.tensor_copy(c1b[:, :], psO[1][0:P, 128:192]))
            settle()
            mark("set")
            dve.wait_ge(s_edges, 80)
            chain(v.tensor_copy(dstf[:, :], dst_i[:, :]))
            chain(v.tensor_copy(nextf[:, :], next_i[:, :]))
            chain(v.memset(same[:, 0:1], 0.0))
            chain(v.memset(W8[:, :], 1.0))
            settle()
            v.tensor_scalar(diag[:, 1, :], ident[0:P, 0:P], dstf[:, 0:1], None, ALU.mult).then_inc(s_ids, 1)
            v.tensor_scalar(diag[:, 2, :], ident[0:P, 0:P], dstf[:, T - 1:T], None, ALU.mult).then_inc(s_ids, 1)
            chain(v.tensor_tensor(same[:, 1:T], dstf[:, 1:T], dstf[:, 0:T - 1], ALU.is_equal))
            chain(v.tensor_tensor(notlast[:, 0:T - 1], dstf[:, 1:T], dstf[:, 0:T - 1], ALU.is_equal))
            chain(v.tensor_tensor(notlast[:, T - 1:T], dstf[:, T - 1:T], nextf[:, :], ALU.is_equal))
            chain(v.tensor_scalar(infirst[:, :], dstf[:, :], dstf[:, 0:1], None, ALU.is_equal))
            chain(v.tensor_tensor(c8[:, 1:2], dstf[:, 0:1], nextf[:, :], ALU.not_equal))
            settle()
            chain(v.tensor_scalar(inopen[:, :], dstf[:, :], dstf[:, T - 1:T], notlast[:, T - 1:T], ALU.is_equal, ALU.mult))
            chain(v.tensor_reduce(c8[:, 0:1], infirst[:, :], AX.X, ALU.add))
            v.tensor_tensor_scan(invdeg[:, :], same[:, :], W8[:, :], 0.0, ALU.mult, ALU.add).then_inc(s_cnt, 1)
            dve.wait_ge(s_pe, 17)
            v.tensor_scalar(Kc[:, :], psS[0:P, 64:64 + P], dstf[:, T - 1:T], None, ALU.is_equal).then_inc(s_kraw, 1)
            v.tensor_scalar(KP[:, :], psS[0:P, 192:192 + P], dstf[:, 0:1], None, ALU.is_equal).then_inc(s_kraw, 1)
            v.tensor_scalar(Bm[:, :], psS[0:P, 192:192 + P], dstf[:, 0:1], c8[:, 1:2], ALU.is_equal, ALU.mult).then_inc(s_kraw, 1)
            dve.wait_ge(s_pe, 19)
            chain(v.tensor_copy(c8[:, 2:3], psS[0:P, 320:321]))
            chain(v.tensor_reduce(lmax[:, 0:1], psS[0:1, 384:384 + P], AX.X, ALU.max))
            dve.wait_ge(s_cnt, 1)
            settle()
            chain(v.scalar_tensor_tensor(invdeg[:, :], infirst[:, :], c8[:, 2:3], invdeg[:, :], ALU.mult, ALU.add))
            chain(v.tensor_copy(lmax_i[:, :], lmax[:, 0:1]))
            chain(v.tensor_copy(Tg[:, :, 0], rep_i[:, :]))
            settle()
            chain(v.tensor_copy(Tg[:, :, 1], invdeg[:, :]))
            chain(v.tensor_scalar(dinvd[:, :], invdeg[:, :], 1.0, None, ALU.add))
            settle()
            v.scalar_tensor_tensor(sct_i[:, :], notlast[:, :], float(2 * N), dstf[:, :], ALU.mult, ALU.add).then_inc(s_pay, 1)
            mark("gate")
            step(v.tensor_scalar(invdeg[:, :], invdeg[:, :], 1.0, None, ALU.max))
            dve.wait_ge(s_act, 5)
            chain(v.reciprocal(dinvd[:, :], dinvd[:, :]))
            chain(v.reciprocal(invdeg[:, :], invdeg[:, :]))
            dve.wait_ge(s_kcut, 3)
            chain(v.tensor_scalar(KP[:, :], KP[:, :], -1.0, BIG, ALU.add, ALU.mult))
            first_len = dve.value_load(lmax_i[0:1, 0:1], min_val=1, max_val=T)
            settle()

            def wide(col, n):
                return col.unsqueeze(2).to_broadcast([P, n, D])

            def moments(x, n, k, meanwhile=None):
                for j in range(n):
                    last = v.bn_stats(st[:, j, :], x(j))
                step(last)
                chain(v.tensor_tensor(k[:, 0, :], st[:, 0:n, 1], st[:, 0:n, 4], ALU.add))
                chain(v.tensor_tensor(k[:, 1, :], st[:, 0:n, 1], st[:, 0:n, 4], ALU.subtract))
                chain(v.tensor_tensor(k[:, 2, :], st[:, 0:n, 2], st[:, 0:n, 5], ALU.add))
                settle()
                chain(v.tensor_scalar(k[:, 4, :], k[:, 0, :], 0.5, None, ALU.mult))
                chain(v.scalar_tensor_tensor(k[:, 3, :], k[:, 1, :], D / 4.0, k[:, 1, :], ALU.mult, ALU.mult))
                settle()
                v.tensor_tensor(k[:, 2, :], k[:, 2, :], k[:, 3, :], ALU.add).then_inc(s_var, 1)
                if meanwhile is not None:
                    meanwhile()
                dve.wait_ge(s_std, see.add("std"))
                step(v.reciprocal(k[:, 5, :], k[:, 5, :]))

            def norm_relu(x, dst, n, scale=None, signal=None, free=None):
                k = sm[:, :, 0:n]

                def subtract_mean():
                    if free:
                        free()
                    chain(v.tensor_tensor(dst, x(None), wide(k[:, 4, :], n), ALU.subtract))

                moments(x, n, k, subtract_mean)
                if scale is not None:
                    step(v.tensor_tensor(k[:, 5, :], k[:, 5, :], scale, ALU.mult))
                ins = v.scalar_tensor_tensor(dst, dst, 0.0, wide(k[:, 5, :], n), ALU.max, ALU.mult)
                if signal is None:
                    step(ins)
                else:
                    ins.then_inc(signal, 1)

            def group_cols(t, g):
                return lambda j: cols(t, g) if j is None else t[0:P, g * GC + j, :]

            def buffer_cols(t):
                return lambda j: t[:, :, :] if j is None else t[:, j, :]

            def add_units(at, n, base=None, first=0, banks=psO):
                for k in range(n):
                    dve.wait_ge(s_o, see.add("o"))
                    v.tensor_tensor(at(k), (base or at)(k), unit_rows(banks[(first + k) % len(banks)]), ALU.add).then_inc(s_ou, 1)
                dve.wait_ge(s_ou, see.value("o"))

            def half(t, z):
                return lambda j: t[:, HC * z:HC * z + HC, :] if j is None else t[:, HC * z + j, :]

            def half_units(t, z):
                return lambda k: t[:, HC * z + UC * k:HC * z + UC * k + UC, :]

            def dense_moments():
                dve.wait_ge(s_dl, see.add("dl", 32))
                moments(buffer_cols(din), DC, smd)

            def dense_h(z):
                cut = slice(HC * z, HC * z + HC)
                step(v.tensor_tensor(dh[:, cut, :], din[:, cut, :], wide(smd[:, 4, cut], HC), ALU.subtract))
                v.scalar_tensor_tensor(dh[:, cut, :], dh[:, cut, :], 0.0, wide(smd[:, 5, cut], HC), ALU.max, ALU.mult).then_inc(s_h, 1)

            def dense_add(z):
                n = see.add(f"ds{z}", 32)
                dve.wait_ge(s_ds[z], n if z == 0 else n - 32)
                add_units(half_units(dout, z), HU, base=half_units(din, z))

            def dense_norm(z):
                norm_relu(half(dout, z), half(dh, z)(None), HC, signal=s_h)

            def dense_end(ahead=True):
                if ahead:
                    dense_moments()
                for z in range(2):
                    add_units(half_units(dout, z), HU)
                    mark("dr")
                    if ahead:
                        dense_h(z)

            def dense_start():
                dense_add(0)
                dense_add(1)
                mark("df")

            def dense(ahead=True):
                dense_add(0)
                dense_norm(0)
                dense_add(1)
                mark("df")
                dense_norm(1)
                dense_end(ahead)

            def scan_sums(dst, src):
                with dve.Fori(0, D // 4) as f:
                    for k in range(4):
                        v.tensor_tensor_scan(dst[0:P, :, f * 4 + k], same[:, :], src[0:P, :, f * 4 + k], 0.0, ALU.mult, ALU.add)

            def carry_sums(dst):
                mark("ct")
                dve.wait_ge(s_ct, see.value("ct"))
                dve.wait_ge(s_cp, see.add("cp"))
                step(v.tensor_copy(carry[:, :], psS[0:P, 0:D]))
                with dve.Fori(0, first_len) as t:
                    v.scalar_tensor_tensor(dst[0:P, t, :], carry[:, :], infirst[:, bass.ts(t, 1)], dst[0:P, t, :], ALU.mult, ALU.add)
                mark("fix")
                dve.wait_ge(s_fix, see.value("fix"))

            def carry_heads(mask):
                dve.wait_ge(s_cp, see.add("cp"))
                step(v.tensor_copy(carry[:, 0:HEADS], psS[0:P, 0:HEADS]))
                for h in range(HEADS):
                    chain(v.scalar_tensor_tensor(Sd[:, :, h], mask[:, :], carry[:, h:h + 1], Sd[:, :, h], ALU.mult, ALU.add))
                settle()

            def tails_out():
                mark("ct")

            def hold():
                step(v.tensor_scalar(W8[:, :], notlast[:, :], -1.0, 1.0, ALU.mult, ALU.add))
                step(v.tensor_tensor(Sd[:, :, :], Sd[:, :, :], W8[:, :].unsqueeze(2).to_broadcast([P, T, HEADS]), ALU.mult))
                for h in range(HEADS):
                    chain(v.tensor_tensor_scan(Sd[:, ::-1, h], notlast[:, ::-1], Sd[:, ::-1, h], 0.0, ALU.mult, ALU.add))
                settle()
                tails_out()
                carry_heads(inopen)

            def softmax():
                hold()
                step(v.tensor_tensor(S[:, :, :], S[:, :, :], Sd[:, :, :], ALU.add))
                step(v.scalar_tensor_tensor(S[:, :, :], S[:, :, :], SLOPE, S[:, :, :], ALU.mult, ALU.max))
                step(v.tensor_scalar(W8[:, :], same[:, :], -1.0, BIG, ALU.add, ALU.mult))
                for h in range(HEADS):
                    chain(v.tensor_tensor_scan(Sd[:, :, h], W8[:, :], S[:, :, h], -BIG, ALU.add, ALU.max))
                settle()
                for h in range(HEADS):
                    chain(v.tensor_scalar(diag[:, h, :], ident[0:P, 0:P], Sd[:, T - 1, h:h + 1], None, ALU.mult))
                settle()
                tails_out()
                dve.wait_ge(s_cp, see.add("cp"))
                tails = psS[0:P, 0:HEADS * P].rearrange("p (h q) -> p h q", h=HEADS)
                step(v.tensor_tensor(diag[:, :, :], tails, KP[:, :].unsqueeze(1).to_broadcast([P, HEADS, P]), ALU.add))
                chain(v.tensor_reduce(carry[:, 0:HEADS], diag[:, :, :], AX.X, ALU.max))
                chain(v.tensor_scalar(W8[:, :], infirst[:, :], -1.0, BIG, ALU.add, ALU.mult))
                settle()
                for h in range(HEADS):
                    chain(v.scalar_tensor_tensor(Sd[:, :, h], W8[:, :], carry[:, h:h + 1], Sd[:, :, h], ALU.add, ALU.max))
                settle()
                hold()
                v.tensor_tensor(S[:, :, :], S[:, :, :], Sd[:, :, :], ALU.subtract).then_inc(s_ex, 1)
                dve.wait_ge(s_exd, 1)
                for h in range(HEADS):
                    chain(v.tensor_tensor_scan(Sd[:, :, h], same[:, :], S[:, :, h], 0.0, ALU.mult, ALU.add))
                settle()
                tails_out()
                carry_heads(infirst)
                hold()
                step(v.tensor_scalar(Sd[:, :, :], Sd[:, :, :], 1e-16, None, ALU.max))
                step(v.reciprocal(Sd[:, :, :], Sd[:, :, :]))
                step(v.tensor_tensor(S[:, :, :], S[:, :, :], Sd[:, :, :], ALU.mult))

            def weighted(g, u):
                dst = (tmpA if u % 2 == 0 else tmpB)[:, 0:HEADS * UC, :].rearrange("p (h c) d -> p h c d", h=HEADS)
                for h in range(HEADS):
                    last = v.tensor_tensor(dst[:, h, :, :], cols(Xs, g, UC * u, UC),
                                           S[:, bass.ds(g * GC + UC * u, UC), h:h + 1].to_broadcast([P, UC, D]), ALU.mult)
                last.then_inc(s_h, 1)

            def take_messages(g, u):
                dve.wait_ge(s_am, see.add("am", HEADS))
                v.tensor_scalar(cols(Xs, g, UC * u, UC), unit_rows(psZ), 1.0, None, ALU.mult).then_inc(s_zu, 1)

            def src_norm(stage, g):
                both(dve, s_gx, see.add("gx", 16 * HALF))
                rows = group_cols(Xs, g)
                if stage == 1:
                    norm_relu(rows, tmpA[:, :, :], GC)
                    chain(v.tensor_tensor(cols(Xs, g), cols(Xs, g), c1b[:, :].unsqueeze(1).to_broadcast([P, GC, D]), ALU.add))
                    step(v.tensor_tensor(cols(Y, g), cols(Y, g), tmpA[:, :, :], ALU.add))
                else:
                    dve.wait_ge(s_hc, see.add("hc") - 1)
                    norm_relu(rows, tmpA[:, :, :], GC, signal=s_h)

            def src_units(g, at=0, banks=psO):
                add_units(lambda k: cols(Xs, g, UC * k, UC), GU, None, at, banks)

            def table_rows(g):
                both(dve, s_gt, see.add("gt", 16 * HALF))
                chain(v.tensor_scalar(cols(rep_i, g), Tg[:, bass.ts(g, GC), 0], float(NOREP), None, ALU.add))
                dve.wait_ge(s_std, see.add("std"))
                step(v.reciprocal(cols(dinvs, g), cols(dinvs, g)))
                chain(v.tensor_tensor(cols(Y, g), cols(Y, g), wide(cols(dinvs, g), GC), ALU.mult))

            def all_messages(g):
                for u in range(GU + 1):
                    if u < GU:
                        weighted(g, u)
                    if u >= 1:
                        take_messages(g, u - 1)

            def take_scores(dst, g):
                for k in range(GU):
                    dve.wait_ge(s_o, see.add("o"))
                    v.tensor_scalar(cols(dst, g, UC * k, UC), psO[k % 2][0:P, 0:UC * HEADS].rearrange("p (c h) -> p c h", h=HEADS),
                                    1.0, None, ALU.mult).then_inc(s_ou, 1)
                dve.wait_ge(s_ou, see.value("o"))

            def dst_ahead(free=None):
                dve.wait_ge(s_xl[0], see.add("xl0", 32))
                norm_relu(buffer_cols(xdg), tmpB[:, :, :], GC, signal=s_h, free=free)

            def take_self_parts():
                for k in range(GU):
                    dve.wait_ge(s_o, see.add("o"))
                    v.tensor_scalar(tmpB[:, UC * k:UC * k + UC, :], unit_rows(ring[k % len(ring)]), 1.0, None, ALU.mult).then_inc(s_ou, 1)
                dve.wait_ge(s_ou, see.value("o"))

            def copy_sums(g, b):
                v.tensor_scalar((tmpA, tmpB)[b][:, :, :], cols(Y, g), 1.0, None, ALU.mult).then_inc(s_h, 1)

            def dst_work(stage, g, b):
                rows = xd0[b] if stage == 0 else xd[b]
                at = lambda k: rows[:, UC * k:UC * k + UC, :]
                if stage == 0:
                    dense_start()
                    both(dve, s_gd, see.add("gd", 16 * HALF))
                elif stage == 1:
                    if not (isinstance(g, int) and g == G - 1):
                        copy_sums(g + 1, 1 - b)
                elif stage == 2:
                    v.tensor_tensor(tmpB[:, :, :], cols(Y, g), wide(cols(invdeg, g), GC), ALU.mult).then_inc(s_h, 1)
                    dve.wait_ge(s_zl, see.add("zl", 32))
                elif stage == 4:
                    v.tensor_tensor(tmpA[:, :, :], cols(Y, g), wide(cols(invdeg, g), GC), ALU.mult).then_inc(s_h, 1)
                if stage in (1, 2, 4):
                    dve.wait_ge(s_xl[b], see.add(f"xl{b}", 32))
                if stage == 0:
                    norm_relu(buffer_cols(rows), tmpA[:, :, :], GC, scale=cols(dinvd, g))
                    step(v.tensor_tensor(tmpA[:, :, :], tmpA[:, :, :], cols(Y, g), ALU.add))
                    v.tensor_tensor(tmpA[:, :, :], tmpA[:, :, :], wide(cols(dinvd, g), GC), ALU.mult).then_inc(s_h, 1)
                    dense_norm(0)
                    add_units(at, GU)
                elif stage == 1:
                    add_units(at, GU)
                elif stage == 2:
                    add_units(lambda k: tmpA[:, UC * k:UC * k + UC, :], GU)
                    v.scalar_tensor_tensor(rows[:, :, :], tmpA[:, :, :], 0.0, rows[:, :, :], ALU.max, ALU.add)
                elif stage == 3:
                    step(v.tensor_tensor(cols(Y, g), cols(Y, g), wide(cols(invdeg, g), GC), ALU.mult))
                else:
                    step(v.tensor_tensor(rows[:, :, :], rows[:, :, :], cols(Xs, g), ALU.add))
                    add_units(at, GU)
                mark("xu")
                if stage == 0:
                    dense_norm(1)
                    dense_end()

            dve.wait_ge(s_ds[0], 32)
            dense_moments()
            dense_h(0)
            dense_h(1)
            with dve.Fori(0, G) as g:
                see.enter(g, TURN["rows"])
                dense_start()
                src_norm(0, g)
                dense_norm(0)
                src_units(g)
                dense_norm(1)
                dense_end()
                see.leave(G)
            with dve.Fori(0, LONE) as g:
                see.enter(g, TURN["lone"])
                dense()
                see.leave(LONE)
            dve.wait_ge(s_hc, see.value("hc"))
            with dve.Fori(0, G) as g:
                see.enter(g, TURN["table"])
                dense()
                table_rows(g)
                see.leave(G)

            for stage in range(STAGES):
                if stage == 1:
                    dve.wait_ge(s_ea, 32 * G)
                if stage > 0:
                    def src_work(g, **chunk):
                        if stage in DENSE_STAGES:
                            dense(**chunk)
                        if stage == 3:
                            dst_ahead()
                            mark("xu")
                        if stage < 4:
                            src_norm(stage, g)
                        if stage == 2:
                            take_self_parts()
                            mark("xu")
                            if not isinstance(g, int):
                                dst_ahead(lambda: dve.wait_ge(s_zs, see.add("zs", 32)))
                            src_units(g, GU, ring)
                        elif stage == 3:
                            take_scores(Sd, g)
                            take_scores(S, g)
                        elif stage == 4:
                            all_messages(g)

                    if stage == 2:
                        dst_ahead()
                    with dve.Fori(0, G - 1) as g:
                        see.enter(g, TURN[stage])
                        src_work(g)
                        see.leave(G - 1)
                    src_work(G - 1, **({"ahead": False} if stage == DENSE_STAGES[-1] else {}))
                if stage in (0, 2, 3):
                    dve.wait_ge(s_hc, see.value("hc"))
                settle()
                if stage == 4:
                    both(dve, s_gx, 16 * HALF * G * 5)
                    dve.wait_ge(s_zu, GU * G + 1)
                scan_sums(Y, Xs if stage == 3 else Y)
                carry_sums(Y)
                if stage == 4:
                    scan_sums(Xs, Xs)
                    carry_sums(Xs)
                mark("sum")
                if stage == 1:
                    copy_sums(0, 0)
                elif stage == 2:
                    dve.wait_ge(s_zs, see.add("zs", 32))
                see.by_pairs(dve, DST_TURN[stage], lambda g, b: dst_work(stage, g, b))
                if stage == 3:
                    dve.wait_ge(s_g1, 32 * G)
                    step(v.memset(Y[:, :, :], 0.0))
                mark("st")
                if stage == 3:
                    softmax()


_INS = ['x', 'src', 'dst', 'edge_attr_64', 'L0_gnn_memory_weights', 'L0_gnn_gru_w_ih', 'L0_gnn_gru_b_ih',
        'L0_gnn_gru_b_hh', 'L0_gnn_wt_w', 'L0_gnn_wt_b', 'L0_gnn_gcn_bias', 'L1_gnn_W1', 'L1_gnn_b1', 'L1_gnn_W2',
        'L1_gnn_b2', 'L2_gnn_W_self', 'L2_gnn_W_neigh', 'L2_gnn_bias', 'L3_gnn_W_att', 'L3_gnn_a_src', 'L3_gnn_a_dst',
        'L3_gnn_W_g', 'L3_gnn_b_g', 'L3_gnn_W_w', 'L3_gnn_b_w']


def kernel(**inputs):
    import concourse.bacc as _bacc
    from concourse.bass_utils import run_bass_kernel_spmd as _run

    nc = _bacc.Bacc("TRN2", target_bir_lowering=False, num_devices=1)
    arrays, args = {}, {}
    for name in _INS:
        v = np.ascontiguousarray(inputs[name])
        arrays[f"in_{name}"] = v
        args[name] = nc.dram_tensor(f"in_{name}", v.shape, mybir.dt.from_np(v.dtype), kind="ExternalInput").ap()
    out = nc.dram_tensor("out_0", (N, D), F32, kind="ExternalOutput").ap()
    gnn_kernel(nc, args, out)
    return _run(nc, [arrays], core_ids=[0]).results[0]["out_0"]
```
